# Optimizing a Trainium2 kernel written in Bass

```python
import numpy as np
import jax
import jax.numpy as jnp

def _softmax(x, axis=-1):
    return jax.nn.softmax(x, axis=axis)

def _gelu(x):
    return jax.nn.gelu(x, approximate=True)

def _silu(x):
    return jax.nn.silu(x)

def _sigmoid(x):
    return jax.nn.sigmoid(x)

def _layernorm(x, axis=-1, eps=1e-05):
    m = jnp.mean(x, axis=axis, keepdims=True)
    v = jnp.var(x, axis=axis, keepdims=True)
    return (x - m) / jnp.sqrt(v + eps)

def _scatter_add(tgt, idx, src, axis=0):
    return tgt.at[idx].add(src)

def _segment_sum(src, seg, n):
    return jax.ops.segment_sum(src, seg, n)
kernel_name = 'mk_decoder_postln_d2_seqx_r8_b51eba'

def setup_inputs(seed: int=0):
    np.random.seed(seed)
    _w = jnp.asarray

    def _rec_inputs():
        import jax
        import jax.numpy as jnp
        _rk = jax.random.key(seed)
        x = 7.22e-05 + 1 * jax.random.normal(jax.random.fold_in(_rk, 1), (8, 128, 128), jnp.float32)
        _lenS = 128 - jax.random.randint(jax.random.fold_in(_rk, 7), (8,), 0, max(1, 128 // 4) + 1, jnp.int32)
        _lenS2 = 128 - jax.random.randint(jax.random.fold_in(_rk, 8), (8,), 0, max(1, 128 // 4) + 1, jnp.int32)
        _ctx_1024P = jax.random.normal(jax.random.fold_in(_rk, 11), (8, 16, 128), jnp.float32)
        _ctx_1024c = jax.random.dirichlet(jax.random.fold_in(_rk, 511), 0.3 * jnp.ones((16,), jnp.float32), (8, 128))
        _ctx_1024t = jnp.einsum('bsk,bkd->bsd', _ctx_1024c, _ctx_1024P)
        _ctx_1024t = _ctx_1024t * jax.lax.rsqrt(jnp.mean(jnp.square(_ctx_1024t)) + 1e-12) * 0.953939
        ctx_1024 = 4.13588e-05 + 0.999923 * (_ctx_1024t + 0.3 * jax.random.normal(jax.random.fold_in(_rk, 611), (8, 128, 128), jnp.float32))
        return (x, ctx_1024)
    x, ctx_1024 = _rec_inputs()

    def _L0_attn_setup():
        import jax, jax.numpy as jnp
        import numpy as np
        N_HEADS = 16
        HIDDEN = 128
        HEAD_DIM = 64
        BSZ = 4
        SEQ = 128
        SCALE = HEAD_DIM ** (-0.5)
        key = jax.random.key(seed)
        k_x, k_q, k_k, k_v, k_o = jax.random.split(key, 5)
        s = HIDDEN ** (-0.5)
        return {'x': jax.random.normal(k_x, (BSZ, SEQ, HIDDEN), dtype=jnp.float32), 'wq': jax.random.normal(k_q, (N_HEADS * HEAD_DIM, HIDDEN), dtype=jnp.float32) * s, 'wk': jax.random.normal(k_k, (N_HEADS * HEAD_DIM, HIDDEN), dtype=jnp.float32) * s, 'wv': jax.random.normal(k_v, (N_HEADS * HEAD_DIM, HIDDEN), dtype=jnp.float32) * s, 'wo': jax.random.normal(k_o, (HIDDEN, N_HEADS * HEAD_DIM), dtype=jnp.float32) * s}
    _L0_attn_all = _L0_attn_setup()
    _L0_attn_in = {k: v for k, v in _L0_attn_all.items() if k in ('wq', 'wk', 'wv', 'wo')}
    del _L0_attn_all

    def _L0_xattn_setup():
        import jax, jax.numpy as jnp
        import numpy as np
        import math
        D_MODEL = 128
        D_K = 128
        D_V = 128
        B, S = (4, 256)
        key = jax.random.key(seed)
        ks = jax.random.split(key, 6)
        scale = 1.0 / math.sqrt(D_MODEL)
        return {'q': jax.random.normal(ks[0], (B, S, D_MODEL), dtype=jnp.float32), 'k': jax.random.normal(ks[1], (B, S, D_MODEL), dtype=jnp.float32), 'v': jax.random.normal(ks[2], (B, S, D_MODEL), dtype=jnp.float32), 'Wq': jax.random.normal(ks[3], (D_K, D_MODEL), dtype=jnp.float32) * scale, 'bq': jnp.zeros((D_K,), dtype=jnp.float32), 'Wk': jax.random.normal(ks[4], (D_K, D_MODEL), dtype=jnp.float32) * scale, 'bk': jnp.zeros((D_K,), dtype=jnp.float32), 'Wv': jax.random.normal(ks[5], (D_V, D_MODEL), dtype=jnp.float32) * scale, 'bv': jnp.zeros((D_V,), dtype=jnp.float32)}
    _L0_xattn_all = _L0_xattn_setup()
    _L0_xattn_in = {k: v for k, v in _L0_xattn_all.items() if k in ('Wq', 'bq', 'Wk', 'bk', 'Wv', 'bv')}
    del _L0_xattn_all

    def _L0_ffn_setup():
        import jax, jax.numpy as jnp
        import numpy as np
        B, S, H, E = (8, 512, 128, 8)
        key = jax.random.key(seed)
        k1, k2, k3 = jax.random.split(key, 3)
        x = jax.random.normal(k1, (B, S, H), dtype=jnp.float32)
        Wg = jax.random.normal(k2, (H, E), dtype=jnp.float32) * (1.0 / np.sqrt(H))
        bg = jnp.zeros((E,), dtype=jnp.float32)
        We = jax.random.normal(k3, (H, H), dtype=jnp.float32) * (1.0 / np.sqrt(H))
        be = jnp.zeros((H,), dtype=jnp.float32)
        return {'x': x, 'Wg': Wg, 'bg': bg, 'We': We, 'be': be}
    _L0_ffn_all = _L0_ffn_setup()
    _L0_ffn_in = {k: v for k, v in _L0_ffn_all.items() if k in ('Wg', 'bg', 'We', 'be')}
    del _L0_ffn_all

    def _L1_attn_setup():
        import jax, jax.numpy as jnp
        import numpy as np
        NUM_HEADS = 16
        key = jax.random.key(seed)
        ks = jax.random.split(key, 3)
        B, S, E = (8, 128, 128)
        x = jax.random.normal(ks[0], (B, S, E), dtype=jnp.float32)
        W_attn = jax.random.normal(ks[1], (E, 3 * E), dtype=jnp.float32) * (1.0 / np.sqrt(E))
        b_attn = jnp.zeros((3 * E,), dtype=jnp.float32)
        W_proj = jax.random.normal(ks[2], (E, E), dtype=jnp.float32) * (1.0 / np.sqrt(E))
        b_proj = jnp.zeros((E,), dtype=jnp.float32)
        return {'x': x, 'W_attn': W_attn, 'b_attn': b_attn, 'W_proj': W_proj, 'b_proj': b_proj}
    _L1_attn_all = _L1_attn_setup()
    _L1_attn_in = {k: v for k, v in _L1_attn_all.items() if k in ('W_attn', 'b_attn', 'W_proj', 'b_proj')}
    del _L1_attn_all

    def _L1_xattn_setup():
        import jax, jax.numpy as jnp
        import numpy as np
        EMBED_DIM = 128
        HEAD_DIM = 128
        GAMMA = 0.96875
        THETA = 10000.0
        SCALE_BASE = 512.0

        def _dup_interleave(x):
            return jnp.repeat(x, 2, axis=-1)

        def _rotate_half(x):
            x_even = x[..., ::2]
            x_odd = x[..., 1::2]
            return jnp.stack((-x_odd, x_even), axis=-1).reshape(x.shape)

        def _xpos(x, offset=0, inverse_scale=False):
            l = x.shape[-2]
            half = HEAD_DIM // 2
            scale_vec = (jnp.arange(0, HEAD_DIM, 2, dtype=jnp.float32) + 0.4 * HEAD_DIM) / (1.4 * HEAD_DIM)
            pos = jnp.arange(offset, offset + l, dtype=jnp.float32)
            scale = scale_vec[None, :] ** (pos / SCALE_BASE)[:, None]
            freqs = 1.0 / THETA ** (jnp.arange(half, dtype=jnp.float32) / half)
            sin_in = pos[:, None] * freqs[None, :]
            sin, cos = (jnp.sin(sin_in), jnp.cos(sin_in))
            if inverse_scale:
                scale = 1.0 / scale
            return x * _dup_interleave(cos * scale) + _rotate_half(x) * _dup_interleave(sin * scale)

        def _decay_mask(l, gamma):
            idx = jnp.arange(l, dtype=jnp.float32)
            diff = idx[:, None] - idx[None, :]
            return jnp.where(diff >= 0, gamma ** diff, 0.0)
        key = jax.random.key(seed)
        k1, k2, k3, k4, k5, k6 = jax.random.split(key, 6)
        B, L = (4, 256)
        s = 1.0 / np.sqrt(EMBED_DIM)
        return {'q': jax.random.normal(k1, (B, L, EMBED_DIM), dtype=jnp.float32), 'k': jax.random.normal(k2, (B, L, EMBED_DIM), dtype=jnp.float32), 'v': jax.random.normal(k3, (B, L, EMBED_DIM), dtype=jnp.float32), 'Wq': jax.random.normal(k4, (EMBED_DIM, HEAD_DIM), dtype=jnp.float32) * s, 'Wk': jax.random.normal(k5, (EMBED_DIM, HEAD_DIM), dtype=jnp.float32) * s, 'Wv': jax.random.normal(k6, (EMBED_DIM, HEAD_DIM), dtype=jnp.float32) * s}
    _L1_xattn_all = _L1_xattn_setup()
    _L1_xattn_in = {k: v for k, v in _L1_xattn_all.items() if k in ('Wq', 'Wk', 'Wv')}
    del _L1_xattn_all

    def _L1_ffn_setup():
        import jax, jax.numpy as jnp
        import numpy as np
        HIDDEN = 128
        INNER = 512

        def _weight_quant(w):
            scale = 1.0 / jnp.clip(jnp.mean(jnp.abs(w)), 1e-05)
            wq = jnp.clip(jnp.round(w * scale), -1.0, 1.0) / scale
            return w + jax.lax.stop_gradient(wq - w)

        def _act_quant(x):
            scale = 127.0 / jnp.clip(jnp.max(jnp.abs(x), axis=-1, keepdims=True), 1e-05)
            xq = jnp.clip(jnp.round(x * scale), -128.0, 127.0) / scale
            return x + jax.lax.stop_gradient(xq - x)

        def _bitlinear(x, w):
            return jnp.einsum('bsi,oi->bso', _act_quant(x), _weight_quant(w))
        key = jax.random.key(seed)
        k0, k1, k2, k3 = jax.random.split(key, 4)
        x = jax.random.normal(k0, (4, 256, HIDDEN), dtype=jnp.float32)
        w_gate = jax.random.normal(k1, (INNER, HIDDEN), dtype=jnp.float32) / np.sqrt(HIDDEN)
        w_up = jax.random.normal(k2, (INNER, HIDDEN), dtype=jnp.float32) / np.sqrt(HIDDEN)
        w_down = jax.random.normal(k3, (HIDDEN, INNER), dtype=jnp.float32) / np.sqrt(INNER)
        return {'x': x, 'w_gate': w_gate, 'w_up': w_up, 'w_down': w_down}
    _L1_ffn_all = _L1_ffn_setup()
    _L1_ffn_in = {k: v for k, v in _L1_ffn_all.items() if k in ('w_gate', 'w_up', 'w_down')}
    del _L1_ffn_all
    return {'x': x, 'ctx_1024': ctx_1024, 'L0_attn_wq': _L0_attn_in['wq'], 'L0_attn_wk': _L0_attn_in['wk'], 'L0_attn_wv': _L0_attn_in['wv'], 'L0_attn_wo': _L0_attn_in['wo'], 'L0_xattn_Wq': _L0_xattn_in['Wq'], 'L0_xattn_bq': _L0_xattn_in['bq'], 'L0_xattn_Wk': _L0_xattn_in['Wk'], 'L0_xattn_bk': _L0_xattn_in['bk'], 'L0_xattn_Wv': _L0_xattn_in['Wv'], 'L0_xattn_bv': _L0_xattn_in['bv'], 'L0_ffn_Wg': _L0_ffn_in['Wg'], 'L0_ffn_bg': _L0_ffn_in['bg'], 'L0_ffn_We': _L0_ffn_in['We'], 'L0_ffn_be': _L0_ffn_in['be'], 'L1_attn_W_attn': _L1_attn_in['W_attn'], 'L1_attn_b_attn': _L1_attn_in['b_attn'], 'L1_attn_W_proj': _L1_attn_in['W_proj'], 'L1_attn_b_proj': _L1_attn_in['b_proj'], 'L1_xattn_Wq': _L1_xattn_in['Wq'], 'L1_xattn_Wk': _L1_xattn_in['Wk'], 'L1_xattn_Wv': _L1_xattn_in['Wv'], 'L1_ffn_w_gate': _L1_ffn_in['w_gate'], 'L1_ffn_w_up': _L1_ffn_in['w_up'], 'L1_ffn_w_down': _L1_ffn_in['w_down']}

def reference(x, ctx_1024, L0_attn_wq, L0_attn_wk, L0_attn_wv, L0_attn_wo, L0_xattn_Wq, L0_xattn_bq, L0_xattn_Wk, L0_xattn_bk, L0_xattn_Wv, L0_xattn_bv, L0_ffn_Wg, L0_ffn_bg, L0_ffn_We, L0_ffn_be, L1_attn_W_attn, L1_attn_b_attn, L1_attn_W_proj, L1_attn_b_proj, L1_xattn_Wq, L1_xattn_Wk, L1_xattn_Wv, L1_ffn_w_gate, L1_ffn_w_up, L1_ffn_w_down):
    import jax
    import jax.numpy as jnp

    def _L0_attn_ref(x, wq, wk, wv, wo):
        import jax, jax.numpy as jnp
        import numpy as np
        N_HEADS = 16
        HIDDEN = 128
        HEAD_DIM = 64
        BSZ = 4
        SEQ = 128
        SCALE = HEAD_DIM ** (-0.5)
        bsz, seqlen, _ = x.shape
        xq = jnp.einsum('bsh,oh->bso', x, wq)
        xk = jnp.einsum('bsh,oh->bso', x, wk)
        xv = jnp.einsum('bsh,oh->bso', x, wv)
        xq = xq.reshape(bsz, N_HEADS, seqlen, HEAD_DIM)
        xk = xk.reshape(bsz, N_HEADS, seqlen, HEAD_DIM)
        xv = xv.reshape(bsz, N_HEADS, seqlen, HEAD_DIM)
        scores = jnp.einsum('bhid,bhjd->bhij', xq, xk) * SCALE
        scores = jax.nn.softmax(scores, axis=-1)
        out = jnp.einsum('bhij,bhjd->bhid', scores, xv)
        out = out.reshape(bsz, seqlen, N_HEADS * HEAD_DIM)
        return jnp.einsum('bso,ho->bsh', out, wo)

    def _L0_xattn_ref(q, k, v, Wq, bq, Wk, bk, Wv, bv):
        import jax, jax.numpy as jnp
        import numpy as np
        import math
        D_MODEL = 128
        D_K = 128
        D_V = 128
        B, S = (4, 256)
        qp = jnp.einsum('bsd,kd->bsk', q, Wq) + bq
        kp = jnp.einsum('bsd,kd->bsk', k, Wk) + bk
        vp = jnp.einsum('bsd,kd->bsk', v, Wv) + bv
        energies = jnp.einsum('bqk,bsk->bqs', qp, kp) / math.sqrt(D_K)
        weights = jax.nn.softmax(energies, axis=-1)
        out = jnp.einsum('bqs,bsv->bqv', weights, vp)
        return out

    def _L0_ffn_ref(x, Wg, bg, We, be):
        import jax, jax.numpy as jnp
        import numpy as np
        B, S, H, E = (8, 512, 128, 8)
        b, s, h = x.shape
        tokens = x.reshape(-1, h)
        logits = tokens @ Wg + bg
        probs = jax.nn.softmax(logits, axis=1)
        best = jnp.argmax(logits, axis=1)
        best_p = jnp.take_along_axis(probs, best[:, None], axis=1)[:, 0]
        expert_out = tokens @ We + be
        out = expert_out * best_p[:, None]
        return out.reshape(b, s, h)

    def _L1_attn_ref(x, W_attn, b_attn, W_proj, b_proj):
        import jax, jax.numpy as jnp
        import numpy as np
        NUM_HEADS = 16
        B, S, E = x.shape
        H = NUM_HEADS
        D = E // H
        qkv = x @ W_attn + b_attn
        q, k, v = jnp.split(qkv, 3, axis=-1)

        def split_heads(t):
            return t.reshape(B, S, H, D).transpose(0, 2, 1, 3)
        q, k, v = (split_heads(q), split_heads(k), split_heads(v))
        scores = jnp.einsum('bhqd,bhkd->bhqk', q, k) / jnp.sqrt(jnp.asarray(D, x.dtype))
        causal = jnp.tril(jnp.ones((S, S), dtype=bool))
        scores = jnp.where(causal, scores, -jnp.inf)
        probs = jax.nn.softmax(scores, axis=-1)
        out = jnp.einsum('bhqk,bhkd->bhqd', probs, v)
        out = out.transpose(0, 2, 1, 3).reshape(B, S, E)
        return out @ W_proj + b_proj

    def _L1_xattn_ref(q, k, v, Wq, Wk, Wv):
        import jax, jax.numpy as jnp
        import numpy as np
        EMBED_DIM = 128
        HEAD_DIM = 128
        GAMMA = 0.96875
        THETA = 10000.0
        SCALE_BASE = 512.0

        def _dup_interleave(x):
            return jnp.repeat(x, 2, axis=-1)

        def _rotate_half(x):
            x_even = x[..., ::2]
            x_odd = x[..., 1::2]
            return jnp.stack((-x_odd, x_even), axis=-1).reshape(x.shape)

        def _xpos(x, offset=0, inverse_scale=False):
            l = x.shape[-2]
            half = HEAD_DIM // 2
            scale_vec = (jnp.arange(0, HEAD_DIM, 2, dtype=jnp.float32) + 0.4 * HEAD_DIM) / (1.4 * HEAD_DIM)
            pos = jnp.arange(offset, offset + l, dtype=jnp.float32)
            scale = scale_vec[None, :] ** (pos / SCALE_BASE)[:, None]
            freqs = 1.0 / THETA ** (jnp.arange(half, dtype=jnp.float32) / half)
            sin_in = pos[:, None] * freqs[None, :]
            sin, cos = (jnp.sin(sin_in), jnp.cos(sin_in))
            if inverse_scale:
                scale = 1.0 / scale
            return x * _dup_interleave(cos * scale) + _rotate_half(x) * _dup_interleave(sin * scale)

        def _decay_mask(l, gamma):
            idx = jnp.arange(l, dtype=jnp.float32)
            diff = idx[:, None] - idx[None, :]
            return jnp.where(diff >= 0, gamma ** diff, 0.0)
        qh = _xpos(q @ Wq, offset=0, inverse_scale=False)
        kh = _xpos(k @ Wk, offset=0, inverse_scale=True)
        vh = v @ Wv
        L = qh.shape[-2]
        mask = _decay_mask(L, GAMMA)
        scores = jnp.einsum('bld,bmd->blm', qh, kh) * mask[None, :, :]
        return scores @ vh

    def _L1_ffn_ref(x, w_gate, w_up, w_down):
        import jax, jax.numpy as jnp
        import numpy as np
        HIDDEN = 128
        INNER = 512

        def _weight_quant(w):
            scale = 1.0 / jnp.clip(jnp.mean(jnp.abs(w)), 1e-05)
            wq = jnp.clip(jnp.round(w * scale), -1.0, 1.0) / scale
            return w + jax.lax.stop_gradient(wq - w)

        def _act_quant(x):
            scale = 127.0 / jnp.clip(jnp.max(jnp.abs(x), axis=-1, keepdims=True), 1e-05)
            xq = jnp.clip(jnp.round(x * scale), -128.0, 127.0) / scale
            return x + jax.lax.stop_gradient(xq - x)

        def _bitlinear(x, w):
            return jnp.einsum('bsi,oi->bso', _act_quant(x), _weight_quant(w))
        gate = jax.nn.silu(_bitlinear(x, w_gate))
        up = _bitlinear(x, w_up)
        return _bitlinear(gate * up, w_down)
    x = _layernorm(x + _L0_attn_ref(x, L0_attn_wq, L0_attn_wk, L0_attn_wv, L0_attn_wo), axis=-1)
    x = _layernorm(x + _L0_xattn_ref(x, ctx_1024, ctx_1024, L0_xattn_Wq, L0_xattn_bq, L0_xattn_Wk, L0_xattn_bk, L0_xattn_Wv, L0_xattn_bv), axis=-1)
    x = _layernorm(x + _L0_ffn_ref(x, L0_ffn_Wg, L0_ffn_bg, L0_ffn_We, L0_ffn_be), axis=-1)
    x = _layernorm(x + _L1_attn_ref(x, L1_attn_W_attn, L1_attn_b_attn, L1_attn_W_proj, L1_attn_b_proj), axis=-1)
    x = _layernorm(x + _L1_xattn_ref(x, ctx_1024, ctx_1024, L1_xattn_Wq, L1_xattn_Wk, L1_xattn_Wv), axis=-1)
    x = _layernorm(x + _L1_ffn_ref(x, L1_ffn_w_gate, L1_ffn_w_up, L1_ffn_w_down), axis=-1)
    return x

_drawn_inputs = setup_inputs


def setup_inputs(seed=0):
    import zlib

    import numpy as np

    out = dict(_drawn_inputs(seed))
    spreads = {'L0_xattn_bq': (0.0, 0.1),
     'L0_xattn_bk': (0.0, 0.8),
     'L0_xattn_bv': (0.0, 0.1),
     'L0_ffn_bg': (0.0, 0.376),
     'L0_ffn_be': (0.0, 0.1),
     'L1_attn_b_attn': (0.0, 0.1),
     'L1_attn_b_proj': (0.0, 0.1)}
    factors = {}
    for name, (base, spread) in spreads.items():
        noise = np.random.default_rng([zlib.crc32(name.encode()), seed]).standard_normal(out[name].shape)
        drawn = base * np.exp(spread * noise) if base else spread * noise
        out[name] = jnp.asarray(drawn.astype(out[name].dtype))
    for name, factor in factors.items():
        out[name] = (out[name] * factor).astype(out[name].dtype)
    return out
```

```python
from contextlib import ExitStack

import concourse.bass as bass
from concourse import mybir

ALU = mybir.AluOpType
ACT = mybir.ActivationFunctionType
F32 = mybir.dt.float32
F32R = mybir.dt.float32r
F16 = mybir.dt.float16
BF16 = mybir.dt.bfloat16
I32 = mybir.dt.int32
AX_X = mybir.AxisListType.X

P = 128
NB = 8
NTOK = NB * P
H = 16
DH0 = 64
G = 8
DH1 = 8
INNER = 512
NE = 8
NPAIR = NB // 2
TP = 2 * P
HP = 2 * H
QP = HP // 4
VW = 96
NPROJ = 12
SLOTS_PT = 3
SCALE0 = DH0 ** -0.5
SCALE1 = DH1 ** -0.5
SCALEX = P ** -0.5
EPS = 1e-5
MAGIC = 1.5 * 2.0 ** 23
RSQRT_BITS = 0x5F3759DF
MASKED = -1e30
NW = INNER * P


def decoder(nc, x_tok, x_T, ctx_T, wq0, wk0, wv0, wo0, xwq0, xbq0, xwk0, xbk0, xwv0, xbv0,
            wge, bge, wqk1, bqk1, wv1, bv1, wp1, bp1, xwq1, xwq1s, xwk1, xwk1s, xwv1,
            wgu, wdn, rot, decay, out):
    k_piece = nc.dram_tensor("k_piece", [2, P, NTOK], F16, kind="Internal").ap()
    q_piece = nc.dram_tensor("q_piece", [2, P, NTOK], F16, kind="Internal").ap()

    with ExitStack() as ctx:
        def sb(name, shape, dt=F32):
            return ctx.enter_context(nc.sbuf_tensor(name, shape, dt))

        def sem(name):
            return ctx.enter_context(nc.semaphore(name))

        PS = ctx.enter_context(nc.psum_tensor("PS", [P, 8, 512], F32))
        xt = sb("xt", [P, NB, P])
        xT = sb("xT", [P, NTOK])
        cT = sb("cT", [P, NTOK])
        w0 = sb("w0", [P, 3, 1024])
        w0h = sb("w0h", [P, 3, 1024], F32R)
        w0l = sb("w0l", [P, 3, 1024], F32R)
        wo = sb("wo", [P, G, P])
        xh = sb("xh", [P, NTOK], F32R)
        xl = sb("xl", [P, NTOK], F32R)
        arena = sb("arena", [P, 32768], F16)
        VN = sb("VN", [P, 2048])
        V = sb("V", [P, 2, HP, VW])
        PT = sb("PT", [P, SLOTS_PT, 512])
        On = sb("On", [P, HP, DH0])
        OT = sb("OT", [P, 2, G, P])
        En = sb("En", [P, H, P], F16)
        rowmax = sb("rowmax", [P, P])
        MR = sb("MR", [P, 2, P], F16)
        ident = sb("ident", [P, P])
        ident_b = sb("ident_b", [P, P], BF16)
        maskq = sb("maskq", [P, P], BF16)
        maskk = sb("maskk", [P, P], BF16)
        res = sb("res", [P, NB, P])
        stats = sb("stats", [P, NB, 6])
        mv = sb("mv", [P, NB, 2])
        rstd = sb("rstd", [P, NB])
        nwt = sb("nwt", [P, 3, NB])
        rec = sb("rec", [P, 2, H])
        wx0 = sb("wx0", [P, 3, P])
        bx0 = sb("bx0", [P, 2])
        bvx0 = sb("bvx0", [P, P])
        wge_s = sb("wge_s", [P, P + NE])
        bge_s = sb("bge_s", [P, P + NE])
        w1 = sb("w1", [P, 3, P])
        b1 = sb("b1", [P, 2])
        bv1_s = sb("bv1_s", [P, P])
        wp1_s = sb("wp1_s", [P, P])
        bp1_s = sb("bp1_s", [P, P])
        wx1 = sb("wx1", [P, 5, P])
        rot_s = sb("rot_s", [P, 4, P])
        decay_s = sb("decay_s", [P, P])
        wgu_s = sb("wgu_s", [P, 2 * INNER])
        wdn_s = sb("wdn_s", [P, INNER])
        wabs = sb("wabs", [P, 4])
        wscl = sb("wscl", [P, 8])
        ones = sb("ones", [P, P])
        hs = sb("hs", [P, 2, 4])
        sm8 = sb("sm8", [P, 8, NB])
        lgt = sb("lgt", [P, NB, NE])

        def part(i, n=4096):
            return arena[:, i * n:(i + 1) * n]
        QA = [part(0), part(1)]
        QB = [part(2), part(3)]
        KA = [part(4), part(5)]
        Kst = arena[:, 0:16384].rearrange("p (n t) -> p n t", n=H)
        Qst = arena[:, 16384:32768].rearrange("p (n t) -> p n t", n=H)


        def flat(x):
            return x.rearrange("p a b -> p (a b)")
        w0f, Onf, OTf, Vf = (flat(w0[:]), flat(On[:]), OT[:].rearrange("p a b c -> p (a b c)"),
                             V[:].rearrange("p a n c -> p (a n c)"))
        tB, tD, kx1 = (w0f[:, i * NTOK:(i + 1) * NTOK] for i in range(3))
        tA, tC = Onf[:, 0:NTOK], Onf[:, NTOK:2 * NTOK]
        On1, OnT1 = tA[:, 0:P], tA[:, P:2 * P]
        kx0, vx0 = OTf[:, 0:NTOK], OTf[:, NTOK:2 * NTOK].rearrange("p (b d) -> p b d", b=NB)
        VE = Vf[:, 0:NB * H * 32]
        vx1 = Vf[:, 4096:5120].rearrange("p (b d) -> p b d", b=NB)
        hb = Vf[:, 5120:6144].rearrange("p (i c) -> p i c", i=2)
        VNh = VN[:].bitcast(F16)
        kph, kpl, qph, qpl = (VNh[:, i * NTOK:(i + 1) * NTOK] for i in range(4))
        wob = flat(wo[:]).bitcast(BF16)
        wgu_i, wdn_i = wob[:, 0:2 * INNER], wob[:, 2 * INNER:3 * INNER]
        ab = arena[:].bitcast(BF16)
        x5q = ab[:, 0:1024].rearrange("p (b d) -> p b d", b=NB)
        x5T = ab[:, 1024:2048]
        hi, hT = (ab[:, 2048 + i * 1024:3072 + i * 1024].rearrange("p (i c) -> p i c", i=2) for i in range(2))
        silu_buf = arena[:, 4096:6144].bitcast(F32).rearrange("p (i c) -> p i c", i=2)

        def head(buf, n):
            return buf[:, n * P:(n + 1) * P]

        def by_column(buf, i):
            v = buf.rearrange("p (n a g t) -> p a g n t", a=2, g=G, t=8)
            return v[:, :, 2 * (i % 4):2 * (i % 4) + 2, :, :]

        def bank(i):
            return PS[:, i, :]

        named = {}

        def s(name):
            if name not in named:
                named[name] = sem(name)
            return named[name]

        qk_in = [sem("qk_in0"), sem("qk_in1")]
        pj_free = [sem("pj_free0"), sem("pj_free1")]
        s_free = [sem(f"s_free{i}") for i in range(3)]
        s1_free = [sem(f"s1_free{i}") for i in range(3)]
        xn_done = sem("xn_done")

        block = ctx.enter_context(nc.Block())

        MT0, MT1, OT0, OT1, Y0, OT2, OT3, Y1 = range(8)

        @block.sync
        def _(sp):
            sp.dma_start(xT[:], x_T).then_inc(s("ld_x"), 16)
            for i, w in enumerate((wk0, wq0, wv0)):
                sp.dma_start(w0[:, i, :], w).then_inc(s("ld_w0"), 16)
            sp.dma_start(cT[:], ctx_T).then_inc(s("ld_ctx"), 16)
            for dst, src in ((wx0[:, 0, :], xwq0), (wx0[:, 1, :], xwk0), (wx0[:, 2, :], xwv0),
                             (bx0[:, 0:1], xbq0), (bx0[:, 1:2], xbk0),
                             (wx1[:, 0, :], xwq1), (wx1[:, 1, :], xwq1s), (wx1[:, 2, :], xwk1),
                             (wx1[:, 3, :], xwk1s), (wx1[:, 4, :], xwv1),
                             (rot_s[:], rot)):
                sp.dma_start(dst, src).then_inc(s("ld_ctx"), 16)
            sp.dma_start(wo[:], wo0).then_inc(s("ld_wo"), 16)
            sp.dma_start(xt[:], x_tok).then_inc(s("ld_wo"), 16)
            for dst, src in ((bvx0[:], xbv0.partition_broadcast(P)), (wge_s[:], wge),
                             (bge_s[:], bge.partition_broadcast(P)),
                             (w1[:, 0:2, :], wqk1), (w1[:, 2, :], wv1), (b1[:], bqk1),
                             (bv1_s[:], bv1.partition_broadcast(P)), (wp1_s[:], wp1),
                             (bp1_s[:], bp1.partition_broadcast(P)), (decay_s[:], decay)):
                sp.dma_start(dst, src).then_inc(s("ld_mid"), 16)
            sp.dma_start(wgu_s[:], wgu).then_inc(s("ld_late"), 16)
            sp.dma_start(wdn_s[:], wdn).then_inc(s("ld_late"), 16)

            for p in range(NPAIR):
                b = p % 2
                for split, count, dst in ((s("qk_hi"), 8 * p + 8, QA), (pj_free[1], 10 * p + 4, QB)):
                    sp.wait_ge(split, count)
                    sp.dma_start(dst[b][64:P, :], dst[b][0:64, :]).then_inc(qk_in[b], 16)

            for h in range(2):
                cols = slice(h * 512, (h + 1) * 512)
                for ready, src, dst in (("kp_hi", kph, k_piece[0]), ("kp_lo", kpl, k_piece[1]),
                                        ("qp_hi", qph, q_piece[0]), ("qp_lo", qpl, q_piece[1])):
                    sp.wait_ge(s(ready), h + 1)
                    sp.dma_start(dst[:, cols], src[:, cols]).then_inc(s("piece_out"), 16)
                sp.wait_ge(s("piece_out"), 64 * (h + 1))
                sp.wait_ge(s("stack_zero"), 1)
                for i, (kp, qp) in enumerate(((0, 0), (0, 1), (1, 0), (1, 1))):
                    for stack, piece, x in ((Kst, k_piece, kp), (Qst, q_piece, qp)):
                        sp.dma_start(stack[8 * i:8 * i + 8, :, cols],
                                     piece[x].rearrange("(n d) t -> d n t", d=DH1)[:, :, cols])\
                          .then_inc(s(f"stack_in{h}"), 16)
            for b in range(NB):
                sp.wait_ge(xn_done, 5 * NB + b + 1)
                sp.dma_start(out[b], xt[:, b, :]).then_inc(s("out_sem"), 16)
            sp.wait_ge(s("out_sem"), 16 * NB)

        @block.gpsimd
        def _(pool):
            step = [0]

            def link(ins):
                step[0] += 1
                ins.then_inc(s("pool_step"), 1)
                pool.wait_ge(s("pool_step"), step[0])

            pool.memset(ones[:], 1.0)
            pool.memset(ident[:], 0.0)
            pool.memset(ident_b[:], 0.0)
            pool.memset(En[:], 0.0)
            pool.memset(maskq[:], 0.0)
            pool.memset(maskk[:], 0.0)
            pool.memset(MR[:], 0.0)
            link(pool.memset(V[:, :, :, DH0:VW], 0.0))
            link(pool.memset(V[:, :, :, DH0:DH0 + 1], 1.0))
            for m in (ident, ident_b):
                pool.affine_select(out=m[:], in_=m[:], compare_op=ALU.not_equal, fill=1.0,
                                   base=0, pattern=[[-1, P]], channel_multiplier=1)
            link(pool.affine_select(out=En[:], in_=En[:], compare_op=ALU.not_equal, fill=1.0,
                                    base=0, pattern=[[-1, H], [0, P]], channel_multiplier=1))
            pool.affine_select(out=En[:], in_=En[:], compare_op=ALU.not_equal, fill=1.0,
                               base=-32, pattern=[[-1, H], [0, P]], channel_multiplier=1)
            pool.affine_select(out=maskq[:], in_=maskq[:], compare_op=ALU.is_ge, fill=MASKED,
                               base=0, pattern=[[-1, P]], channel_multiplier=1)
            pool.affine_select(out=maskk[:], in_=maskk[:], compare_op=ALU.is_ge, fill=MASKED,
                               base=0, pattern=[[1, P]], channel_multiplier=-1)\
                .then_inc(s("setup"), 1)
            pool.wait_ge(xn_done, NB)
            pool.tensor_tensor(tB.rearrange("p (b d) -> p b d", b=NB), xt[:],
                               bvx0[:].unsqueeze(1).broadcast_to([P, NB, P]), ALU.add)\
                .then_inc(s("x1b"), 1)
            pool.memset(arena[:].bitcast(F32), 0.0).then_inc(s("stack_zero"), 1)
            link(pool.memset(VE, 0.0))
            pool.memset(VE.rearrange("p (x c) -> p x c", c=32)[:, :, DH1:DH1 + 1], 1.0)\
                .then_inc(s("ve_ones"), 1)
            pool.wait_ge(s("w_scale"), 1)
            for n, (src, dst, i) in enumerate(((wgu_s[:, 0:INNER], wgu_i[:, 0:INNER], 0),
                                               (wgu_s[:, INNER:2 * INNER], wgu_i[:, INNER:2 * INNER], 1),
                                               (wdn_s[:], wdn_i[:], 2))):
                link(pool.tensor_scalar(src, src, wscl[:, 4 + i:5 + i], MAGIC, ALU.mult, ALU.add))
                link(pool.tensor_scalar(src, src, MAGIC + 1.0, MAGIC - 1.0, ALU.min, ALU.max))
                pool.tensor_scalar(dst, src, MAGIC, None, ALU.subtract).then_inc(s("w_int"), 1)
            pool.wait_ge(xn_done, 3 * NB)
            pool.tensor_tensor(tB.rearrange("p (b d) -> p b d", b=NB), xt[:],
                               bp1_s[:].unsqueeze(1).broadcast_to([P, NB, P]), ALU.add)\
                .then_inc(s("x3b"), 1)
            for h in range(2):
                cols = slice(h * 512, (h + 1) * 512)
                pool.wait_ge(s("q_rot"), h + 1)
                pool.tensor_tensor(tA[:, cols], tA[:, cols], tC[:, cols], ALU.add)\
                    .then_inc(s("qx1"), 1)


        def q_use(b, q):
            return q if b == 0 else 4 + 8 * (b - 1) + 2 * q

        def k_use(b, q):
            return 4 + 8 * b + 2 * q + 1 if b + 1 < NB else 4 + 8 * b + q

        @block.tensor
        def _(pe):
            mm, turn = nc.tensor.matmul, nc.tensor.transpose

            def halves(event, out0, lhsT, rhs):
                for h in range(2):
                    mm(bank(out0 + h), lhsT, rhs[:, h * 512:(h + 1) * 512], start=True, stop=True)\
                        .then_inc(s(event), 1)

            def tiles(event, out0, lhsT, rhs, shared=True):
                for b in range(NB):
                    m = mm(bank(out0 + b // 4)[:, (b % 4) * P:(b % 4 + 1) * P], lhsT[:, b * P:(b + 1) * P],
                           rhs if shared else rhs[:, b * P:(b + 1) * P], start=True, stop=True)
                    if b % 4 == 3:
                        m.then_inc(s(event), 1)

            pe.wait_ge(s("setup"), 1)
            def project(p, i):
                w, slot = i // 4, i % 2
                if p or i >= 2:
                    pe.wait_ge(pj_free[slot], 10 * p + i // 2)
                for gi in range(2):
                    g = slice((2 * (i % 4) + gi) * P, (2 * (i % 4) + gi + 1) * P)
                    dst = bank(slot)[:, gi * TP:(gi + 1) * TP]
                    x = slice(p * TP, (p + 1) * TP)
                    mm(dst, w0l[:, w, g], xh[:, x], start=True, stop=False)
                    mm(dst, w0h[:, w, g], xl[:, x], start=False, stop=False)
                    m = mm(dst, w0h[:, w, g], xh[:, x], start=False, stop=True)
                m.then_inc(s("proj_done"), 1)

            def turn_v(p, q):
                i = NPROJ + q
                pe.wait_ge(pj_free[i % 2], 10 * p + i // 2)
                if q == 0:
                    pe.wait_ge(pj_free[1], 10 * p + 6)
                for h in range(4):
                    m = turn(bank(i % 2)[0:64, h * P:(h + 1) * P],
                             VN[:, (4 * q + h) * 64:(4 * q + h + 1) * 64], ident[:])
                m.then_inc(s("proj_done"), 1)

            def scores_q(p, q):
                w = 16 * p + q
                if q == 0:
                    pe.wait_ge(qk_in[p % 2], 32 * (p // 2 + 1))
                if w >= 3:
                    pe.wait_ge(s_free[w % 3], w // 3)
                for h in range(4):
                    n, dst = 4 * q + h, bank(2 + w % 3)[:, h * P:(h + 1) * P]
                    mm(dst, head(QB[p % 2], n), head(KA[p % 2], n), start=True, stop=False)
                    m = mm(dst, head(QA[p % 2], n), head(KA[p % 2], n), start=False, stop=True)
                m.then_inc(s("scores_done"), 1)

            def scores_k(p, q):
                w, b = 16 * p + 8 + q, 2 * p + q // 4
                pe.wait_ge(s_free[w % 3], w // 3)
                pe.wait_ge(s("turn_free"), 8 * p + q // 4 + 1)
                for h in range(4):
                    n, dst = 4 * q + h, bank(2 + w % 3)[:, h * P:(h + 1) * P]
                    mm(dst, head(KA[p % 2], n), head(QB[p % 2], n), start=True, stop=False)
                    mm(dst, head(KA[p % 2], n), head(QA[p % 2], n), start=False, stop=False)
                    m = mm(dst, En[:, n % H, :], MR[:, b % 2, :], start=False, stop=True)
                m.then_inc(s("scores_done"), 1)

            def weigh(p, q):
                v, w, i = 8 * p + q, 16 * p + 8 + q, NPROJ + q
                pe.wait_ge(s_free[w % 3], w // 3 + 1)
                pe.wait_ge(pj_free[i % 2], 10 * p + i // 2 + 1)
                if v >= 2:
                    pe.wait_ge(s("norm_done"), v - 1)
                for h in range(4):
                    m = mm(bank(5 + v % 2)[:, h * VW:(h + 1) * VW], PT[:, v % SLOTS_PT, h * P:(h + 1) * P],
                           V[:, p % 2, 4 * q + h, :], start=True, stop=True)
                m.then_inc(s("pv_done"), 1)

            def turn_max(p, half):
                z, w = 8 * p + (MT0, MT1)[half], 16 * p + 4 * half + 3
                if z:
                    pe.wait_ge(s("turn_free"), z)
                pe.wait_ge(s_free[w % 3], w // 3 + 1)
                b = 2 * p + half
                turn(bank(7)[0:H, 0:P], rowmax[:, b * H:(b + 1) * H], ident[:]).then_inc(s("turn_done"), 1)

            def turn_out(p, o):
                z = 8 * p + (OT0, OT1, OT2, OT3)[o]
                pe.wait_ge(s("turn_free"), z)
                pe.wait_ge(s("norm_done"), 8 * p + 2 * o + 2)
                for r in range(4):
                    n = 8 * o + 2 * r
                    m = turn(bank(7)[:, r * P:(r + 1) * P], On[:, n:n + 2, :], ident[:])
                m.then_inc(s("turn_done"), 1)

            def project_out(p, half):
                z, b = 8 * p + (Y0, Y1)[half], 2 * p + half
                pe.wait_ge(s("turn_free"), z)
                for g in range(G):
                    m = mm(bank(7)[:, 0:P], OT[:, b % 2, g, :], wo[:, g, :], start=(g == 0), stop=(g == G - 1))
                m.then_inc(s("turn_done"), 1)

            pe.wait_ge(s("hi"), 4)
            pe.wait_ge(s("lo"), 4)
            for i in range(NPROJ):
                project(0, i)
            for q in range(QP):
                turn_v(0, q)
            pe.wait_ge(s("w_abs"), 1)
            mm(bank(2)[:, 0:3], ones[:], wabs[:, 0:3], start=True, stop=True).then_inc(s("pe_wsum"), 1)
            pe.wait_ge(s("w_scale"), 1)
            for p in range(NPAIR):
                for q in range(QP):
                    scores_q(p, q)
                    if p + 1 < NPAIR:
                        project(p + 1, q)
                    if p and q == 1:
                        turn_out(p - 1, 3)
                    if p and q == 3:
                        project_out(p - 1, 1)
                    if q == 5:
                        turn_max(p, 0)
                if p + 1 < NPAIR:
                    for i in range(8, NPROJ):
                        project(p + 1, i)
                turn_max(p, 1)
                for q in range(QP):
                    scores_k(p, q)
                    if p + 1 < NPAIR:
                        turn_v(p + 1, q)
                    if q:
                        weigh(p, q - 1)
                    if q == 3:
                        turn_out(p, 0)
                    if q == 5:
                        turn_out(p, 1)
                    if q == 6:
                        if p == 0:
                            pe.wait_ge(s("ld_wo"), 32)
                        project_out(p, 0)
                    if q == 7:
                        turn_out(p, 2)
                weigh(p, QP - 1)
            turn_out(NPAIR - 1, 3)
            project_out(NPAIR - 1, 1)

            def turn_x(k, name, at=0):
                for b in range(NB):
                    pe.wait_ge(xn_done, NB * k + b + 1)
                    m = turn(bank(at + b // 4)[:, (b % 4) * P:(b % 4 + 1) * P], xt[:, b, :], ident[:])
                    if b % 4 == 3:
                        m.then_inc(s(name), 1)

            def wait_xT(name):
                pe.wait_ge(s(name + "_act"), 1)
                pe.wait_ge(s(name + "_dve"), 1)

            pe.wait_ge(s("ld_ctx"), 16 * 12)
            halves("pe_kx0", 2, wx0[:, 1, :], cT[:])
            tiles("pe_vx0", 4, cT[:], wx0[:, 2, :])
            halves("pe_k1", 0, wx1[:, 2, :], cT[:])
            pe.wait_ge(s("turn_free"), 8 * NPAIR)
            halves("pe_k1s", 6, wx1[:, 3, :], cT[:])
            pe.wait_ge(s("kx0"), 2)
            turn_x(0, "t0", 2)
            wait_xT("x0T")
            halves("pe_q0", 2, wx0[:, 0, :], xT[:])
            pe.wait_ge(s("vx0"), 2)
            pe.wait_ge(s("q0_act"), 1)
            pe.wait_ge(s("q0_dve"), 1)
            tiles("pe_s0", 4, tA, kx0, shared=False)
            pe.wait_ge(s("k1_rot"), 2)
            for h in range(2):
                pe.wait_ge(s("exp0"), h + 1)
                for b in range(4):
                    m = turn(bank(6 + h)[:, b * P:(b + 1) * P], tC[:, (4 * h + b) * P:(4 * h + b + 1) * P], ident[:])
                m.then_inc(s("pe_p0"), 1)
            pe.wait_ge(s("p0T_act"), 1)
            pe.wait_ge(s("p0T_dve"), 1)
            for b in range(NB):
                m = mm(bank(b // 4)[:, (b % 4) * P:(b % 4 + 1) * P], tA[:, b * P:(b + 1) * P], vx0[:, b, :],
                       start=True, stop=True)
                if b % 4 == 3:
                    m.then_inc(s("pe_o0"), 1)

            tiles("pe_vx1", 6, cT[:], wx1[:, 4, :])

            turn_x(1, "t1")
            wait_xT("x1T")
            pe.wait_ge(s("ld_mid"), 160)
            for b in range(NB):
                m = mm(bank(2 + b // 2)[:, (b % 2) * 256:(b % 2) * 256 + P + NE], xT[:, b * P:(b + 1) * P],
                       wge_s[:], start=True, stop=True)
            m.then_inc(s("pe_ffn"), 1)

            turn_x(2, "t2")
            wait_xT("x2T")
            pe.wait_ge(s("vx1"), 2)
            halves("pe_k1a", 2, w1[:, 1, :], xT[:])
            halves("pe_q1a", 4, w1[:, 0, :], xT[:])
            tiles("pe_v1a", 6, xT[:], w1[:, 2, :])

            def scores1(w, b, q, of_keys):
                if w < 3:
                    pe.wait_ge(s("kp_lo"), 2)
                    pe.wait_ge(s("qp_lo"), 2)
                    pe.wait_ge(s("ve_done"), 2)
                else:
                    pe.wait_ge(s1_free[w % 3], w // 3)
                pe.wait_ge(s(f"stack_in{b // 4}"), 128)
                if of_keys:
                    pe.wait_ge(s("mr1_done"), b + 1)
                t = slice(b * P, (b + 1) * P)
                dst = bank(w % 3)
                mm(dst, ident_b[:], (maskk if of_keys else maskq)[:].unsqueeze(1).broadcast_to([P, 4, P]),
                   start=True, stop=False)
                for h in range(4):
                    n, part_ = 4 * q + h, dst[:, h * P:(h + 1) * P]
                    if of_keys:
                        mm(part_, Kst[:, n, t], Qst[:, n, t], start=False, stop=False)
                        m = mm(part_, En[:, n, :], MR[:, b % 2, :], start=False, stop=(h == 3))
                    else:
                        m = mm(part_, Qst[:, n, t], Kst[:, n, t], start=False, stop=(h == 3))
                m.then_inc(s("scores1_done"), 1)

            def weigh1(b, q):
                v = 4 * b + q
                w = k_use(b, q)
                pe.wait_ge(s1_free[w % 3], w // 3 + 1)
                if q == 0 and b >= 2:
                    pe.wait_ge(s("o1_out"), b - 1)
                for r in range(4):
                    m = mm(bank(3 + b % 2)[32 * r:32 * r + 32, q * P:(q + 1) * P],
                           VE[:, (b * H + 4 * q + r) * 32:(b * H + 4 * q + r + 1) * 32],
                           PT[:, v % SLOTS_PT, r * P:(r + 1) * P], start=True, stop=True)
                m.then_inc(s("pv1_done"), 1)

            def turn_max1(b):
                w = q_use(b, 3)
                pe.wait_ge(s1_free[w % 3], w // 3 + 1)
                if b:
                    pe.wait_ge(s("mr1_done"), b)
                turn(bank(5)[0:H, 0:P], rowmax[:, b * H:(b + 1) * H], ident[:]).then_inc(s("pe_mt1"), 1)

            def outputs1(b):
                pe.wait_ge(s("o1_out"), b + 1)
                if b:
                    pe.wait_ge(s("on1_done"), b)
                for q in range(4):
                    m = turn(bank(6)[:, q * P:(q + 1) * P], hb[:, b % 2, q * P:(q + 1) * P], ident[:])
                m.then_inc(s("pe_ot1"), 1)
                pe.wait_ge(s("on1_done"), b + 1)
                if b:
                    pe.wait_ge(s("res1_done"), b)
                turn(bank(7)[:, 0:P], On1, ident[:]).then_inc(s("pe_on1"), 1)
                pe.wait_ge(s("onT1_done"), b + 1)
                mm(bank(7)[:, P:2 * P], OnT1, wp1_s[:], start=True, stop=True).then_inc(s("pe_y1"), 1)

            pe.wait_ge(s("ve_done"), 2)
            for b in range(NB + 1):
                for q in range(4):
                    if b < NB:
                        scores1(q_use(b, q), b, q, False)
                    if b:
                        scores1(k_use(b - 1, q), b - 1, q, True)
                        if q:
                            weigh1(b - 1, q - 1)
                    if b >= 2 and q == 0:
                        outputs1(b - 2)
                if b < NB:
                    turn_max1(b)
                if b:
                    weigh1(b - 1, 3)
            outputs1(NB - 1)

            turn_x(3, "t3")
            wait_xT("x3T")
            halves("pe_qr", 2, wx1[:, 0, :], xT[:])
            halves("pe_qs", 4, wx1[:, 1, :], xT[:])
            for h in range(2):
                pe.wait_ge(s("qx1"), h + 1)
                for b in range(4 * h, 4 * h + 4):
                    m = mm(bank(6 + h)[:, (b % 4) * P:(b % 4 + 1) * P], kx1[:, b * P:(b + 1) * P],
                           tA[:, b * P:(b + 1) * P], start=True, stop=True)
                m.then_inc(s("pe_sx1"), 1)
            for h in range(2):
                pe.wait_ge(s("sx1"), h + 1)
                for b in range(4 * h, 4 * h + 4):
                    m = mm(bank(h)[:, (b % 4) * P:(b % 4 + 1) * P], tD[:, b * P:(b + 1) * P],
                           vx1[:, b, :], start=True, stop=True)
                m.then_inc(s("pe_ox1"), 1)

            pe.wait_ge(s("x5q"), 1)
            for b in range(NB):
                m = turn(bank(6)[:].bitcast(BF16)[:, b * P:(b + 1) * P], x5q[:, b, :], ident_b[:])
            m.then_inc(s("pe_x5T"), 1)
            pe.wait_ge(s("x5T"), 1)
            pe.wait_ge(s("w_int"), 3)

            def down(b):
                pe.wait_ge(s("h_int"), b + 1)
                if b:
                    pe.wait_ge(s("hT"), b)
                for c in range(4):
                    m = turn(bank(6)[:].bitcast(BF16)[:, c * P:(c + 1) * P], hi[:, b % 2, c * P:(c + 1) * P], ident_b[:])
                m.then_inc(s("pe_hT"), 1)
                pe.wait_ge(s("hT"), b + 1)
                if b:
                    pe.wait_ge(s("res_f1"), b)
                for c in range(4):
                    m = mm(bank(7)[:, 0:P], hT[:, b % 2, c * P:(c + 1) * P], wdn_i[:, c * P:(c + 1) * P],
                           start=(c == 0), stop=(c == 3))
                m.then_inc(s("pe_down"), 1)

            for b in range(NB + 1):
                if b < NB:
                    if b >= 3:
                        pe.wait_ge(s("h_done"), b - 2)
                    for i in range(2):
                        m = mm(bank(2 * (b % 3) + i), x5T[:, b * P:(b + 1) * P], wgu_i[:, i * INNER:(i + 1) * INNER],
                               start=True, stop=True)
                    m.then_inc(s("pe_gu"), 1)
                if b:
                    down(b - 1)


        @block.scalar
        def _(act):
            step = [0]
            fn = nc.scalar.activation

            def tok(x):
                return x.rearrange("p (b d) -> p b d", b=4)

            def half(x, h):
                return x[:, h * 512:(h + 1) * 512]

            act.wait_ge(s("ld_x"), 16)
            fn(xh[:], xT[:], ACT.Copy).then_inc(s("hi"), 1)
            act.wait_ge(s("ld_w0"), 48)
            for w in range(3):
                fn(w0h[:, w, :], w0[:, w, :], ACT.Copy).then_inc(s("hi"), 1)
            def by_head(buf, i):
                return buf.rearrange("p (n g t) -> p g n t", g=G, t=8)[:, 2 * (i % 4):2 * (i % 4) + 2, :, :]

            def empty_projection(p, i):
                src = bank(i % 2).rearrange("p (g n t) -> p g n t", g=2, t=8)
                act.wait_ge(s("proj_done"), 20 * p + i + 1)
                if i < 8:
                    if p >= 2:
                        act.wait_ge(s("scores_done"), 16 * (p - 1))
                    dst = by_column((KA, QA)[i // 4][p % 2][0:64, :], i)
                    for a in range(2):
                        m = fn(dst[:, a], src[a * 64:(a + 1) * 64], ACT.Copy)
                    m.then_inc(s("qk_hi"), 1)
                else:
                    fn(by_head(VN[:], i), src, ACT.Copy).then_inc(pj_free[i % 2], 1)

            def empty_turned_v(p, q):
                i = NPROJ + q
                act.wait_ge(s("proj_done"), 20 * p + i + 1)
                if q == 0 and p >= 2:
                    act.wait_ge(s("pv_done"), 8 * (p - 1))
                src = bank(i % 2)[0:64, :].rearrange("p (n a d) -> p n a d", n=4, a=2)
                for a in range(2):
                    m = fn(V[a * 64:(a + 1) * 64, p % 2, 4 * q:4 * q + 4, 0:DH0], src[:, :, a, :], ACT.Copy)
                m.then_inc(pj_free[i % 2], 1)

            def exp0(p, q):
                v, w = 8 * p + q, 16 * p + 8 + q
                act.wait_ge(s("scores_done"), w + 1)
                if v >= SLOTS_PT:
                    act.wait_ge(s("pv_done"), v - SLOTS_PT + 1)
                fn(PT[:, v % SLOTS_PT, :], bank(2 + w % 3), ACT.Exp, scale=SCALE0).then_inc(s_free[w % 3], 1)

            for i in range(NPROJ):
                empty_projection(0, i)
            act.wait_ge(s("setup"), 1)
            for q in range(QP):
                empty_turned_v(0, q)
            for p in range(NPAIR):
                if p + 1 < NPAIR:
                    for i in range(NPROJ):
                        empty_projection(p + 1, i)
                for q in range(QP):
                    exp0(p, q)
                    if p + 1 < NPAIR:
                        empty_turned_v(p + 1, q)

            def copy_half(event_in, dst, src, event_out, n=1):
                act.wait_ge(s(event_in), n)
                fn(dst, src, ACT.Copy).then_inc(s(event_out), 1)

            for h in range(2):
                act.wait_ge(s("pe_kx0"), h + 1)
                if h == 0:
                    act.wait_ge(s("turn_done"), 8 * NPAIR)
                fn(half(kx0, h), bank(2 + h), ACT.Identity, bias=bx0[:, 1:2]).then_inc(s("kx0"), 1)
            for h in range(2):
                act.wait_ge(s("pe_vx0"), h + 1)
                fn(vx0[:, 4 * h:4 * h + 4, :], tok(bank(4 + h)), ACT.Copy).then_inc(s("vx0"), 1)
            copy_half("t0", half(xT, 0), bank(2), "x0T_act")
            act.wait_ge(s("pe_q0"), 1)
            fn(half(tA, 0), bank(2), ACT.Identity, bias=bx0[:, 0:1]).then_inc(s("q0_act"), 1)
            for h in range(2):
                act.wait_ge(s("sub0"), h + 1)
                fn(half(tC, h), half(tC, h), ACT.Exp, scale=SCALEX).then_inc(s("exp0"), 1)
            copy_half("pe_p0", half(tA, 0), bank(6), "p0T_act")
            for h in range(2):
                act.wait_ge(s("pe_vx1"), h + 1)
                fn(vx1[:, 4 * h:4 * h + 4, :], tok(bank(6 + h)), ACT.Copy).then_inc(s("vx1"), 1)
            copy_half("t1", half(xT, 0), bank(0), "x1T_act")
            act.wait_ge(s("gate_sub"), 1)
            fn(lgt[:], lgt[:], ACT.Exp).then_inc(s("gate_exp"), 1)

            copy_half("t2", half(xT, 0), bank(0), "x2T_act")
            act.wait_ge(s("ld_mid"), 160)
            for event, b0, dst, i, out_ in (("pe_k1a", 2, kph, 1, "kp_hi"), ("pe_q1a", 4, qph, 0, "qp_hi")):
                for h in range(2):
                    act.wait_ge(s(event), h + 1)
                    fn(half(dst, h), bank(b0 + h), ACT.Identity, bias=b1[:, i:i + 1]).then_inc(s(out_), 1)

            def exp1(b, q):
                v, w = 4 * b + q, k_use(b, q)
                act.wait_ge(s("scores1_done"), w + 1)
                if v >= SLOTS_PT:
                    act.wait_ge(s("pv1_done"), v - SLOTS_PT + 1)
                fn(PT[:, v % SLOTS_PT, :], bank(w % 3), ACT.Exp, scale=SCALE1).then_inc(s1_free[w % 3], 1)

            def empty_o1(b):
                act.wait_ge(s("pv1_done"), 4 * b + 4)
                if b >= 2:
                    act.wait_ge(s("pe_ot1"), b - 1)
                fn(hb[:, b % 2, :], bank(3 + b % 2), ACT.Copy).then_inc(s("o1_out"), 1)

            def empty_on1(b):
                act.wait_ge(s("pe_on1"), b + 1)
                if b:
                    act.wait_ge(s("pe_y1"), b)
                fn(OnT1, bank(7)[:, 0:P], ACT.Copy).then_inc(s("onT1_done"), 1)

            for b in range(1, NB + 1):
                for q in range(4):
                    exp1(b - 1, q)
                    if q == 0 and b >= 2:
                        empty_on1(b - 2)
                empty_o1(b - 1)
            empty_on1(NB - 1)

            copy_half("t3", half(xT, 0), bank(0), "x3T_act")

            act.wait_ge(s("x5_round"), 1)
            fn(x5q.rearrange("p b d -> p (b d)"), tA, ACT.Copy, bias=-MAGIC).then_inc(s("x5q"), 1)
            act.wait_ge(s("pe_x5T"), 1)
            fn(x5T, bank(6)[:].bitcast(BF16), ACT.Copy).then_inc(s("x5T"), 1)

            def finish_h(b):
                act.wait_ge(s("h_round"), b + 1)
                if b >= 2:
                    act.wait_ge(s("pe_hT"), b - 1)
                fn(hi[:, b % 2, :], hb[:, b % 2, :], ACT.Copy, bias=-MAGIC).then_inc(s("h_int"), 1)
                act.wait_ge(s("pe_hT"), b + 1)
                if b >= 2:
                    act.wait_ge(s("pe_down"), b - 1)
                fn(hT[:, b % 2, :], bank(6)[:].bitcast(BF16)[:, 0:INNER], ACT.Copy).then_inc(s("hT"), 1)

            act.wait_ge(s("gu_scale"), 2)
            for b in range(NB + 1):
                if b < NB:
                    act.wait_ge(s("pe_gu"), b + 1)
                    if b >= 2:
                        act.wait_ge(s("h_done"), b - 1)
                    fn(silu_buf[:, b % 2, :], bank(2 * (b % 3)), ACT.Silu, scale=sm8[:, 4, b:b + 1])\
                        .then_inc(s("silu"), 1)
                if b:
                    finish_h(b - 1)

        @block.vector
        def _(dve):
            step = [0]
            V_ = nc.vector
            tt, ts, stt = V_.tensor_tensor, V_.tensor_scalar, V_.scalar_tensor_tensor

            def link(ins):
                step[0] += 1
                ins.then_inc(s("dve_step"), 1)
                dve.wait_ge(s("dve_step"), step[0])

            def tok(x):
                return x.rearrange("p (b d) -> p b d", b=4)

            def half(x, h):
                return x[:, h * 512:(h + 1) * 512]

            def over(x, n, width):
                return x.unsqueeze(1).broadcast_to([P, n, width])

            def across(x, n, width):
                return x.unsqueeze(2).broadcast_to([P, n, width])

            dve.wait_ge(s("hi"), 1)
            tt(xl[:], xT[:], xh[:].bitcast(F32), ALU.subtract).then_inc(s("lo"), 1)
            for w in range(3):
                dve.wait_ge(s("hi"), w + 2)
                tt(w0l[:, w, :], w0[:, w, :], w0h[:, w, :].bitcast(F32), ALU.subtract).then_inc(s("lo"), 1)
            def lower_parts(p, i):
                src = bank(i % 2).rearrange("p (g n t) -> p g n t", g=2, t=8)
                dve.wait_ge(s("qk_hi"), 8 * p + i + 1)
                upper = by_column((KA, QA)[i // 4][p % 2][0:64, :], i)
                lower = by_column((KA[p % 2][64:P, :], QB[p % 2][0:64, :])[i // 4], i)
                for a in range(2):
                    m = tt(lower[:, a], src[a * 64:(a + 1) * 64], upper[:, a], ALU.subtract)
                m.then_inc(pj_free[i % 2], 1)

            def maxima(p, q):
                w = 16 * p + q
                dve.wait_ge(s("scores_done"), w + 1)
                V_.reduce_max(rowmax[:, HP * p + 4 * q:HP * p + 4 * q + 4],
                              tok(bank(2 + w % 3)), AX_X).then_inc(s_free[w % 3], 1)

            def negated_maxima(event, count, src, b, done):
                dve.wait_ge(s(event), count)
                link(ts(MR[0:H, b % 2, :], src[0:H, 0:P], -1.0, None, ALU.mult))
                stt(MR[32:32 + H, b % 2, :], src[0:H, 0:P], -1.0, MR[0:H, b % 2, :],
                    ALU.mult, ALU.subtract).then_inc(s(done), 1)

            def max_rows(p, hf):
                b = 2 * p + hf
                if p:
                    dve.wait_ge(s("scores_done"), 16 * (p - 1) + 8 + 4 * (hf + 1))
                negated_maxima("turn_done", 8 * p + (MT0, MT1)[hf] + 1, bank(7), b, "turn_free")

            def normalize(p, q):
                v = 8 * p + q
                o = bank(5 + v % 2)[:, 0:4 * VW].rearrange("p (n d) -> p n d", n=4)
                dve.wait_ge(s("pv_done"), v + 1)
                if q == 0 and p:
                    dve.wait_ge(s("turn_done"), 8 * p)
                link(V_.reciprocal(rec[:, v % 2, 0:4], o[:, :, DH0]))
                tt(On[:, 4 * q:4 * q + 4, :], o[:, :, 0:DH0], across(rec[:, v % 2, 0:4], 4, DH0), ALU.mult)\
                    .then_inc(s("norm_done"), 1)

            def place_out(p, o):
                b = 2 * p + o // 2
                dve.wait_ge(s("turn_done"), 8 * p + (OT0, OT1, OT2, OT3)[o] + 1)
                src = bank(7).rearrange("p (r a g t) -> p r a g t", r=4, a=2, g=G)
                dst = OT[:, b % 2, :, :].rearrange("p g (m h t) -> p h m g t", h=2, t=8)
                if p and o % 2 == 0:
                    dve.wait_ge(s("turn_done"), 8 * (p - 1) + (Y0, Y1)[o // 2] + 1)
                for h in range(2):
                    for a in range(2):
                        m = V_.tensor_copy(dst[a * 64:(a + 1) * 64, h, 4 * (o % 2):4 * (o % 2) + 4],
                                           src[h * 64:(h + 1) * 64, :, a])
                m.then_inc(s("turn_free"), 1)

            def add_out(p, hf):
                b = 2 * p + hf
                dve.wait_ge(s("turn_done"), 8 * p + (Y0, Y1)[hf] + 1)
                tt(res[:, b, :], bank(7)[:, 0:P], xt[:, b, :], ALU.add).then_inc(s("turn_free"), 1)

            for i in range(8):
                lower_parts(0, i)
            dve.wait_ge(s("ld_late"), 32)
            for i in range(2):
                V_.tensor_reduce(wabs[:, i:i + 1], wgu_s[:, i * INNER:(i + 1) * INNER], AX_X, ALU.add,
                                 apply_absolute_value=True)
            V_.tensor_reduce(wabs[:, 2:3], wdn_s[:], AX_X, ALU.add, apply_absolute_value=True)\
                .then_inc(s("w_abs"), 1)
            dve.wait_ge(s("pe_wsum"), 1)
            link(ts(wscl[:, 0:3], bank(2)[:, 0:3], 1.0 / NW, 1e-5, ALU.mult, ALU.max))
            V_.reciprocal(wscl[:, 4:7], wscl[:, 0:3]).then_inc(s("w_scale"), 1)
            for p in range(NPAIR):
                for q in range(QP):
                    maxima(p, q)
                    if p + 1 < NPAIR:
                        lower_parts(p + 1, q)
                    if p and q == 1:
                        place_out(p - 1, 3)
                    if p and q == 3:
                        add_out(p - 1, 1)
                    if q == 5:
                        max_rows(p, 0)
                max_rows(p, 1)
                for q in range(QP):
                    if q:
                        normalize(p, q - 1)
                    if q == 3:
                        place_out(p, 0)
                    if q == 5:
                        place_out(p, 1)
                    if q == 6:
                        if p == 0:
                            dve.wait_ge(s("ld_wo"), 32)
                        add_out(p, 0)
                    if q == 7:
                        place_out(p, 2)
                normalize(p, QP - 1)
            place_out(NPAIR - 1, 3)
            add_out(NPAIR - 1, 1)
            step_res = s("turn_free"), 8 * NPAIR

            def layer_norm(last):
                dve.wait_ge(*last)
                for b in range(NB):
                    m = V_.bn_stats(stats[:, b, :], res[:, b, :])
                link(m)
                for b in range(NB):
                    m = V_.bn_aggr(mv[:, b, :], stats[:, b, :])
                link(m)
                v, y, e = (nwt[:, i, :] for i in range(3))
                link(ts(v, mv[:, :, 1], EPS, None, ALU.add))
                link(ts(e.bitcast(I32), v.bitcast(I32), 1, None, ALU.logical_shift_right))
                link(ts(y.bitcast(I32), e.bitcast(I32), -1, RSQRT_BITS, ALU.mult, ALU.add))
                for i in range(3):
                    link(tt(e, y, y, ALU.mult))
                    link(tt(e, e, v, ALU.mult))
                    link(ts(e, e, -0.5, 1.5, ALU.mult, ALU.add))
                    link(tt(rstd[:] if i == 2 else y, y, e, ALU.mult))
                for b in range(NB):
                    ts(xt[:, b, :], res[:, b, :], mv[:, b, 0:1], rstd[:, b:b + 1], ALU.subtract, ALU.mult)\
                        .then_inc(xn_done, 1)

            def copy_half(event_in, dst, src, event_out, n=2):
                dve.wait_ge(s(event_in), n)
                V_.tensor_copy(dst, src).then_inc(s(event_out), 1)

            layer_norm(step_res)
            copy_half("t0", half(xT, 1), bank(3), "x0T_dve")
            dve.wait_ge(s("ld_ctx"), 16 * 12)
            for h in range(2):
                dve.wait_ge(s("pe_k1s"), h + 1)
                tt(tok(half(tD, h)), tok(bank(h)), over(rot_s[:, 2, :], 4, P), ALU.mult)
                link(tt(tok(half(tC, h)), tok(bank(6 + h)), over(rot_s[:, 3, :], 4, P), ALU.mult))
                tt(half(kx1, h), half(tD, h), half(tC, h), ALU.add).then_inc(s("k1_rot"), 1)
            dve.wait_ge(s("pe_q0"), 2)
            ts(half(tA, 1), bank(3), bx0[:, 0:1], None, ALU.add).then_inc(s("q0_dve"), 1)
            for h in range(2):
                dve.wait_ge(s("pe_s0"), h + 1)
                link(V_.reduce_max(sm8[:, 0, 4 * h:4 * h + 4], tok(bank(4 + h)), AX_X))
                tt(tok(half(tC, h)), tok(bank(4 + h)), across(sm8[:, 0, 4 * h:4 * h + 4], 4, P), ALU.subtract)\
                    .then_inc(s("sub0"), 1)
            for h in range(2):
                dve.wait_ge(s("exp0"), h + 1)
                m = V_.reduce_sum(sm8[:, 1, 4 * h:4 * h + 4], tok(half(tC, h)), AX_X)
            link(m)
            copy_half("pe_p0", half(tA, 1), bank(7), "p0T_dve")
            link(V_.reciprocal(sm8[:, 2, :], sm8[:, 1, :]))
            dve.wait_ge(s("x1b"), 1)
            for b in range(NB):
                dve.wait_ge(s("pe_o0"), b // 4 + 1)
                m = stt(res[:, b, :], bank(b // 4)[:, (b % 4) * P:(b % 4 + 1) * P], sm8[:, 2, b:b + 1],
                        tB[:, b * P:(b + 1) * P], ALU.mult, ALU.add)
            m.then_inc(s("res_x0"), 1)

            layer_norm((s("res_x0"), 1))
            copy_half("t1", half(xT, 1), bank(1), "x1T_dve")
            dve.wait_ge(s("pe_ffn"), 1)
            ge = PS[:, 2:6, :].rearrange("p k (i c) -> p (k i) c", i=2)
            link(tt(lgt[:], ge[:, :, P:P + NE], over(bge_s[:, P:P + NE], NB, NE), ALU.add))
            link(V_.reduce_max(sm8[:, 0, :], lgt[:], AX_X))
            tt(lgt[:], lgt[:], across(sm8[:, 0, :], NB, NE), ALU.subtract).then_inc(s("gate_sub"), 1)
            tt(tC.rearrange("p (b d) -> p b d", b=NB), ge[:, :, 0:P], over(bge_s[:, 0:P], NB, P), ALU.add)
            dve.wait_ge(s("gate_exp"), 1)
            link(V_.reduce_sum(sm8[:, 1, :], lgt[:], AX_X))
            link(V_.reciprocal(sm8[:, 2, :], sm8[:, 1, :]))
            for b in range(NB):
                m = stt(res[:, b, :], tC[:, b * P:(b + 1) * P], sm8[:, 2, b:b + 1], xt[:, b, :],
                        ALU.mult, ALU.add)
            m.then_inc(s("res_f0"), 1)

            layer_norm((s("res_f0"), 1))
            copy_half("t2", half(xT, 1), bank(1), "x2T_dve")
            for hi_, b0, src, dst, i, out_ in (("kp_hi", 2, kph, kpl, 1, "kp_lo"),
                                               ("qp_hi", 4, qph, qpl, 0, "qp_lo")):
                for h in range(2):
                    dve.wait_ge(s(hi_), h + 1)
                    stt(half(dst, h), bank(b0 + h), b1[:, i:i + 1], half(src, h), ALU.add, ALU.subtract)\
                        .then_inc(s(out_), 1)
            dve.wait_ge(s("ve_ones"), 1)
            for h in range(2):
                dve.wait_ge(s("pe_v1a"), h + 1)
                tt(VE.rearrange("p (b n c) -> p b n c", b=NB, n=H)[:, 4 * h:4 * h + 4, :, 0:DH1],
                   bank(6 + h).rearrange("p (b n c) -> p b n c", b=4, n=H),
                   bv1_s[:].rearrange("p (n c) -> p n c", n=H).unsqueeze(1).broadcast_to([P, 4, H, DH1]),
                   ALU.add).then_inc(s("ve_done"), 1)

            def maxima1(b, q):
                w = q_use(b, q)
                dve.wait_ge(s("scores1_done"), w + 1)
                V_.reduce_max(rowmax[:, b * H + 4 * q:b * H + 4 * q + 4], tok(bank(w % 3)), AX_X)\
                    .then_inc(s1_free[w % 3], 1)

            def max_rows1(b):
                if b >= 2:
                    dve.wait_ge(s("scores1_done"), k_use(b - 2, 3) + 1)
                negated_maxima("pe_mt1", b + 1, bank(5), b, "mr1_done")

            def outputs1(b):
                o = bank(6).rearrange("p (n c) -> p n c", n=H)
                dve.wait_ge(s("pe_ot1"), b + 1)
                link(V_.reciprocal(rec[:, b % 2, :], o[:, :, DH1]))
                if b:
                    dve.wait_ge(s("pe_on1"), b)
                tt(On1.rearrange("p (n c) -> p n c", n=H), o[:, :, 0:DH1], across(rec[:, b % 2, :], H, DH1),
                   ALU.mult).then_inc(s("on1_done"), 1)
                dve.wait_ge(s("pe_y1"), b + 1)
                tt(res[:, b, :], bank(7)[:, P:2 * P], tB[:, b * P:(b + 1) * P], ALU.add)\
                    .then_inc(s("res1_done"), 1)

            for b in range(NB + 1):
                for q in range(4):
                    if b < NB:
                        maxima1(b, q)
                    if q == 0 and b == 2:
                        dve.wait_ge(s("x3b"), 1)
                    if q == 0 and b >= 2:
                        outputs1(b - 2)
                if b < NB:
                    max_rows1(b)
            outputs1(NB - 1)

            layer_norm((s("res1_done"), NB))
            copy_half("t3", half(xT, 1), bank(1), "x3T_dve")
            for h in range(2):
                dve.wait_ge(s("pe_qr"), h + 1)
                tt(tok(half(tA, h)), tok(bank(2 + h)), over(rot_s[:, 0, :], 4, P), ALU.mult)
                dve.wait_ge(s("pe_qs"), h + 1)
                tt(tok(half(tC, h)), tok(bank(4 + h)), over(rot_s[:, 1, :], 4, P), ALU.mult)\
                    .then_inc(s("q_rot"), 1)
            for h in range(2):
                dve.wait_ge(s("pe_sx1"), h + 1)
                tt(tok(half(tD, h)), tok(bank(6 + h)), over(decay_s[:], 4, P), ALU.mult)\
                    .then_inc(s("sx1"), 1)
            for h in range(2):
                dve.wait_ge(s("pe_ox1"), h + 1)
                m = tt(res[:, 4 * h:4 * h + 4, :], tok(bank(h)), xt[:, 4 * h:4 * h + 4, :], ALU.add)
            m.then_inc(s("res_x1"), 1)

            layer_norm((s("res_x1"), 1))
            dve.wait_ge(xn_done, 5 * NB)
            link(V_.tensor_reduce(sm8[:, 0, :], xt[:], AX_X, ALU.max, apply_absolute_value=True))
            link(ts(sm8[:, 1, :], sm8[:, 0, :], 1e-5, None, ALU.max))
            link(V_.reciprocal(sm8[:, 2, :], sm8[:, 1, :]))
            link(ts(sm8[:, 3, :], sm8[:, 2, :], 127.0, None, ALU.mult))
            for b in range(NB):
                m = ts(tC[:, b * P:(b + 1) * P], xt[:, b, :], sm8[:, 3, b:b + 1], MAGIC, ALU.mult, ALU.add)
            link(m)
            ts(tA, tC, MAGIC + 127.0, MAGIC - 128.0, ALU.min, ALU.max).then_inc(s("x5_round"), 1)
            for i in range(2):
                ts(sm8[:, 4 + i, :], sm8[:, 1, :], 1.0 / 127.0, wscl[:, i:i + 1], ALU.mult, ALU.mult)\
                    .then_inc(s("gu_scale"), 1)
            dve.wait_ge(s("gu_scale"), 2)

            def hidden(b):
                h, sc = hb[:, b % 2, :], hs[:, b % 2, :]
                dve.wait_ge(s("silu"), b + 1)
                if b >= 2:
                    dve.wait_ge(s("h_int"), b - 1)
                ins = stt(h, bank(2 * (b % 3) + 1), sm8[:, 5, b:b + 1], silu_buf[:, b % 2, :], ALU.mult, ALU.mult)
                ins.then_inc(s("h_done"), 1)
                dve.wait_ge(s("h_done"), b + 1)
                link(V_.tensor_reduce(sc[:, 0:1], h, AX_X, ALU.max, apply_absolute_value=True))
                link(ts(sc[:, 1:2], sc[:, 0:1], 1e-5, None, ALU.max))
                link(V_.reciprocal(sc[:, 2:3], sc[:, 1:2]))
                link(ts(sc[:, 3:4], sc[:, 2:3], 127.0, None, ALU.mult))
                link(ts(h, h, sc[:, 3:4], MAGIC, ALU.mult, ALU.add))
                ts(h, h, MAGIC + 127.0, MAGIC - 128.0, ALU.min, ALU.max).then_inc(s("h_round"), 1)
                link(ts(sm8[:, 6, b:b + 1], sc[:, 1:2], 1.0 / 127.0, wscl[:, 2:3], ALU.mult, ALU.mult))

            def add_down(b):
                dve.wait_ge(s("pe_down"), b + 1)
                stt(res[:, b, :], bank(7)[:, 0:P], sm8[:, 6, b:b + 1], xt[:, b, :], ALU.mult, ALU.add)\
                    .then_inc(s("res_f1"), 1)

            for b in range(NB + 1):
                if b < NB:
                    hidden(b)
                if b:
                    add_down(b - 1)
            layer_norm((s("res_f1"), NB))


def kernel(**inputs):
    import numpy as np
    import concourse.bacc as bacc
    from concourse.bass_utils import run_bass_kernel_spmd

    f = {k: np.asarray(v) for k, v in inputs.items()}
    c = np.ascontiguousarray

    def by_group(w):
        return c(w.reshape(2, G, DH0, P).transpose(3, 1, 0, 2).reshape(P, 1024))

    swap = np.arange(P) ^ 1
    f32 = np.float32
    base = (np.arange(0, P, 2, dtype=f32) + f32(0.4 * P)) / f32(1.4 * P)
    pos = np.arange(P, dtype=f32)
    scale = base[None, :] ** (pos / f32(512.0))[:, None]
    freqs = f32(1.0) / f32(10000.0) ** (np.arange(P // 2, dtype=f32) / f32(P // 2))
    angle = pos[:, None] * freqs[None, :]
    sign = np.where(np.arange(P) % 2 == 0, -1.0, 1.0).astype(f32)

    def twice(t):
        return np.repeat(t, 2, axis=1).T.astype(f32)
    rot = np.stack([twice(np.cos(angle) * scale), twice(np.sin(angle) * scale) * sign[:, None],
                    twice(np.cos(angle) * (f32(1.0) / scale)),
                    twice(np.sin(angle) * (f32(1.0) / scale)) * sign[:, None]], axis=1)
    ahead = pos[None, :] - pos[:, None]
    decay = np.where(ahead >= 0, f32(0.96875) ** np.maximum(ahead, 0), 0).astype(f32)

    wa, ba = f["L1_attn_W_attn"], f["L1_attn_b_attn"]
    arrays = {
        "x_tok": c(f["x"].transpose(1, 0, 2)), "x_T": c(f["x"].transpose(2, 0, 1).reshape(P, NTOK)),
        "ctx_T": c(f["ctx_1024"].transpose(2, 0, 1).reshape(P, NTOK)),
        "wq0": by_group(f["L0_attn_wq"]), "wk0": by_group(f["L0_attn_wk"]), "wv0": by_group(f["L0_attn_wv"]),
        "wo0": c(f["L0_attn_wo"].reshape(P, 2, G, DH0).transpose(1, 3, 2, 0).reshape(P, G, P)),
        "xwq0": c(f["L0_xattn_Wq"].T), "xbq0": f["L0_xattn_bq"].reshape(P, 1),
        "xwk0": c(f["L0_xattn_Wk"].T), "xbk0": f["L0_xattn_bk"].reshape(P, 1),
        "xwv0": c(f["L0_xattn_Wv"].T), "xbv0": f["L0_xattn_bv"].reshape(1, P),
        "wge": c(np.concatenate([f["L0_ffn_We"], f["L0_ffn_Wg"]], axis=1)),
        "bge": np.concatenate([f["L0_ffn_be"], f["L0_ffn_bg"]]).reshape(1, P + NE),
        "wqk1": c(wa[:, 0:2 * P].reshape(P, 2, P)), "bqk1": c(ba[0:2 * P].reshape(2, P).T),
        "wv1": c(wa[:, 2 * P:3 * P]), "bv1": c(ba[2 * P:3 * P].reshape(1, P)),
        "wp1": f["L1_attn_W_proj"], "bp1": f["L1_attn_b_proj"].reshape(1, P),
        "xwq1": f["L1_xattn_Wq"], "xwq1s": c(f["L1_xattn_Wq"][:, swap]),
        "xwk1": f["L1_xattn_Wk"], "xwk1s": c(f["L1_xattn_Wk"][:, swap]), "xwv1": f["L1_xattn_Wv"],
        "wgu": c(np.concatenate([f["L1_ffn_w_gate"].T, f["L1_ffn_w_up"].T], axis=1)),
        "wdn": c(f["L1_ffn_w_down"].T.reshape(4, P, P).transpose(1, 0, 2).reshape(P, INNER)),
        "rot": c(rot), "decay": decay,
    }
    nc = bacc.Bacc("TRN2", target_bir_lowering=False, num_devices=1)
    args = [nc.dram_tensor(n, a.shape, mybir.dt.from_np(a.dtype), kind="ExternalInput").ap()
            for n, a in arrays.items()]
    result = nc.dram_tensor("out", (NB, P, P), F32, kind="ExternalOutput").ap()
    decoder(nc, *args, result)
    done = run_bass_kernel_spmd(nc, [arrays], core_ids=[0])
    return done.results[0]["out"]
```

```python
from contextlib import ExitStack

import concourse.bass as bass
from concourse import mybir

ALU = mybir.AluOpType
ACT = mybir.ActivationFunctionType
F32 = mybir.dt.float32
F32R = mybir.dt.float32r
F16 = mybir.dt.float16
BF16 = mybir.dt.bfloat16
I32 = mybir.dt.int32
AX_X = mybir.AxisListType.X

P = 128
NB = 8
NTOK = NB * P
H = 16
DH0 = 64
G = 8
DH1 = 8
INNER = 512
NE = 8
NPAIR = NB // 2
TP = 2 * P
HP = 2 * H
QP = HP // 4
VW = 96
NPROJ = 12
SLOTS_PT = 3
NH = NB // 2
HT = NH * P
NQ = NPAIR * QP
AHEAD = 5
TICKS0 = NQ + 3
T1 = NQ
MID1 = TICKS0 - T1
GAP = 10
SCALE0 = DH0 ** -0.5
SCALE1 = DH1 ** -0.5
SCALEX = P ** -0.5
EPS = 1e-5
MAGIC = 1.5 * 2.0 ** 23
RSQRT_BITS = 0x5F3759DF
MASKED = -1e30
NW = INNER * P


def decoder(nc, x_tok, x_T, ctx_T, wq0, wk0, wv0, wo0, xwq0, xbq0, xwk0, xbk0, xwv0, xbv0,
            wge, bge, wqk1, bqk1, wv1, bv1, wp1, bp1, xwq1, xwq1s, xwk1, xwk1s, xwv1,
            wgu, wdn, rot, decay, out):
    k_piece = nc.dram_tensor("k_piece", [2, P, NTOK], F16, kind="Internal").ap()
    q_piece = nc.dram_tensor("q_piece", [2, P, NTOK], F16, kind="Internal").ap()

    with ExitStack() as ctx:
        def sb(name, shape, dt=F32):
            return ctx.enter_context(nc.sbuf_tensor(name, shape, dt))

        def sem(name):
            return ctx.enter_context(nc.semaphore(name))

        PS = ctx.enter_context(nc.psum_tensor("PS", [P, 8, 512], F32))
        xt = sb("xt", [P, NB, P])
        xT = sb("xT", [P, NTOK])
        cT = sb("cT", [P, NTOK])
        w0 = sb("w0", [P, 3, 1024])
        w0h = sb("w0h", [P, 3, 1024], F32R)
        w0l = sb("w0l", [P, 3, 1024], F32R)
        wo = sb("wo", [P, G, P])
        xh = sb("xh", [P, NTOK], F32R)
        xl = sb("xl", [P, NTOK], F32R)
        arena = sb("arena", [P, 32768], F16)
        VN = sb("VN", [P, 2048])
        V = sb("V", [P, 2, HP, VW])
        PT = sb("PT", [P, SLOTS_PT, 512])
        On = sb("On", [P, HP, DH0])
        OT = sb("OT", [P, 2, G, P])
        En = sb("En", [P, H, P], F16)
        rowmax = sb("rowmax", [P, P])
        MR = sb("MR", [P, 2, P], F16)
        ident = sb("ident", [P, P])
        ident_b = sb("ident_b", [P, P], BF16)
        maskq = sb("maskq", [P, P], BF16)
        maskk = sb("maskk", [P, P], BF16)
        res = sb("res", [P, NB, P])
        stats = sb("stats", [P, NB, 6])
        mv = sb("mv", [P, NB, 2])
        rstd = sb("rstd", [P, NB])
        shift = sb("shift", [P, NB])
        nwt = sb("nwt", [P, 3, NB])
        rec = sb("rec", [P, 2, H])
        wx0 = sb("wx0", [P, 3, P])
        bx0 = sb("bx0", [P, 2])
        bvx0 = sb("bvx0", [P, P])
        wge_s = sb("wge_s", [P, P + NE])
        bge_s = sb("bge_s", [P, P + NE])
        w1 = sb("w1", [P, 3, P])
        b1 = sb("b1", [P, 2])
        bv1_s = sb("bv1_s", [P, P])
        wp1_s = sb("wp1_s", [P, P])
        bp1_s = sb("bp1_s", [P, P])
        wx1 = sb("wx1", [P, 5, P])
        rot_s = sb("rot_s", [P, 4, P])
        decay_s = sb("decay_s", [P, P])
        wgu_s = sb("wgu_s", [P, 2 * INNER])
        wdn_s = sb("wdn_s", [P, INNER])
        wabs = sb("wabs", [P, 4])
        wscl = sb("wscl", [P, 8])
        ones = sb("ones", [P, P])
        hs = sb("hs", [P, 2, 4])
        sm8 = sb("sm8", [P, 8, NB])
        lgt = sb("lgt", [P, NB, NE])

        def part(i, n=4096):
            return arena[:, i * n:(i + 1) * n]

        def flat(x):
            return x.rearrange("p a b -> p (a b)")
        QA = [part(0), part(3)]
        QB = [part(1), part(4)]
        KA = [part(2), part(5)]

        w0f, Vf, af = flat(w0[:]), V[:].rearrange("p a n c -> p (a n c)"), arena[:].bitcast(F32)
        ab = arena[:].bitcast(BF16)
        tB = w0f[:, 0:NTOK]
        mA, mC, kx0, vx0 = (w0f[:, NTOK + i * HT:NTOK + (i + 1) * HT] for i in range(4))
        Kst = [arena[:, 24576:32768], arena[:, 12288:20480]]
        Qst = [arena[:, 0:8192], Vf[:, 0:4096].bitcast(F16)]
        Kst, Qst = ([x.rearrange("p (n t) -> p n t", n=H) for x in st] for st in (Kst, Qst))
        VE = [af[:, 4096:6144], af[:, 10240:12288]]
        o1 = Vf[:, 4096:5120].rearrange("p (i c) -> p i c", i=2)
        On1, OnT1 = Vf[:, 5120:5120 + P], Vf[:, 5120 + P:5120 + 2 * P]
        VNh = VN[:].bitcast(F16)
        kph, kpl, qph, qpl = (VNh[:, i * NTOK:(i + 1) * NTOK] for i in range(4))
        lA, lC, lD, lE, kx1, vx1 = (af[:, i * HT:(i + 1) * HT] for i in range(6))
        hb = af[:, 12288:13312].rearrange("p (i c) -> p i c", i=2)
        th = af[:, 13312:14336].rearrange("p (i c) -> p i c", i=2)
        x5r = af[:, 14336:14848]
        x5q, x5T = ab[:, 29696:30208], ab[:, 30208:30720]
        hi, hT = (ab[:, 30720 + i * 1024:31744 + i * 1024].rearrange("p (i c) -> p i c", i=2) for i in range(2))
        wob = flat(wo[:]).bitcast(BF16)
        wgu_i, wdn_i = wob[:, 0:2 * INNER], wob[:, 2 * INNER:3 * INNER]

        def head(buf, n):
            return buf[:, n * P:(n + 1) * P]

        def by_column(buf, i):
            v = buf.rearrange("p (n a g t) -> p a g n t", a=2, g=G, t=8)
            return v[:, :, 2 * (i % 4):2 * (i % 4) + 2, :, :]

        def bank(i):
            return PS[:, i, :]

        named = {}

        def s(name):
            if name not in named:
                named[name] = sem(name)
            return named[name]

        qk_in = [sem("qk_in0"), sem("qk_in1")]
        pj_free = [sem("pj_free0"), sem("pj_free1")]
        s1_free = [sem(f"s1_free{i}") for i in range(3)]

        block = ctx.enter_context(nc.Block())

        PJ = ((0, 1, 2), (3, 4, 5), (6, 7), (8, 9), (10, 11), (12, 13), (14, 15, 16), (17, 18, 19))

        def next_projection(t, k):
            banks = PJ[t % QP]
            return ((t // QP + 1, banks[k]),) if t < NQ - QP and k < len(banks) else ()

        def quad_bank(Q):
            return 3 if Q in (1, 3) else 2

        def z_max(b):
            return 4 * b - 3 if b else 0

        def z_out(o):
            return 4 * (o // 2) + 2 + o % 2 - (o // 2 == NB - 1)

        def z_y(b):
            return 4 * b + 4 - (b == NB - 1)

        def u1(b):
            return 4 * b + (GAP if b >= NH else 0)
        LATE0 = max(u1(NH - 1) + 11, MID1 + 22)
        LATE1 = max(u1(NB - 1) + 11, LATE0 + 24)
        TICKS1 = LATE1 + 24
        q_use, k_use = {}, {}
        for u in range(TICKS1):
            for uses, at in ((q_use, 0), (k_use, 4)):
                for b in range(NB):
                    if 0 <= u - at - u1(b) < 4:
                        uses[b, u - at - u1(b)] = len(q_use) + len(k_use)

        def v_there(p, q):
            return (pj_free[q % 2], 10 * (p - 1) + (NPROJ + q) // 2 + 1) if p else (s("v_in"), q + 1)

        MID0 = (0, None, None, 2, 3, 4, 5, 6, 7, 8, 9, None, None, 11, 12, 13, 14, 15, None, None,
                17, 18, 19, 20, 21)

        def mid0(t, k):
            i = 2 * t + k - 2 * (4 * (NH - 1) + 6) - 1
            return MID0[i] if 0 <= i < len(MID0) else None

        @block.sync
        def _(sp):
            sp.dma_start(xT[:], x_T).then_inc(s("ld_x"), 16)
            for name, i, w in (("ld_wk", 0, wk0), ("ld_wq", 1, wq0), ("ld_wv", 2, wv0)):
                for j in range(2):
                    cols = slice(j * 512, (j + 1) * 512)
                    sp.dma_start(w0[:, i, cols], w[:, cols]).then_inc(s(name + str(j)), 16)
            sp.dma_start(wo[:], wo0).then_inc(s("ld_wo"), 16)
            sp.dma_start(xt[:], x_tok).then_inc(s("ld_wo"), 16)
            sp.dma_start(cT[:], ctx_T).then_inc(s("ld_ctx"), 16)
            for dst, src in ((wx0[:, 0, :], xwq0), (wx0[:, 1, :], xwk0), (wx0[:, 2, :], xwv0),
                             (bx0[:, 0:1], xbq0), (bx0[:, 1:2], xbk0),
                             (wx1[:, 0, :], xwq1), (wx1[:, 1, :], xwq1s), (wx1[:, 2, :], xwk1),
                             (wx1[:, 3, :], xwk1s), (wx1[:, 4, :], xwv1),
                             (rot_s[:], rot)):
                sp.dma_start(dst, src).then_inc(s("ld_ctx"), 16)
            sp.dma_start(wgu_s[:], wgu).then_inc(s("ld_late"), 16)
            sp.dma_start(wdn_s[:], wdn).then_inc(s("ld_late"), 16)
            for dst, src in ((bvx0[:], xbv0.partition_broadcast(P)), (wge_s[:], wge),
                             (bge_s[:], bge.partition_broadcast(P)),
                             (w1[:, 0:2, :], wqk1), (w1[:, 2, :], wv1), (b1[:], bqk1),
                             (bv1_s[:], bv1.partition_broadcast(P)), (wp1_s[:], wp1),
                             (bp1_s[:], bp1.partition_broadcast(P)), (decay_s[:], decay)):
                sp.dma_start(dst, src).then_inc(s("ld_mid"), 16)

            for p in range(NPAIR):
                b = p % 2
                lower = (pj_free[1], 10 * (p - 1) + 4) if p else (s("qk_lo"), 8)
                for (split, count), dst in (((s("qk_hi"), 8 * p + 8), QA), (lower, QB)):
                    sp.wait_ge(split, count)
                    sp.dma_start(dst[b][64:P, :], dst[b][0:64, :]).then_inc(qk_in[b], 16)

            for h in range(2):
                cols = slice(h * HT, (h + 1) * HT)
                sp.wait_ge(s(f"stack_zero{h}"), 1)
                for x, hi_, lo_, piece, stack, order in (("k", kph, kpl, k_piece, Kst[h], (0, 0, 1, 1)),
                                                         ("q", qph, qpl, q_piece, Qst[h], (0, 1, 0, 1))):
                    for i, src in enumerate((hi_, lo_)):
                        sp.wait_ge(s(f"{x}p_{('hi', 'lo')[i]}{h}"), 1)
                        sp.dma_start(piece[i][:, cols], src[:, cols]).then_inc(s(f"{x}_out{h}"), 16)
                    sp.wait_ge(s(f"{x}_out{h}"), 32)
                    for row, i in enumerate(order):
                        sp.dma_start(stack[8 * row:8 * row + 8, :, :],
                                     piece[i].rearrange("(n d) t -> d n t", d=DH1)[:, :, cols])\
                            .then_inc(s(f"stack_in{h}"), 16)
            for b in range(NB):
                sp.wait_ge(s(f"xn{b // NH}"), 5 * NH + b % NH + 1)
                sp.dma_start(out[b], xt[:, b, :]).then_inc(s("out_sem"), 16)
            sp.wait_ge(s("out_sem"), 16 * NB)

        def tok(x):
            return x.rearrange("p (b d) -> p b d", b=NH)

        def half(x, h):
            return x[:, h * HT:(h + 1) * HT]

        def of_half(x, h):
            return x[:, NH * h:NH * h + NH]

        @block.gpsimd
        def _(pool):
            step = [0]
            ts, tt = nc.gpsimd.tensor_scalar, nc.gpsimd.tensor_tensor

            def link(ins):
                step[0] += 1
                ins.then_inc(s("pool_step"), 1)
                pool.wait_ge(s("pool_step"), step[0])

            pool.memset(ident[:], 0.0)
            link(pool.memset(ident_b[:], 0.0))
            for m in (ident, ident_b):
                m = pool.affine_select(out=m[:], in_=m[:], compare_op=ALU.not_equal, fill=1.0,
                                       base=0, pattern=[[-1, P]], channel_multiplier=1)
            m.then_inc(s("ident_set"), 1)
            link(pool.memset(V[:, :, :, DH0:VW], 0.0))
            pool.memset(V[:, :, :, DH0:DH0 + 1], 1.0).then_inc(s("v_ones"), 1)
            pool.memset(En[:], 0.0)
            link(pool.memset(MR[:], 0.0))
            link(pool.affine_select(out=En[:], in_=En[:], compare_op=ALU.not_equal, fill=1.0,
                                    base=0, pattern=[[-1, H], [0, P]], channel_multiplier=1))
            pool.affine_select(out=En[:], in_=En[:], compare_op=ALU.not_equal, fill=1.0,
                               base=-32, pattern=[[-1, H], [0, P]], channel_multiplier=1)\
                .then_inc(s("setup"), 1)
            pool.memset(maskq[:], 0.0)
            pool.memset(maskk[:], 0.0)
            link(pool.memset(ones[:], 1.0))
            pool.affine_select(out=maskq[:], in_=maskq[:], compare_op=ALU.is_ge, fill=MASKED,
                               base=0, pattern=[[-1, P]], channel_multiplier=1)
            pool.affine_select(out=maskk[:], in_=maskk[:], compare_op=ALU.is_ge, fill=MASKED,
                               base=0, pattern=[[1, P]], channel_multiplier=-1)\
                .then_inc(s("masks"), 1)
            pool.memset(af[:, 12288:16384], 0.0)

            def rsqrt(h, k):
                if h:
                    return
                v, y, e = (nwt[:, i, NH * h:NH * h + NH] for i in range(3))
                r = of_half(rstd, h)
                pool.wait_ge(s(f"moments{h}"), k + 1)
                ts(of_half(shift, h), of_half(mv, h)[:, :, 0], -1.0, None, ALU.mult)
                link(ts(v, of_half(mv, h)[:, :, 1], EPS, 0.5, ALU.add, ALU.mult))
                link(ts(y.bitcast(I32), v.bitcast(I32), -0.5, RSQRT_BITS - 2 ** 22, ALU.mult, ALU.add))
                for i in range(3):
                    link(tt(e, y, y, ALU.mult))
                    link(tt(e, e, v, ALU.mult))
                    link(ts(e, e, -1.0, 1.5, ALU.mult, ALU.add))
                    link(tt(r if i == 2 else y, y, e, ALU.mult))
                tt(of_half(shift, h), of_half(shift, h), r, ALU.mult)\
                    .then_inc(s(f"rstd{h}"), 1)

            def add_bias(h, k, bias, event):
                pool.wait_ge(s(f"xn{h}"), NH * (k + 1))
                tt(tok(half(tB, h)), of_half(xt, h), bias.unsqueeze(1).broadcast_to([P, NH, P]), ALU.add)\
                    .then_inc(s(event), 1)

            def ternary(n):
                src, dst = ((wgu_s[:, 0:INNER], wgu_i[:, 0:INNER]),
                            (wgu_s[:, INNER:2 * INNER], wgu_i[:, INNER:2 * INNER]), (wdn_s[:], wdn_i[:]))[n]
                link(ts(src, src, wscl[:, 4 + n:5 + n], MAGIC, ALU.mult, ALU.add))
                link(ts(src, src, MAGIC + 1.0, MAGIC - 1.0, ALU.min, ALU.max))
                ts(dst, src, MAGIC, None, ALU.subtract).then_inc(s("w_int"), 1)

            def zero(h):
                if h == 0:
                    pool.wait_ge(s("sk_done"), QP * (NPAIR - 1))
                    pool.memset(af[:, 0:4096], 0.0).then_inc(s("stack_zero0"), 1)
                else:
                    pool.wait_ge(s("pv_done"), NQ)
                    pool.memset(af[:, 6144:10240], 0.0)
                    pool.memset(Vf[:, 0:4096], 0.0).then_inc(s("stack_zero1"), 1)
                link(pool.memset(VE[h], 0.0))
                pool.memset(VE[h].rearrange("p (x c) -> p x c", c=32)[:, :, DH1:DH1 + 1], 1.0)\
                    .then_inc(s(f"ve_ones{h}"), 1)

            def mid(h, i):
                if i == 0:
                    rsqrt(h, 0)
                if i == 2:
                    if h == 0:
                        pool.wait_ge(s("ld_mid"), 160)
                    add_bias(h, 0, bvx0[:], f"x1b{h}")
                if i == 3 + 9 * (1 - h):
                    zero(h)
                if i == 4 and h:
                    pool.wait_ge(s("w_scale"), 1)
                    pool.wait_ge(s("turn_done"), 8 * NPAIR)
                    ternary(0)
                if i == 9:
                    rsqrt(h, 1)
                if i == 12 and h:
                    ternary(1)
                if i == 15:
                    rsqrt(h, 2)
                if i == 18:
                    add_bias(h, 2, bp1_s[:], f"x3b{h}")
                if i == 19 and h:
                    ternary(2)

            def late(h, i):
                if i == 0:
                    rsqrt(h, 3)
                    pool.wait_ge(s("k1_mul"), h + 1)
                    tt(kx1, lD, lC, ALU.add).then_inc(s("k1_rot"), 1)
                if i == 4:
                    pool.wait_ge(s("q_mul"), h + 1)
                    tt(lA, lA, lE, ALU.add).then_inc(s("q_rot"), 1)
                if i == 7:
                    rsqrt(h, 4)
                if i == 21:
                    rsqrt(h, 5)

            for t in range(TICKS0):
                for k in range(2):
                    mid(0, mid0(t, k))
            for u in range(MID1, TICKS1):
                mid(1, u - MID1)
                late(0, u - LATE0)
                late(1, u - LATE1)

        @block.tensor
        def _(pe):
            mm, turn = nc.tensor.matmul, nc.tensor.transpose

            def tiles(dst, lhsT, rhs, shared=False):
                for b in range(NH):
                    c = slice(b * P, (b + 1) * P)
                    m = mm(dst[:, c], lhsT[:, c], rhs if shared else rhs[:, c], start=True, stop=True)
                return m

            def project(p, i):
                w, slot = i // 4, i % 2
                at = i % 8 if p == 0 else slot
                if p == 0:
                    pe.wait_ge(s("hi"), 2 + i // 2)
                    pe.wait_ge(s("lo"), 2 + i // 2)
                    if i >= 8:
                        pe.wait_ge(s("qk_lo"), i - 7)
                elif p > 1 or i >= 2:
                    pe.wait_ge(pj_free[slot], 10 * (p - 1) + i // 2)
                for gi in range(2):
                    g = slice((2 * (i % 4) + gi) * P, (2 * (i % 4) + gi + 1) * P)
                    dst = bank(at)[:, gi * TP:(gi + 1) * TP]
                    x = slice(p * TP, (p + 1) * TP)
                    mm(dst, w0l[:, w, g], xh[:, x], start=True, stop=False)
                    mm(dst, w0h[:, w, g], xl[:, x], start=False, stop=False)
                    m = mm(dst, w0h[:, w, g], xh[:, x], start=False, stop=True)
                m.then_inc(s("proj_done"), 1)

            def turn_v(p, q):
                i = NPROJ + q
                at = 4 + q % 4 if p == 0 else i % 2
                if p:
                    pe.wait_ge(pj_free[i % 2], 10 * (p - 1) + i // 2)
                elif q < 4:
                    pe.wait_ge(s("qk_lo"), 5 + q)
                else:
                    pe.wait_ge(s("v_in"), q - 3)
                if q == 0:
                    pe.wait_ge(*((pj_free[1], 10 * (p - 1) + 6) if p else (s("vn_in"), 4)))
                for h in range(4):
                    m = turn(bank(at)[0:64, h * P:(h + 1) * P],
                             VN[:, (4 * q + h) * 64:(4 * q + h + 1) * 64], ident[:])
                m.then_inc(s("proj_done"), 1)

            def scores_q(Q):
                p, q = Q // QP, Q % QP
                if q == 0:
                    pe.wait_ge(qk_in[p % 2], 32 * (p // 2 + 1))
                if Q >= 2:
                    pe.wait_ge(s("max_done"), Q if Q > AHEAD - 1 else Q - 1)
                for h in range(4):
                    n, dst = 4 * q + h, bank(quad_bank(Q))[:, h * P:(h + 1) * P]
                    mm(dst, head(QB[p % 2], n), head(KA[p % 2], n), start=True, stop=False)
                    m = mm(dst, head(QA[p % 2], n), head(KA[p % 2], n), start=False, stop=True)
                m.then_inc(s("sq_done"), 1)

            def scores_k(Q):
                p, q, b = Q // QP, Q % QP, Q // 4
                if Q:
                    pe.wait_ge(s("exp_done"), Q)
                else:
                    pe.wait_ge(s("max_done"), 4)
                pe.wait_ge(s("turn_free"), z_max(b) + 1)
                for h in range(4):
                    n, dst = 4 * q + h, bank(3)[:, h * P:(h + 1) * P]
                    mm(dst, head(KA[p % 2], n), head(QB[p % 2], n), start=True, stop=False)
                    mm(dst, head(KA[p % 2], n), head(QA[p % 2], n), start=False, stop=False)
                    m = mm(dst, En[:, n % H, :], MR[:, b % 2, :], start=False, stop=True)
                m.then_inc(s("sk_done"), 1)

            def weigh(Q):
                p, q = Q // QP, Q % QP
                pe.wait_ge(s("exp_done"), Q + 1)
                pe.wait_ge(*v_there(p, q))
                if Q:
                    pe.wait_ge(s("norm_done"), Q)
                for h in range(4):
                    m = mm(bank(4)[:, h * VW:(h + 1) * VW], PT[:, Q % SLOTS_PT, h * P:(h + 1) * P],
                           V[:, p % 2, 4 * q + h, :], start=True, stop=True)
                m.then_inc(s("pv_done"), 1)

            def turn_max(b):
                z = z_max(b)
                if z:
                    pe.wait_ge(s("turn_free"), z)
                else:
                    pe.wait_ge(s("v_in"), 8)
                pe.wait_ge(s("max_done"), 4 * b + 4)
                turn(bank(5)[0:H, 0:P], rowmax[:, b * H:(b + 1) * H], ident[:]).then_inc(s("turn_done"), 1)

            def turn_out(o):
                pe.wait_ge(s("turn_free"), z_out(o))
                pe.wait_ge(s("norm_done"), 2 * o + 2)
                for r in range(4):
                    n = 8 * (o % 4) + 2 * r
                    m = turn(bank(5)[:, r * P:(r + 1) * P], On[:, n:n + 2, :], ident[:])
                m.then_inc(s("turn_done"), 1)

            def project_out(b):
                pe.wait_ge(s("turn_free"), z_y(b))
                if b == 0:
                    pe.wait_ge(s("ld_wo"), 32)
                for g in range(G):
                    m = mm(bank(5)[:, 0:P], OT[:, b % 2, g, :], wo[:, g, :], start=(g == 0), stop=(g == G - 1))
                m.then_inc(s("turn_done"), 1)

            def project_next(t, k):
                for p, i in next_projection(t, k):
                    if i < NPROJ:
                        project(p, i)
                    else:
                        turn_v(p, i - NPROJ)

            def turn_x(h, k, at):
                for b in range(NH):
                    pe.wait_ge(s(f"xn{h}"), NH * k + b + 1)
                    m = turn(bank(at)[:, b * P:(b + 1) * P], xt[:, NH * h + b, :], ident[:])
                m.then_inc(s(f"pe_x{h}"), 1)
                return

            def mid(h, i):
                if i == 0:
                    if h == 0:
                        pe.wait_ge(s("ld_ctx"), 16 * 12)
                    mm(bank(6), wx0[:, 1, :], half(cT, h), start=True, stop=True).then_inc(s("pe_kx0"), 1)
                    tiles(bank(7), half(cT, h), wx0[:, 2, :], True).then_inc(s("pe_vx0"), 1)
                if i == 3:
                    pe.wait_ge(s("kx0"), h + 1)
                    turn_x(h, 0, 6)
                if i == 4:
                    pe.wait_ge(s("vx0"), h + 1)
                    pe.wait_ge(s(f"xT{h}"), 1)
                    mm(bank(7), wx0[:, 0, :], half(xT, h), start=True, stop=True).then_inc(s("pe_q0"), 1)
                if i == 5:
                    pe.wait_ge(s("q0"), h + 1)
                    tiles(bank(6), mA, kx0).then_inc(s("pe_s0"), 1)
                if i == 7:
                    pe.wait_ge(s("exp0"), h + 1)
                    for b in range(NH):
                        m = turn(bank(7)[:, b * P:(b + 1) * P], mC[:, b * P:(b + 1) * P], ident[:])
                    m.then_inc(s("pe_p0"), 1)
                if i == 8:
                    pe.wait_ge(s("p0T"), h + 1)
                    tiles(bank(6), mA, vx0).then_inc(s("pe_o0"), 1)
                if i == 12:
                    turn_x(h, 1, 7)
                if i == 13:
                    pe.wait_ge(s(f"xT{h}"), 2)
                    if h == 0:
                        pe.wait_ge(s("ld_mid"), 160)
                    for b in range(NH):
                        m = mm(bank(6 + b // 2)[:, (b % 2) * 256:(b % 2) * 256 + P + NE],
                               half(xT, h)[:, b * P:(b + 1) * P], wge_s[:], start=True, stop=True)
                    m.then_inc(s("pe_ffn"), 1)
                if i == 18:
                    turn_x(h, 2, 6)
                if i == 19:
                    pe.wait_ge(s(f"xT{h}"), 3)
                    mm(bank(7), w1[:, 1, :], half(xT, h), start=True, stop=True).then_inc(s("pe_k1a"), 1)
                if i == 20:
                    mm(bank(6), w1[:, 0, :], half(xT, h), start=True, stop=True).then_inc(s("pe_q1a"), 1)
                if i == 21:
                    pe.wait_ge(s(f"kp_lo{h}"), 1)
                    tiles(bank(7), half(xT, h), w1[:, 2, :], True).then_inc(s("pe_v1a"), 1)
                    if h == 0:
                        pe.wait_ge(s("qp_lo0"), 1)
                        pe.wait_ge(s("ve_done0"), 1)

            def scores1(w, b, q, of_keys):
                if w >= 3:
                    pe.wait_ge(s1_free[w % 3], w // 3)
                else:
                    pe.wait_ge(s("max_done"), NQ)
                pe.wait_ge(s(f"stack_in{b // NH}"), 128)
                if of_keys:
                    pe.wait_ge(s("mr1_done"), b + 1)
                t = slice((b % NH) * P, (b % NH + 1) * P)
                K, Q, dst = Kst[b // NH], Qst[b // NH], bank(w % 3)
                mm(dst, ident_b[:], (maskk if of_keys else maskq)[:].unsqueeze(1).broadcast_to([P, 4, P]),
                   start=True, stop=False)
                for h in range(4):
                    n, part_ = 4 * q + h, dst[:, h * P:(h + 1) * P]
                    if of_keys:
                        mm(part_, K[:, n, t], Q[:, n, t], start=False, stop=False)
                        m = mm(part_, En[:, n, :], MR[:, b % 2, :], start=False, stop=(h == 3))
                    else:
                        m = mm(part_, Q[:, n, t], K[:, n, t], start=False, stop=(h == 3))
                m.then_inc(s("scores1_done"), 1)

            def weigh1(b, q):
                v, w = 4 * b + q, k_use[b, q]
                pe.wait_ge(s1_free[w % 3], w // 3 + 1)
                if q == 0:
                    pe.wait_ge(s(f"ve_done{b // NH}"), 1)
                    if b:
                        pe.wait_ge(s("o1_out"), b)
                for r in range(4):
                    n = (b % NH) * H + 4 * q + r
                    m = mm(bank(3)[32 * r:32 * r + 32, q * P:(q + 1) * P], VE[b // NH][:, 32 * n:32 * n + 32],
                           PT[:, v % SLOTS_PT, r * P:(r + 1) * P], start=True, stop=True)
                m.then_inc(s("pv1_done"), 1)

            def main1(u):
                for b in range(NB):
                    if 0 <= u - u1(b) < 4:
                        scores1(q_use[b, u - u1(b)], b, u - u1(b), False)
                for b in range(NB):
                    if 4 <= u - u1(b) < 8:
                        q = u - u1(b) - 4
                        scores1(k_use[b, q], b, q, True)
                        if q:
                            weigh1(b, q - 1)
                for b in range(NB):
                    step_out = u - u1(b) - 8
                    if step_out == 0:
                        pe.wait_ge(s("o1_out"), b + 1)
                        last = [c for c in range(NB) if u1(c) + 3 < u][-1]
                        pe.wait_ge(s("mr1_done"), last + 1)
                        if b:
                            pe.wait_ge(s("res1_done"), b)
                        for q in range(4):
                            m = turn(bank(4)[:, q * P:(q + 1) * P], o1[:, b % 2, q * P:(q + 1) * P], ident[:])
                        m.then_inc(s("pe_ot1"), 1)
                    if step_out == 1:
                        pe.wait_ge(s("on1_done"), b + 1)
                        turn(bank(4)[:, 0:P], On1, ident[:]).then_inc(s("pe_on1"), 1)
                    if step_out == 2:
                        pe.wait_ge(s("onT1_done"), b + 1)
                        mm(bank(4)[:, P:2 * P], OnT1, wp1_s[:], start=True, stop=True).then_inc(s("pe_y1"), 1)
                for b in range(NB):
                    if u - u1(b) == 3:
                        w = q_use[b, 3]
                        pe.wait_ge(s1_free[w % 3], w // 3 + 1)
                        outs = len([c for c in range(NB) if u1(c) + 10 <= u])
                        if outs:
                            pe.wait_ge(s("res1_done"), outs)
                        if b:
                            pe.wait_ge(s("mr1_done"), b)
                        turn(bank(4)[0:H, 0:P], rowmax[:, b * H:(b + 1) * H], ident[:])\
                            .then_inc(s("pe_mt1"), 1)
                    if u - u1(b) == 7:
                        weigh1(b, 3)

            def gate_bank(b):
                return 6 if b < NH else (6, 0, 2, 6)[b - NH]

            def late(h, i):
                if i == 0:
                    if h == 0:
                        pe.wait_ge(s("turn_free"), 8 * NPAIR)
                        pe.wait_ge(s("qp_lo1"), 1)
                        pe.wait_ge(s("ve_done1"), 1)
                    else:
                        pe.wait_ge(s("res_f1"), NH)
                    mm(bank(6), wx1[:, 2, :], half(cT, h), start=True, stop=True)
                    mm(bank(7), wx1[:, 3, :], half(cT, h), start=True, stop=True).then_inc(s("pe_k1"), 1)
                    tiles(bank(5), half(cT, h), wx1[:, 4, :], True).then_inc(s("pe_vx1"), 1)
                if i == 3:
                    pe.wait_ge(s("vx1"), h + 1)
                    turn_x(h, 3, 5)
                if i == 4:
                    pe.wait_ge(s("k1_mul"), h + 1)
                    pe.wait_ge(s(f"xT{h}"), 4)
                    mm(bank(6), wx1[:, 0, :], half(xT, h), start=True, stop=True)
                    mm(bank(7), wx1[:, 1, :], half(xT, h), start=True, stop=True).then_inc(s("pe_q"), 1)
                if i == 6:
                    pe.wait_ge(s("k1_rot"), h + 1)
                    pe.wait_ge(s("q_rot"), h + 1)
                    tiles(bank(5), kx1, lA).then_inc(s("pe_sx1"), 1)
                if i == 7:
                    pe.wait_ge(s("sx1"), h + 1)
                    tiles(bank(6), lD, vx1).then_inc(s("pe_ox1"), 1)
                if i == 11:
                    pe.wait_ge(s("x5q"), h + 1)
                    for b in range(NH):
                        c = slice(b * P, (b + 1) * P)
                        m = turn(bank(5).bitcast(BF16)[:, c], x5q[:, c], ident_b[:])
                    m.then_inc(s("pe_x5T"), 1)
                if 12 <= i <= 20 and i % 2 == 0:
                    j = i // 2 - 6
                    if j == 0:
                        pe.wait_ge(s("x5T"), h + 1)
                        pe.wait_ge(s("w_int"), 3)
                    if j < NH:
                        b = NH * h + j
                        before = [c for c in range(b) if gate_bank(c) == gate_bank(b)]
                        if before:
                            pe.wait_ge(s("h_done"), before[-1] + 1)
                        for k in range(2):
                            m = mm(bank(gate_bank(b) + k), x5T[:, j * P:(j + 1) * P],
                                   wgu_i[:, k * INNER:(k + 1) * INNER], start=True, stop=True)
                        m.then_inc(s("pe_gu"), 1)
                    if j:
                        down(NH * h + j - 1)

            def down(b):
                at = 5 if b < NH else 4
                pe.wait_ge(s("h_int"), b + 1)
                if b:
                    pe.wait_ge(s("res_f1" if b < NH else "hT"), b)
                for c in range(4):
                    m = turn(bank(5).bitcast(BF16)[:, c * P:(c + 1) * P], hi[:, b % 2, c * P:(c + 1) * P],
                             ident_b[:])
                m.then_inc(s("pe_hT"), 1)
                pe.wait_ge(s("hT"), b + 1)
                if b:
                    pe.wait_ge(s("res_f1"), b)
                for c in range(4):
                    m = mm(bank(at)[:, 0:P], hT[:, b % 2, c * P:(c + 1) * P], wdn_i[:, c * P:(c + 1) * P],
                           start=(c == 0), stop=(c == 3))
                m.then_inc(s("pe_down"), 1)

            for i in range(NPROJ):
                project(0, i)
            pe.wait_ge(s("ident_set"), 1)
            for q in range(4):
                turn_v(0, q)
            pe.wait_ge(s("vn_in"), 4)
            for Q in range(AHEAD):
                scores_q(Q)
                if Q < 4:
                    turn_v(0, 4 + Q)
            pe.wait_ge(s("setup"), 1)
            turn_max(0)
            for t in range(TICKS0):
                project_next(t, 0)
                if t < NQ:
                    scores_k(t)
                if t % 4 == 3 and t < NQ - 1:
                    turn_max(t // 4 + 1)
                project_next(t, 1)
                if t == 1:
                    pe.wait_ge(s("w_abs"), 1)
                    pe.wait_ge(s("masks"), 1)
                    mm(bank(6)[:, 0:3], ones[:], wabs[:, 0:3], start=True, stop=True)\
                        .then_inc(s("pe_wsum"), 1)
                mid(0, mid0(t, 0))
                if 1 <= t <= NQ:
                    weigh(t - 1)
                project_next(t, 2)
                if t % 2 and t >= 3:
                    turn_out((t - 3) // 2)
                if t + AHEAD < NQ:
                    scores_q(t + AHEAD)
                if t % 4 == 2 and t >= 6:
                    project_out((t - 6) // 4)
                mid(0, mid0(t, 1))
                if t >= T1:
                    main1(t - T1)
            for u in range(MID1, TICKS1):
                main1(u)
                mid(1, u - MID1)
                late(0, u - LATE0)
                late(1, u - LATE1)

        @block.scalar
        def _(act):
            fn = nc.scalar.activation

            act.wait_ge(s("ld_x"), 16)
            fn(xh[:], xT[:], ACT.Copy).then_inc(s("hi"), 1)
            for w in range(3):
                for j in range(2):
                    act.wait_ge(s(("ld_wk", "ld_wq", "ld_wv")[w] + str(j)), 16)
                    cols = slice(512 * j, 512 * j + 512)
                    fn(w0h[:, w, cols], w0[:, w, cols], ACT.Copy).then_inc(s("hi"), 1)

            def by_head(buf, i):
                return buf.rearrange("p (n g t) -> p g n t", g=G, t=8)[:, 2 * (i % 4):2 * (i % 4) + 2, :, :]

            def empty_projection(p, i):
                at = i % 8 if p == 0 else i % 2
                src = bank(at).rearrange("p (g n t) -> p g n t", g=2, t=8)
                act.wait_ge(s("proj_done"), 20 * p + i + 1)
                if i < 8:
                    if p >= 2:
                        act.wait_ge(s("sk_done"), QP * (p - 1))
                    dst = by_column((KA, QA)[i // 4][p % 2][0:64, :], i)
                    for a in range(2):
                        m = fn(dst[:, a], src[a * 64:(a + 1) * 64], ACT.Copy)
                    m.then_inc(s("qk_hi"), 1)
                else:
                    fn(by_head(VN[:], i), src, ACT.Copy).then_inc(s("vn_in") if p == 0 else pj_free[i % 2], 1)

            def empty_turned_v(p, q):
                i = NPROJ + q
                at = 4 + q % 4 if p == 0 else i % 2
                act.wait_ge(s("proj_done"), 20 * p + i + 1)
                if q == 0 and p >= 2:
                    act.wait_ge(s("pv_done"), QP * (p - 1))
                src = bank(at)[0:64, :].rearrange("p (n a d) -> p n a d", n=4, a=2)
                for a in range(2):
                    m = fn(V[a * 64:(a + 1) * 64, p % 2, 4 * q:4 * q + 4, 0:DH0], src[:, :, a, :], ACT.Copy)
                m.then_inc(pj_free[i % 2] if p else s("v_in"), 1)

            def exp0(Q):
                act.wait_ge(s("sk_done"), Q + 1)
                if Q >= SLOTS_PT:
                    act.wait_ge(s("pv_done"), Q - SLOTS_PT + 1)
                fn(PT[:, Q % SLOTS_PT, :], bank(3), ACT.Exp, scale=SCALE0).then_inc(s("exp_done"), 1)

            def empty_next(t, k):
                for p, i in next_projection(t, k):
                    if i < NPROJ:
                        empty_projection(p, i)
                    else:
                        empty_turned_v(p, i - NPROJ)

            def normalise(h, k):
                act.wait_ge(s(f"rstd{h}"), k + 1)
                for b in range(NH * h, NH * h + NH):
                    fn(xt[:, b, :], res[:, b, :], ACT.Identity, bias=shift[:, b:b + 1],
                       scale=rstd[:, b:b + 1]).then_inc(s(f"xn{h}"), 1)

            def copy_x(h, k, at):
                act.wait_ge(s(f"pe_x{h}"), k + 1)
                fn(half(xT, h), bank(at), ACT.Copy).then_inc(s(f"xT{h}"), 1)

            def mid(h, i):
                if i == 0:
                    act.wait_ge(s("pe_kx0"), h + 1)
                    fn(kx0, bank(6), ACT.Identity, bias=bx0[:, 1:2]).then_inc(s("kx0"), 1)
                    act.wait_ge(s("pe_vx0"), h + 1)
                    fn(vx0, bank(7), ACT.Copy).then_inc(s("vx0"), 1)
                if i == 2:
                    normalise(h, 0)
                if i == 3:
                    copy_x(h, 0, 6)
                if i == 4:
                    act.wait_ge(s("pe_q0"), h + 1)
                    fn(mA, bank(7), ACT.Identity, bias=bx0[:, 0:1]).then_inc(s("q0"), 1)
                if i == 6:
                    act.wait_ge(s("sub0"), h + 1)
                    fn(mC, mC, ACT.Exp, scale=SCALEX).then_inc(s("exp0"), 1)
                if i == 7:
                    act.wait_ge(s("pe_p0"), h + 1)
                    fn(mA, bank(7), ACT.Copy).then_inc(s("p0T"), 1)
                if i == 11:
                    normalise(h, 1)
                if i == 12:
                    copy_x(h, 1, 7)
                if i == 14:
                    act.wait_ge(s("gate_sub"), h + 1)
                    fn(of_half(lgt, h), of_half(lgt, h), ACT.Exp).then_inc(s("gate_exp"), 1)
                if i == 17:
                    normalise(h, 2)
                if i == 18:
                    copy_x(h, 2, 6)
                if i == 19:
                    act.wait_ge(s("pe_k1a"), h + 1)
                    fn(half(kph, h), bank(7), ACT.Identity, bias=b1[:, 1:2]).then_inc(s(f"kp_hi{h}"), 1)
                if i == 20:
                    act.wait_ge(s("pe_q1a"), h + 1)
                    fn(half(qph, h), bank(6), ACT.Identity, bias=b1[:, 0:1]).then_inc(s(f"qp_hi{h}"), 1)

            def main1(u):
                for b in range(NB):
                    if 4 <= u - u1(b) < 8:
                        q = u - u1(b) - 4
                        v, w = 4 * b + q, k_use[b, q]
                        act.wait_ge(s("scores1_done"), w + 1)
                        if v >= SLOTS_PT:
                            act.wait_ge(s("pv1_done"), v - SLOTS_PT + 1)
                        fn(PT[:, v % SLOTS_PT, :], bank(w % 3), ACT.Exp, scale=SCALE1)\
                            .then_inc(s1_free[w % 3], 1)
                for b in range(NB):
                    if u - u1(b) == 9:
                        act.wait_ge(s("pe_on1"), b + 1)
                        fn(OnT1, bank(4)[:, 0:P], ACT.Copy).then_inc(s("onT1_done"), 1)
                    if u - u1(b) == 7:
                        act.wait_ge(s("pv1_done"), 4 * b + 4)
                        if b >= 2:
                            act.wait_ge(s("pe_ot1"), b - 1)
                        fn(o1[:, b % 2, :], bank(3), ACT.Copy).then_inc(s("o1_out"), 1)

            gate_bank = (6, 6, 6, 6, 6, 0, 2, 6)

            def late(h, i):
                if i == 0:
                    act.wait_ge(s("pe_vx1"), h + 1)
                    fn(vx1, bank(5), ACT.Copy).then_inc(s("vx1"), 1)
                if i == 2:
                    normalise(h, 3)
                if i == 3:
                    copy_x(h, 3, 5)
                if i == 9:
                    normalise(h, 4)
                if i == 11:
                    act.wait_ge(s("pe_x5T"), h + 1)
                    fn(x5T, bank(5).bitcast(BF16)[:, 0:HT], ACT.Copy).then_inc(s("x5T"), 1)
                if 12 <= i <= 20 and i % 2 == 0:
                    j = i // 2 - 6
                    if j == 0:
                        act.wait_ge(s("gu_scale"), h + 1)
                    if j < NH:
                        b = NH * h + j
                        act.wait_ge(s("pe_gu"), b + 1)
                        if b >= 2:
                            act.wait_ge(s("h_done"), b - 1)
                        fn(th[:, b % 2, :], bank(gate_bank[b]), ACT.Tanh, scale=sm8[:, 4, b:b + 1])\
                            .then_inc(s("tanh"), 1)
                    if j:
                        b = NH * h + j - 1
                        act.wait_ge(s("pe_hT"), b + 1)
                        if b >= 2:
                            act.wait_ge(s("pe_down"), b - 1)
                        fn(hT[:, b % 2, :], bank(5).bitcast(BF16)[:, 0:INNER], ACT.Copy).then_inc(s("hT"), 1)
                if i == 23:
                    normalise(h, 5)

            for i in range(NPROJ):
                empty_projection(0, i)
            act.wait_ge(s("v_ones"), 1)
            for q in range(QP):
                empty_turned_v(0, q)
            for t in range(TICKS0):
                empty_next(t, 0)
                if t < NQ:
                    exp0(t)
                empty_next(t, 1)
                mid(0, mid0(t, 0))
                empty_next(t, 2)
                mid(0, mid0(t, 1))
                if t >= T1:
                    main1(t - T1)
            for u in range(MID1, TICKS1):
                main1(u)
                mid(1, u - MID1)
                late(0, u - LATE0)
                late(1, u - LATE1)

        @block.vector
        def _(dve):
            step = [0]
            V_ = nc.vector
            tt, ts, stt = V_.tensor_tensor, V_.tensor_scalar, V_.scalar_tensor_tensor

            def link(ins):
                step[0] += 1
                ins.then_inc(s("dve_step"), 1)
                dve.wait_ge(s("dve_step"), step[0])

            def over(x, n, width):
                return x.unsqueeze(1).broadcast_to([P, n, width])

            def across(x, n, width):
                return x.unsqueeze(2).broadcast_to([P, n, width])

            dve.wait_ge(s("hi"), 1)
            tt(xl[:], xT[:], xh[:].bitcast(F32), ALU.subtract).then_inc(s("lo"), 1)
            for w in range(3):
                for j in range(2):
                    cols = slice(512 * j, 512 * j + 512)
                    dve.wait_ge(s("hi"), 2 * w + j + 2)
                    tt(w0l[:, w, cols], w0[:, w, cols], w0h[:, w, cols].bitcast(F32), ALU.subtract)\
                        .then_inc(s("lo"), 1)

            def lower_parts(p, i):
                at = i % 8 if p == 0 else i % 2
                src = bank(at).rearrange("p (g n t) -> p g n t", g=2, t=8)
                dve.wait_ge(s("qk_hi"), 8 * p + i + 1)
                upper = by_column((KA, QA)[i // 4][p % 2][0:64, :], i)
                lower = by_column((KA[p % 2][64:P, :], QB[p % 2][0:64, :])[i // 4], i)
                for a in range(2):
                    m = tt(lower[:, a], src[a * 64:(a + 1) * 64], upper[:, a], ALU.subtract)
                m.then_inc(s("qk_lo") if p == 0 else pj_free[i % 2], 1)

            def maxima(Q):
                dve.wait_ge(s("sq_done"), Q + 1)
                V_.reduce_max(rowmax[:, 4 * Q:4 * Q + 4], tok(bank(quad_bank(Q))), AX_X)\
                    .then_inc(s("max_done"), 1)

            def negated_maxima(event, count, src, b, done):
                dve.wait_ge(s(event), count)
                link(ts(MR[0:H, b % 2, :], src[0:H, 0:P], -1.0, None, ALU.mult))
                stt(MR[32:32 + H, b % 2, :], src[0:H, 0:P], -1.0, MR[0:H, b % 2, :],
                    ALU.mult, ALU.subtract).then_inc(s(done), 1)

            def max_rows(b):
                if b == 0:
                    dve.wait_ge(s("setup"), 1)
                if b >= 2:
                    dve.wait_ge(s("sk_done"), 4 * (b - 1))
                negated_maxima("turn_done", z_max(b) + 1, bank(5), b, "turn_free")

            def normalize(Q):
                n = 4 * (Q % QP)
                o = bank(4)[:, 0:4 * VW].rearrange("p (n d) -> p n d", n=4)
                dve.wait_ge(s("pv_done"), Q + 1)
                if Q >= QP:
                    dve.wait_ge(s("turn_done"), z_out((Q - QP) // 2) + 1)
                link(V_.reciprocal(rec[:, Q % 2, 0:4], o[:, :, DH0]))
                tt(On[:, n:n + 4, :], o[:, :, 0:DH0], across(rec[:, Q % 2, 0:4], 4, DH0), ALU.mult)\
                    .then_inc(s("norm_done"), 1)

            def place_out(o):
                b = o // 2
                dve.wait_ge(s("turn_done"), z_out(o) + 1)
                src = bank(5).rearrange("p (r a g t) -> p r a g t", r=4, a=2, g=G)
                dst = OT[:, b % 2, :, :].rearrange("p g (m h t) -> p h m g t", h=2, t=8)
                if b >= 2 and o % 2 == 0:
                    dve.wait_ge(s("turn_done"), z_y(b - 2) + 1)
                for h in range(2):
                    for a in range(2):
                        m = V_.tensor_copy(dst[a * 64:(a + 1) * 64, h, 4 * (o % 2):4 * (o % 2) + 4],
                                           src[h * 64:(h + 1) * 64, :, a])
                m.then_inc(s("turn_free"), 1)

            def add_out(b):
                if b == 0:
                    dve.wait_ge(s("ld_wo"), 32)
                dve.wait_ge(s("turn_done"), z_y(b) + 1)
                tt(res[:, b, :], bank(5)[:, 0:P], xt[:, b, :], ALU.add).then_inc(s("turn_free"), 1)

            def lower_next(t, k):
                for p, i in next_projection(t, k):
                    if i < 8:
                        lower_parts(p, i)

            def moments(h, *last):
                if last:
                    dve.wait_ge(*last)
                for b in range(NH * h, NH * h + NH):
                    m = V_.bn_stats(stats[:, b, :], res[:, b, :])
                link(m)
                for b in range(NH * h, NH * h + NH):
                    m = V_.bn_aggr(mv[:, b, :], stats[:, b, :])
                if h == 0:
                    m.then_inc(s("moments0"), 1)
                    return
                link(m)
                v, y, e = (nwt[:, i, NH * h:NH * h + NH] for i in range(3))
                r = of_half(rstd, h)
                link(ts(v, of_half(mv, h)[:, :, 1], EPS, 0.5, ALU.add, ALU.mult))
                link(ts(y.bitcast(I32), v.bitcast(I32), -0.5, RSQRT_BITS - 2 ** 22, ALU.mult, ALU.add))
                for i in range(3):
                    link(stt(e, y, -1.0, y, ALU.mult, ALU.mult))
                    link(tt(e, e, v, ALU.mult))
                    link(stt(r if i == 2 else y, e, 1.5, y, ALU.add, ALU.mult))
                stt(of_half(shift, h), of_half(mv, h)[:, :, 0], -1.0, r, ALU.mult, ALU.mult)\
                    .then_inc(s("rstd1"), 1)

            def mid(h, i):
                hb4 = slice(NH * h, NH * h + NH)
                if i == 0:
                    moments(h, s("turn_free"), z_y(NH * h + NH - 1) + 1)
                if i == 5:
                    dve.wait_ge(s("pe_s0"), h + 1)
                    link(V_.reduce_max(sm8[:, 0, hb4], tok(bank(6)), AX_X))
                    tt(tok(mC), tok(bank(6)), across(sm8[:, 0, hb4], NH, P), ALU.subtract).then_inc(s("sub0"), 1)
                if i == 7:
                    dve.wait_ge(s("exp0"), h + 1)
                    link(V_.reduce_sum(sm8[:, 1, hb4], tok(mC), AX_X))
                    link(V_.reciprocal(sm8[:, 2, hb4], sm8[:, 1, hb4]))
                if i == 8:
                    dve.wait_ge(s(f"x1b{h}"), 1)
                    dve.wait_ge(s("pe_o0"), h + 1)
                    for j in range(NH):
                        b = NH * h + j
                        m = stt(res[:, b, :], bank(6)[:, j * P:(j + 1) * P], sm8[:, 2, b:b + 1],
                                tB[:, b * P:(b + 1) * P], ALU.mult, ALU.add)
                    link(m)
                if i == 9:
                    moments(h)
                if i == 13:
                    if h == 0:
                        dve.wait_ge(s("ld_mid"), 160)
                    dve.wait_ge(s("pe_ffn"), h + 1)
                    ge = PS[:, 6:8, :].rearrange("p k (i c) -> p (k i) c", i=2)
                    l4 = of_half(lgt, h)
                    link(tt(l4, ge[:, :, P:P + NE], over(bge_s[:, P:P + NE], NH, NE), ALU.add))
                    link(V_.reduce_max(sm8[:, 0, hb4], l4, AX_X))
                    tt(l4, l4, across(sm8[:, 0, hb4], NH, NE), ALU.subtract).then_inc(s("gate_sub"), 1)
                    tt(tok(mC), ge[:, :, 0:P], over(bge_s[:, 0:P], NH, P), ALU.add)
                if i == 15:
                    dve.wait_ge(s("gate_exp"), h + 1)
                    link(V_.reduce_sum(sm8[:, 1, hb4], of_half(lgt, h), AX_X))
                    link(V_.reciprocal(sm8[:, 2, hb4], sm8[:, 1, hb4]))
                    for j in range(NH):
                        b = NH * h + j
                        m = stt(res[:, b, :], mC[:, j * P:(j + 1) * P], sm8[:, 2, b:b + 1], xt[:, b, :],
                                ALU.mult, ALU.add)
                    link(m)
                    moments(h)
                if i == 19:
                    dve.wait_ge(s(f"kp_hi{h}"), 1)
                    stt(half(kpl, h), bank(7), b1[:, 1:2], half(kph, h), ALU.add, ALU.subtract)\
                        .then_inc(s(f"kp_lo{h}"), 1)
                if i == 20:
                    dve.wait_ge(s(f"qp_hi{h}"), 1)
                    stt(half(qpl, h), bank(6), b1[:, 0:1], half(qph, h), ALU.add, ALU.subtract)\
                        .then_inc(s(f"qp_lo{h}"), 1)
                if i == 21:
                    dve.wait_ge(s(f"ve_ones{h}"), 1)
                    dve.wait_ge(s("pe_v1a"), h + 1)
                    tt(VE[h].rearrange("p (b n c) -> p b n c", b=NH, n=H)[:, :, :, 0:DH1],
                       bank(7).rearrange("p (b n c) -> p b n c", b=NH, n=H),
                       bv1_s[:].rearrange("p (n c) -> p n c", n=H).unsqueeze(1).broadcast_to([P, NH, H, DH1]),
                       ALU.add).then_inc(s(f"ve_done{h}"), 1)

            def main1(u):
                for b in range(NB):
                    if 0 <= u - u1(b) < 4:
                        q = u - u1(b)
                        w = q_use[b, q]
                        dve.wait_ge(s("scores1_done"), w + 1)
                        V_.reduce_max(rowmax[:, b * H + 4 * q:b * H + 4 * q + 4], tok(bank(w % 3)), AX_X)\
                            .then_inc(s1_free[w % 3], 1)
                for b in range(NB):
                    if u - u1(b) == 8:
                        o = bank(4).rearrange("p (n c) -> p n c", n=H)
                        dve.wait_ge(s("pe_ot1"), b + 1)
                        link(V_.reciprocal(rec[:, b % 2, :], o[:, :, DH1]))
                        if b:
                            dve.wait_ge(s("pe_on1"), b)
                        tt(On1.rearrange("p (n c) -> p n c", n=H), o[:, :, 0:DH1],
                           across(rec[:, b % 2, :], H, DH1), ALU.mult).then_inc(s("on1_done"), 1)
                    if u - u1(b) == 10:
                        dve.wait_ge(s(f"x3b{b // NH}"), 1)
                        dve.wait_ge(s("pe_y1"), b + 1)
                        tt(res[:, b, :], bank(4)[:, P:2 * P], tB[:, b * P:(b + 1) * P], ALU.add)\
                            .then_inc(s("res1_done"), 1)
                for b in range(NB):
                    if u - u1(b) == 3:
                        if b >= 2:
                            dve.wait_ge(s("scores1_done"), k_use[b - 2, 3] + 1)
                        negated_maxima("pe_mt1", b + 1, bank(4), b, "mr1_done")

            gate_bank = (6, 6, 6, 6, 6, 0, 2, 6)

            def hidden(b):
                h, sc = hb[:, b % 2, :], hs[:, b % 2, :]
                dve.wait_ge(s("tanh"), b + 1)
                link(stt(h, th[:, b % 2, :], 1.0, bank(gate_bank[b]), ALU.add, ALU.mult))
                stt(h, bank(gate_bank[b] + 1), sm8[:, 5, b:b + 1], h, ALU.mult, ALU.mult)\
                    .then_inc(s("h_done"), 1)
                dve.wait_ge(s("h_done"), b + 1)
                link(V_.tensor_reduce(sc[:, 0:1], h, AX_X, ALU.max, apply_absolute_value=True))
                link(ts(sc[:, 1:2], sc[:, 0:1], 1e-5, 1.0 / 127.0, ALU.max, ALU.mult))
                link(V_.reciprocal(sc[:, 2:3], sc[:, 1:2]))
                link(ts(h, h, sc[:, 2:3], MAGIC, ALU.mult, ALU.add))
                if b >= 2:
                    dve.wait_ge(s("pe_hT"), b - 1)
                ts(hi[:, b % 2, :], h, MAGIC + 127.0, MAGIC, ALU.min, ALU.subtract).then_inc(s("h_int"), 1)
                link(ts(sm8[:, 6, b:b + 1], sc[:, 1:2], wscl[:, 2:3], None, ALU.mult))

            def add_down(b):
                dve.wait_ge(s("pe_down"), b + 1)
                stt(res[:, b, :], bank(5 if b < NH else 4)[:, 0:P], sm8[:, 6, b:b + 1], xt[:, b, :],
                    ALU.mult, ALU.add).then_inc(s("res_f1"), 1)

            def late(h, i):
                hb4 = slice(NH * h, NH * h + NH)
                if i == 0:
                    moments(h, s("res1_done"), NH * (h + 1))
                    dve.wait_ge(s("pe_k1"), h + 1)
                    tt(tok(lD), tok(bank(6)), over(rot_s[:, 2, :], NH, P), ALU.mult)
                    tt(tok(lC), tok(bank(7)), over(rot_s[:, 3, :], NH, P), ALU.mult).then_inc(s("k1_mul"), 1)
                if i == 4:
                    dve.wait_ge(s("pe_q"), h + 1)
                    tt(tok(lA), tok(bank(6)), over(rot_s[:, 0, :], NH, P), ALU.mult)
                    tt(tok(lE), tok(bank(7)), over(rot_s[:, 1, :], NH, P), ALU.mult).then_inc(s("q_mul"), 1)
                if i == 6:
                    dve.wait_ge(s("pe_sx1"), h + 1)
                    tt(tok(lD), tok(bank(5)), over(decay_s[:], NH, P), ALU.mult).then_inc(s("sx1"), 1)
                if i == 7:
                    dve.wait_ge(s("pe_ox1"), h + 1)
                    link(tt(of_half(res, h), tok(bank(6)), of_half(xt, h), ALU.add))
                    moments(h)
                if i == 10:
                    dve.wait_ge(s(f"xn{h}"), 5 * NH)
                    link(V_.tensor_reduce(sm8[:, 0, hb4], of_half(xt, h), AX_X, ALU.max,
                                          apply_absolute_value=True))
                    link(ts(sm8[:, 1, hb4], sm8[:, 0, hb4], 1e-5, 1.0 / 127.0, ALU.max, ALU.mult))
                    link(V_.reciprocal(sm8[:, 2, hb4], sm8[:, 1, hb4]))
                    for j in range(NH):
                        b = NH * h + j
                        m = ts(x5r[:, j * P:(j + 1) * P], xt[:, b, :], sm8[:, 2, b:b + 1], MAGIC,
                               ALU.mult, ALU.add)
                    link(m)
                    ts(x5q, x5r, MAGIC + 127.0, MAGIC, ALU.min, ALU.subtract).then_inc(s("x5q"), 1)
                    link(ts(sm8[:, 4, hb4], sm8[:, 1, hb4], wscl[:, 0:1], 0.5, ALU.mult, ALU.mult))
                    link(ts(sm8[:, 5, hb4], sm8[:, 1, hb4], wscl[:, 1:2], None, ALU.mult))
                    tt(sm8[:, 5, hb4], sm8[:, 5, hb4], sm8[:, 4, hb4], ALU.mult).then_inc(s("gu_scale"), 1)
                if 12 <= i <= 20 and i % 2 == 0:
                    j = i // 2 - 6
                    if j == 0:
                        dve.wait_ge(s("gu_scale"), h + 1)
                    if j < NH:
                        hidden(NH * h + j)
                    if j:
                        add_down(NH * h + j - 1)
                if i == 21:
                    moments(h, s("res_f1"), NH * (h + 1))

            for i in range(8):
                lower_parts(0, i)
            for Q in range(AHEAD):
                maxima(Q)
            max_rows(0)
            for t in range(TICKS0):
                lower_next(t, 0)
                if t % 4 == 3 and t < NQ - 1:
                    max_rows(t // 4 + 1)
                lower_next(t, 1)
                if t == 0:
                    dve.wait_ge(s("ld_late"), 32)
                    for i in range(2):
                        V_.tensor_reduce(wabs[:, i:i + 1], wgu_s[:, i * INNER:(i + 1) * INNER], AX_X, ALU.add,
                                         apply_absolute_value=True)
                    V_.tensor_reduce(wabs[:, 2:3], wdn_s[:], AX_X, ALU.add, apply_absolute_value=True)\
                        .then_inc(s("w_abs"), 1)
                if t == 2:
                    dve.wait_ge(s("pe_wsum"), 1)
                    link(ts(wscl[:, 0:3], bank(6)[:, 0:3], 1.0 / NW, 1e-5, ALU.mult, ALU.max))
                    V_.reciprocal(wscl[:, 4:7], wscl[:, 0:3]).then_inc(s("w_scale"), 1)
                mid(0, mid0(t, 0))
                if 1 <= t <= NQ:
                    normalize(t - 1)
                lower_next(t, 2)
                if t % 2 and t >= 3:
                    place_out((t - 3) // 2)
                if t + AHEAD < NQ:
                    maxima(t + AHEAD)
                if t % 4 == 2 and t >= 6:
                    add_out((t - 6) // 4)
                mid(0, mid0(t, 1))
                if t >= T1:
                    main1(t - T1)
            for u in range(MID1, TICKS1):
                main1(u)
                mid(1, u - MID1)
                late(0, u - LATE0)
                late(1, u - LATE1)


def kernel(**inputs):
    import numpy as np
    import concourse.bacc as bacc
    from concourse.bass_utils import run_bass_kernel_spmd

    f = {k: np.asarray(v) for k, v in inputs.items()}
    c = np.ascontiguousarray

    def by_group(w):
        return c(w.reshape(2, G, DH0, P).transpose(3, 1, 0, 2).reshape(P, 1024))

    swap = np.arange(P) ^ 1
    f32 = np.float32
    base = (np.arange(0, P, 2, dtype=f32) + f32(0.4 * P)) / f32(1.4 * P)
    pos = np.arange(P, dtype=f32)
    scale = base[None, :] ** (pos / f32(512.0))[:, None]
    freqs = f32(1.0) / f32(10000.0) ** (np.arange(P // 2, dtype=f32) / f32(P // 2))
    angle = pos[:, None] * freqs[None, :]
    sign = np.where(np.arange(P) % 2 == 0, -1.0, 1.0).astype(f32)

    def twice(t):
        return np.repeat(t, 2, axis=1).T.astype(f32)
    rot = np.stack([twice(np.cos(angle) * scale), twice(np.sin(angle) * scale) * sign[:, None],
                    twice(np.cos(angle) * (f32(1.0) / scale)),
                    twice(np.sin(angle) * (f32(1.0) / scale)) * sign[:, None]], axis=1)
    ahead = pos[None, :] - pos[:, None]
    decay = np.where(ahead >= 0, f32(0.96875) ** np.maximum(ahead, 0), 0).astype(f32)

    wa, ba = f["L1_attn_W_attn"], f["L1_attn_b_attn"]
    arrays = {
        "x_tok": c(f["x"].transpose(1, 0, 2)), "x_T": c(f["x"].transpose(2, 0, 1).reshape(P, NTOK)),
        "ctx_T": c(f["ctx_1024"].transpose(2, 0, 1).reshape(P, NTOK)),
        "wq0": by_group(f["L0_attn_wq"]), "wk0": by_group(f["L0_attn_wk"]), "wv0": by_group(f["L0_attn_wv"]),
        "wo0": c(f["L0_attn_wo"].reshape(P, 2, G, DH0).transpose(1, 3, 2, 0).reshape(P, G, P)),
        "xwq0": c(f["L0_xattn_Wq"].T), "xbq0": f["L0_xattn_bq"].reshape(P, 1),
        "xwk0": c(f["L0_xattn_Wk"].T), "xbk0": f["L0_xattn_bk"].reshape(P, 1),
        "xwv0": c(f["L0_xattn_Wv"].T), "xbv0": f["L0_xattn_bv"].reshape(1, P),
        "wge": c(np.concatenate([f["L0_ffn_We"], f["L0_ffn_Wg"]], axis=1)),
        "bge": np.concatenate([f["L0_ffn_be"], f["L0_ffn_bg"]]).reshape(1, P + NE),
        "wqk1": c(wa[:, 0:2 * P].reshape(P, 2, P)), "bqk1": c(ba[0:2 * P].reshape(2, P).T),
        "wv1": c(wa[:, 2 * P:3 * P]), "bv1": c(ba[2 * P:3 * P].reshape(1, P)),
        "wp1": f["L1_attn_W_proj"], "bp1": f["L1_attn_b_proj"].reshape(1, P),
        "xwq1": f["L1_xattn_Wq"], "xwq1s": c(f["L1_xattn_Wq"][:, swap]),
        "xwk1": f["L1_xattn_Wk"], "xwk1s": c(f["L1_xattn_Wk"][:, swap]), "xwv1": f["L1_xattn_Wv"],
        "wgu": c(np.concatenate([f["L1_ffn_w_gate"].T, f["L1_ffn_w_up"].T], axis=1)),
        "wdn": c(f["L1_ffn_w_down"].T.reshape(4, P, P).transpose(1, 0, 2).reshape(P, INNER)),
        "rot": c(rot), "decay": decay,
    }
    nc = bacc.Bacc("TRN2", target_bir_lowering=False, num_devices=1)
    args = [nc.dram_tensor(n, a.shape, mybir.dt.from_np(a.dtype), kind="ExternalInput").ap()
            for n, a in arrays.items()]
    result = nc.dram_tensor("out", (NB, P, P), F32, kind="ExternalOutput").ap()
    decoder(nc, *args, result)
    done = run_bass_kernel_spmd(nc, [arrays], core_ids=[0])
    return done.results[0]["out"]
```

```python
from contextlib import ExitStack

import concourse.bass as bass
from concourse import mybir

ALU = mybir.AluOpType
ACT = mybir.ActivationFunctionType
F32 = mybir.dt.float32
F32R = mybir.dt.float32r
F16 = mybir.dt.float16
BF16 = mybir.dt.bfloat16
I32 = mybir.dt.int32
AX_X = mybir.AxisListType.X

P = 128
NB = 8
NTOK = NB * P
H = 16
DH0 = 64
G = 8
DH1 = 8
INNER = 512
NE = 8
NPAIR = NB // 2
TP = 2 * P
HP = 2 * H
QP = HP // 4
VW = 96
NPROJ = 12
SLOTS_PT = 3
N = (3, 3, 2, 4, 4)
B0 = (0, 3, 6, 0, 4)
LAST = tuple(b + n - 1 for b, n in zip(B0, N))
MIDS, LATES = (0, 1, 2), (3, 4)
GROUP = tuple(g for g in MIDS for _ in range(N[g]))
ON_POOL = (0, 3)
NQ = NPAIR * QP
AHEAD = 5
TICKS0 = NQ + 3
T1 = NQ
GAP = 2
SCALE0 = DH0 ** -0.5
SCALE1 = DH1 ** -0.5
SCALEX = P ** -0.5
EPS = 1e-5
MAGIC = 1.5 * 2.0 ** 23
RSQRT_BITS = 0x5F3759DF
MASKED = -1e30
NW = INNER * P


def decoder(nc, x_tok, x_T, ctx_T, wq0, wk0, wv0, wo0, xwq0, xbq0, xwk0, xbk0, xwv0, xbv0,
            wge, bge, wqk1, bqk1, wv1, bv1, wp1, bp1, xwq1, xwq1s, xwk1, xwk1s, xwv1,
            wgu, wdn, rot, decay, out):
    k_piece = nc.dram_tensor("k_piece", [2, P, NTOK], F16, kind="Internal").ap()
    q_piece = nc.dram_tensor("q_piece", [2, P, NTOK], F16, kind="Internal").ap()

    with ExitStack() as ctx:
        def sb(name, shape, dt=F32):
            return ctx.enter_context(nc.sbuf_tensor(name, shape, dt))

        def sem(name):
            return ctx.enter_context(nc.semaphore(name))

        PS = ctx.enter_context(nc.psum_tensor("PS", [P, 8, 512], F32))
        xt = sb("xt", [P, NB, P])
        xT = sb("xT", [P, NTOK])
        cT = sb("cT", [P, NTOK])
        w0 = sb("w0", [P, 3, 1024])
        w0h = sb("w0h", [P, 3, 1024], F32R)
        w0l = sb("w0l", [P, 3, 1024], F32R)
        wo = sb("wo", [P, G, P])
        xh = sb("xh", [P, NTOK], F32R)
        xl = sb("xl", [P, NTOK], F32R)
        arena = sb("arena", [P, 32768], F16)
        VN = sb("VN", [P, 2048])
        V = sb("V", [P, 2, HP, VW])
        PT = sb("PT", [P, SLOTS_PT, 512])
        On = sb("On", [P, HP, DH0])
        OT = sb("OT", [P, 2, G, P])
        En = sb("En", [P, H, P], F16)
        rowmax = sb("rowmax", [P, P])
        MR = sb("MR", [P, 2, P], F16)
        ident = sb("ident", [P, P])
        ident_b = sb("ident_b", [P, P], BF16)
        maskq = sb("maskq", [P, P], BF16)
        maskk = sb("maskk", [P, P], BF16)
        res = sb("res", [P, NB, P])
        stats = sb("stats", [P, NB, 6])
        mv = sb("mv", [P, NB, 2])
        rstd = sb("rstd", [P, NB])
        shift = sb("shift", [P, NB])
        nwt = sb("nwt", [P, 3, NB])
        rec = sb("rec", [P, 2, H])
        wx0 = sb("wx0", [P, 3, P])
        bx0 = sb("bx0", [P, 2])
        bvx0 = sb("bvx0", [P, P])
        wge_s = sb("wge_s", [P, P + NE])
        bge_s = sb("bge_s", [P, P + NE])
        w1 = sb("w1", [P, 3, P])
        b1 = sb("b1", [P, 2])
        bv1_s = sb("bv1_s", [P, P])
        wp1_s = sb("wp1_s", [P, P])
        bp1_s = sb("bp1_s", [P, P])
        wx1 = sb("wx1", [P, 5, P])
        rot_s = sb("rot_s", [P, 4, P])
        decay_s = sb("decay_s", [P, P])
        wgu_s = sb("wgu_s", [P, 2 * INNER])
        wdn_s = sb("wdn_s", [P, INNER])
        wabs = sb("wabs", [P, 4])
        wscl = sb("wscl", [P, 8])
        ones = sb("ones", [P, P])
        hs = sb("hs", [P, 4, 4])
        sm8 = sb("sm8", [P, 8, NB])
        lgt = sb("lgt", [P, NB, NE])

        def part(i, n=4096):
            return arena[:, i * n:(i + 1) * n]

        def flat(x):
            return x.rearrange("p a b -> p (a b)")
        QA = [part(0), part(3)]
        QB = [part(1), part(4)]
        KA = [part(2), part(5)]

        w0f, Vf, af = flat(w0[:]), V[:].rearrange("p a n c -> p (a n c)"), arena[:].bitcast(F32)
        ab = arena[:].bitcast(BF16)
        tB = w0f[:, 0:NTOK]
        mA, mC, kx0, vx0 = (w0f[:, NTOK + i * 512:NTOK + (i + 1) * 512] for i in range(4))
        stacks = [arena[:, 0:12288], arena[:, 12288:24576], Vf[:, 0:4096].bitcast(F16)]
        Kst, Qst = ([st.rearrange("p (i n t) -> p i n t", i=2, n=H)[:, i] for st in stacks] for i in range(2))
        VE = [af[:, 12288 + B0[g] * H * 32:12288 + (B0[g] + N[g]) * H * 32]
              for g in MIDS]
        o1 = Vf[:, 4096:5120].rearrange("p (i c) -> p i c", i=2)
        On1, OnT1 = Vf[:, 5120:5120 + P], Vf[:, 5120 + P:5120 + 2 * P]
        VNh = VN[:].bitcast(F16)
        kph, kpl, qph, qpl = (VNh[:, i * NTOK:(i + 1) * NTOK] for i in range(4))
        def two(first, offset, n, where=af):
            return dict(zip(LATES, (where[:, x + first:x + first + n] for x in (0, offset))))

        def ring(both):
            return {g: x.rearrange("p (i c) -> p i c", i=2) for g, x in both.items()}
        lA, lC, lD, lE = (dict(zip(LATES, (x, Vf[:, i * 512:(i + 1) * 512])))
                          for i, x in enumerate((mA, mC, kx0, vx0)))
        kx1, vx1, x5r = (two(i * 512, 6144, 512) for i in range(3))
        hb, th = (ring(two(1536 + i * 1024, 6144, 1024)) for i in range(2))
        x5q, x5T = (two(7168 + i * 512, 12288, 512, ab) for i in range(2))
        hi, hT = (ring(two(8192 + i * 1024, 12288, 1024, ab)) for i in range(2))
        LBANKS = {3: (5, 6, 7), 4: (4, 0, 1)}

        def gate_bank(b):
            return 6 if b < B0[-1] else 2 * (b % 2)

        def gates_at(g, j):
            ahead = int(g == LATES[-1])
            return [B0[g] + k for k in (range(ahead + 1) if j == 0 else (j + ahead,)) if k < N[g]]

        def down_bank(b):
            return LBANKS[LATES[b >= B0[-1]]][0]
        wob = flat(wo[:]).bitcast(BF16)
        wgu_i, wdn_i = wob[:, 0:2 * INNER], wob[:, 2 * INNER:3 * INNER]

        def head(buf, n):
            return buf[:, n * P:(n + 1) * P]

        def by_column(buf, i):
            v = buf.rearrange("p (n a g t) -> p a g n t", a=2, g=G, t=8)
            return v[:, :, 2 * (i % 4):2 * (i % 4) + 2, :, :]

        def bank(i):
            return PS[:, i, :]

        named = {}

        def s(name):
            if name not in named:
                named[name] = sem(name)
            return named[name]

        qk_in = [sem("qk_in0"), sem("qk_in1")]
        pj_free = [sem("pj_free0"), sem("pj_free1")]
        s1_free = [sem(f"s1_free{i}") for i in range(3)]

        block = ctx.enter_context(nc.Block())

        PJ = ((0, 1, 2), (3, 4, 5), (6, 7), (8, 9), (10, 11), (12, 13), (14, 15, 16), (17, 18, 19))

        def next_projection(t, k):
            banks = PJ[t % QP]
            return ((t // QP + 1, banks[k]),) if t < NQ - QP and k < len(banks) else ()

        def quad_bank(Q):
            return 3 if Q in (1, 3) else 2

        def z_max(b):
            return 4 * b - 3 if b else 0

        def z_out(o):
            return 4 * (o // 2) + 2 + o % 2 - (o // 2 == NB - 1)

        def z_y(b):
            return 4 * b + 4 - (b == NB - 1)

        def u1(b):
            return 4 * b + (GAP if b >= B0[-1] else 0)

        def out_step(b, u):
            i = u - u1(b) - 10
            return (0, 1, 2) if i == 0 and b == NB - 1 else (i,) if 0 <= i <= 2 and b < NB - 1 else ()

        def normalised(g, k, j):
            if g != LATES[-1]:
                return s(f"xn{g}"), N[g] * k + j + 1
            return (s("xn4"), 2 * k + j + 1) if j < 2 else (s("xn4_dve"), 2 * k + j - 1)

        FFN_END = {}
        TICKS = {}

        def plan(kind, g, t, k, places, ffn_from=(0, 0)):
            F = 12 + 2 * N[g]
            steps = {"mid": (0, 2, 3, 4, 5, 6, 7, 8, 9, 11, 12, 13, 14, 15, 17, 18, 19, 20, 21),
                     "late": (0, 2, 3, 4, 6, 7, 9, 10, 11, *range(12, F + 1), F + 1, F + 3)}[kind]
            roots = {"mid": (0, 9, 15), "late": (0, 7, F + 1)}[kind]
            for i in steps:
                if kind == "late" and i == 12:
                    t, k = max((t, k), ffn_from)
                TICKS.setdefault((t, places[k]), []).append((kind, g, i))
                skip = 1 + (WAITS[kind] if i in roots and g in ON_POOL else 0)
                if t < TICKS0 and i in roots and g not in ON_POOL:
                    skip += MROOT
                if t >= TICKS0:
                    skip += SLACK[kind].get(i, 0)
                t, k = t + (k + skip) // len(places), (k + skip) % len(places)
                if i == F:
                    FFN_END[g] = t, k
            return t, k
        WAITS = {"mid": 3, "late": 6}
        MROOT = 2
        SLACK = {"mid": {}, "late": {2: 1, 9: 1, 10: 3, 12: 2, 14: 2, 16: 2, 18: 2, 21: 14}}
        at = plan("mid", 0, 4 * LAST[0] + 6, 1, (0, 2))
        at = plan("mid", 1, *max((at[0] + 1, 0), (4 * LAST[1] + 7, 0)), (0, 1, 2))
        at = plan("mid", 2, *max((at[0] + 1, 0), (4 * LAST[2] + 7, 0)), (1,))
        at = plan("late", 3, *max(at, (T1 + u1(LAST[3]) + 13, 0)), (0, 1))
        at = max(at, plan("late", 4, T1 + u1(LAST[4]) + 11, 0, (0, 1), FFN_END[3]))
        TICKS1 = at[0] + 1 - T1

        q_use, k_use = {}, {}
        for u in range(TICKS1):
            for uses, at in ((q_use, 0), (k_use, 5)):
                for b in range(NB):
                    if 0 <= u - at - u1(b) < 4:
                        uses[b, u - at - u1(b)] = len(q_use) + len(k_use)

        def v_there(p, q):
            return (pj_free[q % 2], 10 * (p - 1) + (NPROJ + q) // 2 + 1) if p else (s("v_in"), q + 1)

        @block.sync
        def _(sp):
            sp.dma_start(xT[:], x_T).then_inc(s("ld_x"), 16)
            for name, i, w in (("ld_wk", 0, wk0), ("ld_wq", 1, wq0), ("ld_wv", 2, wv0)):
                for j in range(2):
                    cols = slice(j * 512, (j + 1) * 512)
                    sp.dma_start(w0[:, i, cols], w[:, cols]).then_inc(s(name + str(j)), 16)
            sp.dma_start(wo[:], wo0).then_inc(s("ld_wo"), 16)
            sp.dma_start(xt[:], x_tok).then_inc(s("ld_wo"), 16)
            sp.dma_start(cT[:], ctx_T).then_inc(s("ld_ctx"), 16)
            for dst, src in ((wx0[:, 0, :], xwq0), (wx0[:, 1, :], xwk0), (wx0[:, 2, :], xwv0),
                             (bx0[:, 0:1], xbq0), (bx0[:, 1:2], xbk0),
                             (wx1[:, 0, :], xwq1), (wx1[:, 1, :], xwq1s), (wx1[:, 2, :], xwk1),
                             (wx1[:, 3, :], xwk1s), (wx1[:, 4, :], xwv1),
                             (rot_s[:], rot)):
                sp.dma_start(dst, src).then_inc(s("ld_ctx"), 16)
            sp.dma_start(wgu_s[:], wgu).then_inc(s("ld_late"), 16)
            sp.dma_start(wdn_s[:], wdn).then_inc(s("ld_late"), 16)
            for dst, src in ((bvx0[:], xbv0.partition_broadcast(P)), (wge_s[:], wge),
                             (bge_s[:], bge.partition_broadcast(P)),
                             (w1[:, 0:2, :], wqk1), (w1[:, 2, :], wv1), (b1[:], bqk1),
                             (bv1_s[:], bv1.partition_broadcast(P)), (wp1_s[:], wp1),
                             (bp1_s[:], bp1.partition_broadcast(P)), (decay_s[:], decay)):
                sp.dma_start(dst, src).then_inc(s("ld_mid"), 16)

            for p in range(NPAIR):
                b = p % 2
                lower = (pj_free[1], 10 * (p - 1) + 4) if p else (s("qk_lo"), 8)
                for (split, count), dst in (((s("qk_hi"), 8 * p + 8), QA), (lower, QB)):
                    sp.wait_ge(split, count)
                    sp.dma_start(dst[b][64:P, :], dst[b][0:64, :]).then_inc(qk_in[b], 16)

            for h in MIDS:
                cols = slice(B0[h] * P, (B0[h] + N[h]) * P)
                sp.wait_ge(s(f"stack_zero{h}"), 1)
                for x, hi_, lo_, piece, stack, order in (("k", kph, kpl, k_piece, Kst[h], (0, 0, 1, 1)),
                                                         ("q", qph, qpl, q_piece, Qst[h], (0, 1, 0, 1))):
                    for i, src in enumerate((hi_, lo_)):
                        sp.wait_ge(s(f"{x}p_{('hi', 'lo')[i]}{h}"), 1)
                        sp.dma_start(piece[i][:, cols], src[:, cols]).then_inc(s(f"{x}_out{h}"), 16)
                    sp.wait_ge(s(f"{x}_out{h}"), 32)
                    for row, i in enumerate(order):
                        sp.dma_start(stack[8 * row:8 * row + 8, :, :],
                                     piece[i].rearrange("(n d) t -> d n t", d=DH1)[:, :, cols])\
                            .then_inc(s(f"stack_in{h}"), 16)
            for b in range(NB):
                g = LATES[b >= B0[-1]]
                sp.wait_ge(*normalised(g, 2, b - B0[g]))
                sp.dma_start(out[b], xt[:, b, :]).then_inc(s("out_sem"), 16)
            sp.wait_ge(s("out_sem"), 16 * NB)

        def tok(x, n=4):
            return x[:, 0:n * P].rearrange("p (b d) -> p b d", b=n)

        def tokens(x, g):
            return x[:, B0[g] * P:(B0[g] + N[g]) * P]

        def batches(x, g):
            return x[:, B0[g]:B0[g] + N[g]]

        def part_of(x, g):
            return x[:, 0:N[g] * P]

        @block.gpsimd
        def _(pool):
            step = [0]
            ts, tt = nc.gpsimd.tensor_scalar, nc.gpsimd.tensor_tensor

            def link(ins):
                step[0] += 1
                ins.then_inc(s("pool_step"), 1)
                pool.wait_ge(s("pool_step"), step[0])

            pool.memset(ident[:], 0.0)
            link(pool.memset(ident_b[:], 0.0))
            for m in (ident, ident_b):
                m = pool.affine_select(out=m[:], in_=m[:], compare_op=ALU.not_equal, fill=1.0,
                                       base=0, pattern=[[-1, P]], channel_multiplier=1)
            m.then_inc(s("ident_set"), 1)
            link(pool.memset(V[:, :, :, DH0:VW], 0.0))
            pool.memset(V[:, :, :, DH0:DH0 + 1], 1.0).then_inc(s("v_ones"), 1)
            pool.memset(En[:], 0.0)
            link(pool.memset(MR[:], 0.0))
            link(pool.affine_select(out=En[:], in_=En[:], compare_op=ALU.not_equal, fill=1.0,
                                    base=0, pattern=[[-1, H], [0, P]], channel_multiplier=1))
            pool.affine_select(out=En[:], in_=En[:], compare_op=ALU.not_equal, fill=1.0,
                               base=-32, pattern=[[-1, H], [0, P]], channel_multiplier=1)\
                .then_inc(s("setup"), 1)
            pool.memset(maskq[:], 0.0)
            pool.memset(maskk[:], 0.0)
            link(pool.memset(ones[:], 1.0))
            pool.affine_select(out=maskq[:], in_=maskq[:], compare_op=ALU.is_ge, fill=MASKED,
                               base=0, pattern=[[-1, P]], channel_multiplier=1)
            pool.affine_select(out=maskk[:], in_=maskk[:], compare_op=ALU.is_ge, fill=MASKED,
                               base=0, pattern=[[1, P]], channel_multiplier=-1)\
                .then_inc(s("masks"), 1)
            link(pool.memset(af[:, 12288:16384], 0.0))
            for v in VE:
                m = pool.memset(v.rearrange("p (x c) -> p x c", c=32)[:, :, DH1:DH1 + 1], 1.0)
            m.then_inc(s("ve_ones"), 1)

            def rsqrt(g, k):
                if g not in ON_POOL:
                    return
                v, y, e = (nwt[:, i, B0[g]:B0[g] + N[g]] for i in range(3))
                r = batches(rstd, g)
                pool.wait_ge(s(f"moments{g}"), k + 1)
                ts(batches(shift, g), batches(mv, g)[:, :, 0], -1.0, None, ALU.mult)
                link(ts(v, batches(mv, g)[:, :, 1], EPS, 0.5, ALU.add, ALU.mult))
                link(ts(y.bitcast(I32), v.bitcast(I32), -0.5, RSQRT_BITS - 2 ** 22, ALU.mult, ALU.add))
                for i in range(3):
                    link(tt(e, y, y, ALU.mult))
                    link(tt(e, e, v, ALU.mult))
                    link(ts(e, e, -1.0, 1.5, ALU.mult, ALU.add))
                    link(tt(r if i == 2 else y, y, e, ALU.mult))
                tt(batches(shift, g), batches(shift, g), r, ALU.mult)\
                    .then_inc(s(f"rstd{g}"), 1)

            def add_bias(g, k, bias, event):
                pool.wait_ge(s(f"xn{g}"), N[g] * (k + 1))
                tt(tok(tokens(tB, g), N[g]), batches(xt, g), bias.unsqueeze(1).broadcast_to([P, N[g], P]), ALU.add)\
                    .then_inc(s(event), 1)

            def ternary(n):
                src, dst = ((wgu_s[:, 0:INNER], wgu_i[:, 0:INNER]),
                            (wgu_s[:, INNER:2 * INNER], wgu_i[:, INNER:2 * INNER]), (wdn_s[:], wdn_i[:]))[n]
                link(ts(src, src, wscl[:, 4 + n:5 + n], MAGIC, ALU.mult, ALU.add))
                link(ts(src, src, MAGIC + 1.0, MAGIC - 1.0, ALU.min, ALU.max))
                ts(dst, src, MAGIC, None, ALU.subtract).then_inc(s("w_int"), 1)

            def zero(g):
                pool.wait_ge(*((s("sk_done"), 24), (s("sk_done"), NQ), (s("pv_done"), NQ))[g])
                x = (af[:, 0:6144], af[:, 6144:12288], Vf[:, 0:4096])[g]
                pool.memset(x, 0.0).then_inc(s(f"stack_zero{g}"), 1)

            def mid(g, i):
                if i == 0:
                    rsqrt(g, 0)
                if i == 2:
                    if g == 0:
                        pool.wait_ge(s("ld_mid"), 160)
                    add_bias(g, 0, bvx0[:], f"x1b{g}")
                if i == (17, 17, 3)[g]:
                    zero(g)
                if i == 4 and g == 2:
                    pool.wait_ge(s("w_scale"), 1)
                    pool.wait_ge(s("turn_done"), 8 * NPAIR)
                    ternary(0)
                if i == 9:
                    rsqrt(g, 1)
                if i == 12 and g == 2:
                    ternary(1)
                if i == 15:
                    rsqrt(g, 2)
                if i == 18:
                    add_bias(g, 2, bp1_s[:], f"x3b{g}")
                if i == 19 and g == 2:
                    ternary(2)

            def late(g, i):
                if i == 0:
                    rsqrt(g, 0)
                if i == 7:
                    rsqrt(g, 1)
                if i == 13 + 2 * N[g]:
                    rsqrt(g, 2)

            def run(t, k):
                for kind, g, i in TICKS.get((t, k), ()):
                    (mid if kind == "mid" else late)(g, i)

            for t in range(T1 + TICKS1):
                for k in range(3):
                    run(t, k)

        @block.tensor
        def _(pe):
            mm, turn = nc.tensor.matmul, nc.tensor.transpose

            def tiles(g, dst, lhsT, rhs, shared=False):
                for b in range(N[g]):
                    c = slice(b * P, (b + 1) * P)
                    m = mm(dst[:, c], lhsT[:, c], rhs if shared else rhs[:, c], start=True, stop=True)
                return m

            def project(p, i):
                w, slot = i // 4, i % 2
                at = i % 8 if p == 0 else slot
                if p == 0:
                    pe.wait_ge(s("hi"), 2 + i // 2)
                    pe.wait_ge(s("lo"), 2 + i // 2)
                    if i >= 8:
                        pe.wait_ge(s("qk_lo"), i - 7)
                elif p > 1 or i >= 2:
                    pe.wait_ge(pj_free[slot], 10 * (p - 1) + i // 2)
                for gi in range(2):
                    g = slice((2 * (i % 4) + gi) * P, (2 * (i % 4) + gi + 1) * P)
                    dst = bank(at)[:, gi * TP:(gi + 1) * TP]
                    x = slice(p * TP, (p + 1) * TP)
                    mm(dst, w0l[:, w, g], xh[:, x], start=True, stop=False)
                    mm(dst, w0h[:, w, g], xl[:, x], start=False, stop=False)
                    m = mm(dst, w0h[:, w, g], xh[:, x], start=False, stop=True)
                m.then_inc(s("proj_done"), 1)

            def turn_v(p, q):
                i = NPROJ + q
                at = 4 + q % 4 if p == 0 else i % 2
                if p:
                    pe.wait_ge(pj_free[i % 2], 10 * (p - 1) + i // 2)
                elif q < 4:
                    pe.wait_ge(s("qk_lo"), 5 + q)
                else:
                    pe.wait_ge(s("v_in"), q - 3)
                if q == 0:
                    pe.wait_ge(*((pj_free[1], 10 * (p - 1) + 6) if p else (s("vn_in"), 4)))
                for h in range(4):
                    m = turn(bank(at)[0:64, h * P:(h + 1) * P],
                             VN[:, (4 * q + h) * 64:(4 * q + h + 1) * 64], ident[:])
                m.then_inc(s("proj_done"), 1)

            def scores_q(Q):
                p, q = Q // QP, Q % QP
                if q == 0:
                    pe.wait_ge(qk_in[p % 2], 32 * (p // 2 + 1))
                if Q >= 2:
                    pe.wait_ge(s("max_done"), Q if Q > AHEAD - 1 else Q - 1)
                for h in range(4):
                    n, dst = 4 * q + h, bank(quad_bank(Q))[:, h * P:(h + 1) * P]
                    mm(dst, head(QB[p % 2], n), head(KA[p % 2], n), start=True, stop=False)
                    m = mm(dst, head(QA[p % 2], n), head(KA[p % 2], n), start=False, stop=True)
                m.then_inc(s("sq_done"), 1)

            def scores_k(Q):
                p, q, b = Q // QP, Q % QP, Q // 4
                if Q:
                    pe.wait_ge(s("exp_done"), Q)
                else:
                    pe.wait_ge(s("max_done"), 4)
                pe.wait_ge(s("turn_free"), z_max(b) + 1)
                for h in range(4):
                    n, dst = 4 * q + h, bank(3)[:, h * P:(h + 1) * P]
                    mm(dst, head(KA[p % 2], n), head(QB[p % 2], n), start=True, stop=False)
                    mm(dst, head(KA[p % 2], n), head(QA[p % 2], n), start=False, stop=False)
                    m = mm(dst, En[:, n % H, :], MR[:, b % 2, :], start=False, stop=True)
                m.then_inc(s("sk_done"), 1)

            def weigh(Q):
                p, q = Q // QP, Q % QP
                pe.wait_ge(s("exp_done"), Q + 1)
                pe.wait_ge(*v_there(p, q))
                if Q:
                    pe.wait_ge(s("norm_done"), Q)
                for h in range(4):
                    m = mm(bank(4)[:, h * VW:(h + 1) * VW], PT[:, Q % SLOTS_PT, h * P:(h + 1) * P],
                           V[:, p % 2, 4 * q + h, :], start=True, stop=True)
                m.then_inc(s("pv_done"), 1)

            def turn_max(b):
                z = z_max(b)
                if z:
                    pe.wait_ge(s("turn_free"), z)
                else:
                    pe.wait_ge(s("v_in"), 8)
                pe.wait_ge(s("max_done"), 4 * b + 4)
                turn(bank(5)[0:H, 0:P], rowmax[:, b * H:(b + 1) * H], ident[:]).then_inc(s("turn_done"), 1)

            def turn_out(o):
                pe.wait_ge(s("turn_free"), z_out(o))
                pe.wait_ge(s("norm_done"), 2 * o + 2)
                for r in range(4):
                    n = 8 * (o % 4) + 2 * r
                    m = turn(bank(5)[:, r * P:(r + 1) * P], On[:, n:n + 2, :], ident[:])
                m.then_inc(s("turn_done"), 1)

            def project_out(b):
                pe.wait_ge(s("turn_free"), z_y(b))
                if b == 0:
                    pe.wait_ge(s("ld_wo"), 32)
                for g in range(G):
                    m = mm(bank(5)[:, 0:P], OT[:, b % 2, g, :], wo[:, g, :], start=(g == 0), stop=(g == G - 1))
                m.then_inc(s("turn_done"), 1)

            def project_next(t, k):
                for p, i in next_projection(t, k):
                    if i < NPROJ:
                        project(p, i)
                    else:
                        turn_v(p, i - NPROJ)

            def turn_x(g, k, at):
                for b in range(N[g]):
                    pe.wait_ge(*normalised(g, k, b))
                    m = turn(bank(at)[:, b * P:(b + 1) * P], xt[:, B0[g] + b, :], ident[:])
                m.then_inc(s(f"pe_x{g}"), 1)
                return

            def mid(g, i):
                if i == 0:
                    if g == 0:
                        pe.wait_ge(s("ld_ctx"), 16 * 12)
                    else:
                        pe.wait_ge(s(f"qp_lo{g - 1}"), 1)
                        pe.wait_ge(s(f"ve_done{g - 1}"), 1)
                    mm(part_of(bank(6), g), wx0[:, 1, :], tokens(cT, g), start=True, stop=True).then_inc(s("pe_kx0"), 1)
                    tiles(g, part_of(bank(7), g), tokens(cT, g), wx0[:, 2, :], True).then_inc(s("pe_vx0"), 1)
                if i == 3:
                    pe.wait_ge(s("kx0"), g + 1)
                    turn_x(g, 0, 6)
                if i == 4:
                    pe.wait_ge(s("vx0"), g + 1)
                    pe.wait_ge(s(f"xT{g}"), 1)
                    mm(part_of(bank(7), g), wx0[:, 0, :], tokens(xT, g), start=True, stop=True).then_inc(s("pe_q0"), 1)
                if i == 5:
                    pe.wait_ge(s("q0"), g + 1)
                    tiles(g, part_of(bank(6), g), part_of(mA, g), part_of(kx0, g)).then_inc(s("pe_s0"), 1)
                if i == 7:
                    pe.wait_ge(s("exp0"), g + 1)
                    for b in range(N[g]):
                        m = turn(part_of(bank(7), g)[:, b * P:(b + 1) * P], mC[:, b * P:(b + 1) * P], ident[:])
                    m.then_inc(s("pe_p0"), 1)
                if i == 8:
                    pe.wait_ge(s("p0T"), g + 1)
                    tiles(g, part_of(bank(6), g), part_of(mA, g), part_of(vx0, g)).then_inc(s("pe_o0"), 1)
                if i == 12:
                    turn_x(g, 1, 7)
                if i == 13:
                    pe.wait_ge(s(f"xT{g}"), 2)
                    if g == 0:
                        pe.wait_ge(s("ld_mid"), 160)
                    for b in range(N[g]):
                        m = mm(bank(6 + b // 2)[:, (b % 2) * 256:(b % 2) * 256 + P + NE],
                               tokens(xT, g)[:, b * P:(b + 1) * P], wge_s[:], start=True, stop=True)
                    m.then_inc(s("pe_ffn"), 1)
                if i == 18:
                    turn_x(g, 2, 6)
                if i == 19:
                    pe.wait_ge(s(f"xT{g}"), 3)
                    mm(part_of(bank(7), g), w1[:, 1, :], tokens(xT, g), start=True, stop=True).then_inc(s("pe_k1a"), 1)
                if i == 20:
                    mm(part_of(bank(6), g), w1[:, 0, :], tokens(xT, g), start=True, stop=True).then_inc(s("pe_q1a"), 1)
                if i == 21:
                    pe.wait_ge(s(f"kp_lo{g}"), 1)
                    tiles(g, part_of(bank(7), g), tokens(xT, g), w1[:, 2, :], True).then_inc(s("pe_v1a"), 1)

            def scores1(w, b, q, of_keys):
                if w >= 3:
                    pe.wait_ge(s1_free[w % 3], w // 3)
                else:
                    pe.wait_ge(s("max_done"), NQ)
                g = GROUP[b]
                pe.wait_ge(s(f"stack_in{g}"), 128)
                if of_keys:
                    pe.wait_ge(s("mr1_done"), b + 1)
                t = slice((b - B0[g]) * P, (b - B0[g] + 1) * P)
                K, Q, dst = Kst[g], Qst[g], bank(w % 3)
                mm(dst, ident_b[:], (maskk if of_keys else maskq)[:].unsqueeze(1).broadcast_to([P, 4, P]),
                   start=True, stop=False)
                for h in range(4):
                    n, part_ = 4 * q + h, dst[:, h * P:(h + 1) * P]
                    if of_keys:
                        mm(part_, K[:, n, t], Q[:, n, t], start=False, stop=False)
                        m = mm(part_, En[:, n, :], MR[:, b % 2, :], start=False, stop=(h == 3))
                    else:
                        m = mm(part_, Q[:, n, t], K[:, n, t], start=False, stop=(h == 3))
                m.then_inc(s("scores1_done"), 1)

            def weigh1(b, q):
                v, w = 4 * b + q, k_use[b, q]
                pe.wait_ge(s1_free[w % 3], w // 3 + 1)
                if q == 0:
                    pe.wait_ge(s(f"ve_done{GROUP[b]}"), 1)
                    if b:
                        pe.wait_ge(s("o1_out"), b)
                for r in range(4):
                    g = GROUP[b]
                    n = (b - B0[g]) * H + 4 * q + r
                    m = mm(bank(3)[32 * r:32 * r + 32, q * P:(q + 1) * P], VE[g][:, 32 * n:32 * n + 32],
                           PT[:, v % SLOTS_PT, r * P:(r + 1) * P], start=True, stop=True)
                m.then_inc(s("pv1_done"), 1)

            def scores(u):
                for b in range(NB):
                    if 0 <= u - u1(b) < 4:
                        scores1(q_use[b, u - u1(b)], b, u - u1(b), False)
                    if u - u1(b) == 4:
                        w = q_use[b, 3]
                        pe.wait_ge(s1_free[w % 3], w // 3 + 1)
                        for at, read in ((10, "on1_done"), (11, "onT1_done"), (12, "res1_done")):
                            outs = len([c for c in range(NB) if u1(c) + at < u])
                            if outs:
                                pe.wait_ge(s(read), outs)
                        if b:
                            pe.wait_ge(s("mr1_done"), b)
                        turn(bank(4)[0:H, 0:P], rowmax[:, b * H:(b + 1) * H], ident[:])\
                            .then_inc(s("pe_mt1"), 1)
                for b in range(NB):
                    if 5 <= u - u1(b) < 9:
                        scores1(k_use[b, u - u1(b) - 5], b, u - u1(b) - 5, True)

            def outputs(u):
                for b in range(NB):
                    if 6 <= u - u1(b) < 10:
                        weigh1(b, u - u1(b) - 6)
                for b in range(NB):
                    steps = out_step(b, u)
                    if steps:
                        pe.wait_ge(s("mr1_done"), len([c for c in range(NB) if u1(c) + 4 <= u]))
                    if 0 in steps:
                        pe.wait_ge(s("o1_out"), b + 1)
                        if b:
                            pe.wait_ge(s("res1_done"), b)
                        for q in range(4):
                            m = turn(bank(4)[:, q * P:(q + 1) * P], o1[:, b % 2, q * P:(q + 1) * P], ident[:])
                        m.then_inc(s("pe_ot1"), 1)
                    if 1 in steps:
                        pe.wait_ge(s("on1_done"), b + 1)
                        turn(bank(4)[:, 0:P], On1, ident[:]).then_inc(s("pe_on1"), 1)
                    if 2 in steps:
                        pe.wait_ge(s("onT1_done"), b + 1)
                        mm(bank(4)[:, P:2 * P], OnT1, wp1_s[:], start=True, stop=True).then_inc(s("pe_y1"), 1)

            def late(g, i):
                if i == 0:
                    if g == LATES[0]:
                        pe.wait_ge(s("turn_free"), 8 * NPAIR)
                        pe.wait_ge(s("qp_lo2"), 1)
                        pe.wait_ge(s("ve_done2"), 1)
                    else:
                        pe.wait_ge(s("res1_done"), NB)
                    mm(part_of(bank(LBANKS[g][1]), g), wx1[:, 2, :], tokens(cT, g), start=True, stop=True)
                    mm(part_of(bank(LBANKS[g][2]), g), wx1[:, 3, :], tokens(cT, g), start=True, stop=True).then_inc(s("pe_k1"), 1)
                    tiles(g, part_of(bank(LBANKS[g][0]), g), tokens(cT, g), wx1[:, 4, :], True).then_inc(s("pe_vx1"), 1)
                if i == 3:
                    pe.wait_ge(s("vx1"), g - 2)
                    turn_x(g, 0, LBANKS[g][0])
                if i == 4:
                    pe.wait_ge(s("k1_mul"), g - 2)
                    pe.wait_ge(s(f"xT{g}"), 1)
                    mm(part_of(bank(LBANKS[g][1]), g), wx1[:, 0, :], tokens(xT, g), start=True, stop=True)
                    mm(part_of(bank(LBANKS[g][2]), g), wx1[:, 1, :], tokens(xT, g), start=True, stop=True).then_inc(s("pe_q"), 1)
                if i == 6:
                    pe.wait_ge(s("k1_rot"), g - 2)
                    pe.wait_ge(s("q_rot"), g - 2)
                    tiles(g, part_of(bank(LBANKS[g][0]), g), part_of(kx1[g], g), part_of(lA[g], g)).then_inc(s("pe_sx1"), 1)
                if i == 7:
                    pe.wait_ge(s("sx1"), g - 2)
                    tiles(g, part_of(bank(LBANKS[g][1]), g), part_of(lD[g], g), part_of(vx1[g], g)).then_inc(s("pe_ox1"), 1)
                if i == 11:
                    pe.wait_ge(s("x5q"), g - 2)
                    for b in range(N[g]):
                        c = slice(b * P, (b + 1) * P)
                        m = turn(bank(LBANKS[g][0]).bitcast(BF16)[:, c], x5q[g][:, c], ident_b[:])
                    m.then_inc(s("pe_x5T"), 1)
                if 12 <= i <= 12 + 2 * N[g] and i % 2 == 0:
                    j = i // 2 - 6
                    if j == 0:
                        pe.wait_ge(s("x5T"), g - 2)
                        pe.wait_ge(s("w_int"), 3)
                    for b in gates_at(g, j):
                        before = [c for c in range(b) if gate_bank(c) == gate_bank(b)]
                        if before:
                            pe.wait_ge(s("h_done"), before[-1] + 1)
                        for k in range(2):
                            m = mm(bank(gate_bank(b) + k), x5T[g][:, (b - B0[g]) * P:(b - B0[g] + 1) * P],
                                   wgu_i[:, k * INNER:(k + 1) * INNER], start=True, stop=True)
                        m.then_inc(s("pe_gu"), 1)
                    if j:
                        down(B0[g] + j - 1)

            def down(b):
                g = LATES[b >= B0[-1]]
                pe.wait_ge(s("h_int"), b + 1)
                if b:
                    pe.wait_ge(s("res_f1"), b)
                for c in range(4):
                    m = turn(bank(down_bank(b)).bitcast(BF16)[:, c * P:(c + 1) * P],
                             hi[g][:, b % 2, c * P:(c + 1) * P], ident_b[:])
                m.then_inc(s("pe_hT"), 1)
                pe.wait_ge(s("hT"), b + 1)
                for c in range(4):
                    m = mm(bank(down_bank(b))[:, 0:P], hT[g][:, b % 2, c * P:(c + 1) * P],
                           wdn_i[:, c * P:(c + 1) * P], start=(c == 0), stop=(c == 3))
                m.then_inc(s("pe_down"), 1)

            def run(t, k):
                for kind, g, i in TICKS.get((t, k), ()):
                    (mid if kind == "mid" else late)(g, i)

            for i in range(NPROJ):
                project(0, i)
            pe.wait_ge(s("ident_set"), 1)
            for q in range(4):
                turn_v(0, q)
            pe.wait_ge(s("vn_in"), 4)
            for Q in range(AHEAD):
                scores_q(Q)
                if Q < 4:
                    turn_v(0, 4 + Q)
            pe.wait_ge(s("setup"), 1)
            turn_max(0)
            for t in range(TICKS0):
                project_next(t, 0)
                if t < NQ:
                    scores_k(t)
                if t % 4 == 3 and t < NQ - 1:
                    turn_max(t // 4 + 1)
                project_next(t, 1)
                if t == 1:
                    pe.wait_ge(s("w_abs"), 1)
                    pe.wait_ge(s("masks"), 1)
                    mm(bank(6)[:, 0:3], ones[:], wabs[:, 0:3], start=True, stop=True)\
                        .then_inc(s("pe_wsum"), 1)
                run(t, 0)
                if 1 <= t <= NQ:
                    weigh(t - 1)
                project_next(t, 2)
                run(t, 1)
                if t % 2 and t >= 3:
                    turn_out((t - 3) // 2)
                if t + AHEAD < NQ:
                    scores_q(t + AHEAD)
                if t % 4 == 2 and t >= 6:
                    project_out((t - 6) // 4)
                run(t, 2)
                if t >= T1:
                    scores(t - T1)
                    outputs(t - T1)
            for u in range(TICKS0 - T1, TICKS1):
                run(T1 + u, 0)
                scores(u)
                run(T1 + u, 1)
                outputs(u)
                run(T1 + u, 2)

        @block.scalar
        def _(act):
            fn = nc.scalar.activation

            act.wait_ge(s("ld_x"), 16)
            fn(xh[:], xT[:], ACT.Copy).then_inc(s("hi"), 1)
            for w in range(3):
                for j in range(2):
                    act.wait_ge(s(("ld_wk", "ld_wq", "ld_wv")[w] + str(j)), 16)
                    cols = slice(512 * j, 512 * j + 512)
                    fn(w0h[:, w, cols], w0[:, w, cols], ACT.Copy).then_inc(s("hi"), 1)

            def by_head(buf, i):
                return buf.rearrange("p (n g t) -> p g n t", g=G, t=8)[:, 2 * (i % 4):2 * (i % 4) + 2, :, :]

            def empty_projection(p, i):
                at = i % 8 if p == 0 else i % 2
                src = bank(at).rearrange("p (g n t) -> p g n t", g=2, t=8)
                act.wait_ge(s("proj_done"), 20 * p + i + 1)
                if i < 8:
                    if p >= 2:
                        act.wait_ge(s("sk_done"), QP * (p - 1))
                    dst = by_column((KA, QA)[i // 4][p % 2][0:64, :], i)
                    for a in range(2):
                        m = fn(dst[:, a], src[a * 64:(a + 1) * 64], ACT.Copy)
                    m.then_inc(s("qk_hi"), 1)
                else:
                    fn(by_head(VN[:], i), src, ACT.Copy).then_inc(s("vn_in") if p == 0 else pj_free[i % 2], 1)

            def empty_turned_v(p, q):
                i = NPROJ + q
                at = 4 + q % 4 if p == 0 else i % 2
                act.wait_ge(s("proj_done"), 20 * p + i + 1)
                if q == 0 and p >= 2:
                    act.wait_ge(s("pv_done"), QP * (p - 1))
                src = bank(at)[0:64, :].rearrange("p (n a d) -> p n a d", n=4, a=2)
                for a in range(2):
                    m = fn(V[a * 64:(a + 1) * 64, p % 2, 4 * q:4 * q + 4, 0:DH0], src[:, :, a, :], ACT.Copy)
                m.then_inc(pj_free[i % 2] if p else s("v_in"), 1)

            def exp0(Q):
                act.wait_ge(s("sk_done"), Q + 1)
                if Q >= SLOTS_PT:
                    act.wait_ge(s("pv_done"), Q - SLOTS_PT + 1)
                fn(PT[:, Q % SLOTS_PT, :], bank(3), ACT.Exp, scale=SCALE0).then_inc(s("exp_done"), 1)

            def empty_next(t, k):
                for p, i in next_projection(t, k):
                    if i < NPROJ:
                        empty_projection(p, i)
                    else:
                        empty_turned_v(p, i - NPROJ)

            def normalise(g, k):
                act.wait_ge(s(f"rstd{g}"), k + 1)
                for b in range(B0[g], B0[g] + (2 if g == LATES[-1] else N[g])):
                    fn(xt[:, b, :], res[:, b, :], ACT.Identity, bias=shift[:, b:b + 1],
                       scale=rstd[:, b:b + 1]).then_inc(s(f"xn{g}"), 1)

            def copy_x(g, k, at):
                act.wait_ge(s(f"pe_x{g}"), k + 1)
                fn(tokens(xT, g), part_of(bank(at), g), ACT.Copy).then_inc(s(f"xT{g}"), 1)

            def mid(g, i):
                if i == 0:
                    act.wait_ge(s("pe_kx0"), g + 1)
                    fn(part_of(kx0, g), part_of(bank(6), g), ACT.Identity, bias=bx0[:, 1:2]).then_inc(s("kx0"), 1)
                    act.wait_ge(s("pe_vx0"), g + 1)
                    fn(part_of(vx0, g), part_of(bank(7), g), ACT.Copy).then_inc(s("vx0"), 1)
                if i == 2:
                    normalise(g, 0)
                if i == 3:
                    copy_x(g, 0, 6)
                if i == 4:
                    act.wait_ge(s("pe_q0"), g + 1)
                    fn(part_of(mA, g), part_of(bank(7), g), ACT.Identity, bias=bx0[:, 0:1]).then_inc(s("q0"), 1)
                if i == 6:
                    act.wait_ge(s("sub0"), g + 1)
                    fn(part_of(mC, g), part_of(mC, g), ACT.Exp, scale=SCALEX).then_inc(s("exp0"), 1)
                if i == 7:
                    act.wait_ge(s("pe_p0"), g + 1)
                    fn(part_of(mA, g), part_of(bank(7), g), ACT.Copy).then_inc(s("p0T"), 1)
                if i == 11:
                    normalise(g, 1)
                if i == 12:
                    copy_x(g, 1, 7)
                if i == 14:
                    act.wait_ge(s("gate_sub"), g + 1)
                    fn(batches(lgt, g), batches(lgt, g), ACT.Exp).then_inc(s("gate_exp"), 1)
                if i == 17:
                    normalise(g, 2)
                if i == 18:
                    copy_x(g, 2, 6)
                if i == 19:
                    act.wait_ge(s("pe_k1a"), g + 1)
                    fn(tokens(kph, g), part_of(bank(7), g), ACT.Identity, bias=b1[:, 1:2]).then_inc(s(f"kp_hi{g}"), 1)
                if i == 20:
                    act.wait_ge(s("pe_q1a"), g + 1)
                    fn(tokens(qph, g), part_of(bank(6), g), ACT.Identity, bias=b1[:, 0:1]).then_inc(s(f"qp_hi{g}"), 1)

            def scores(u):
                for b in range(NB):
                    if 5 <= u - u1(b) < 9:
                        q = u - u1(b) - 5
                        v, w = 4 * b + q, k_use[b, q]
                        act.wait_ge(s("scores1_done"), w + 1)
                        if v >= SLOTS_PT:
                            act.wait_ge(s("pv1_done"), v - SLOTS_PT + 1)
                        fn(PT[:, v % SLOTS_PT, :], bank(w % 3), ACT.Exp, scale=SCALE1)\
                            .then_inc(s1_free[w % 3], 1)

            def outputs(u):
                for b in range(NB):
                    if 1 in out_step(b, u):
                        act.wait_ge(s("pe_on1"), b + 1)
                        fn(OnT1, bank(4)[:, 0:P], ACT.Copy).then_inc(s("onT1_done"), 1)
                    if u - u1(b) == 9:
                        act.wait_ge(s("pv1_done"), 4 * b + 4)
                        if b >= 2:
                            act.wait_ge(s("pe_ot1"), b - 1)
                        fn(o1[:, b % 2, :], bank(3), ACT.Copy).then_inc(s("o1_out"), 1)

            def late(g, i):
                if i == 0:
                    act.wait_ge(s("pe_vx1"), g - 2)
                    fn(part_of(vx1[g], g), part_of(bank(LBANKS[g][0]), g), ACT.Copy).then_inc(s("vx1"), 1)
                if i == 2:
                    normalise(g, 0)
                if i == 3:
                    copy_x(g, 0, LBANKS[g][0])
                if i == 9:
                    normalise(g, 1)
                if i == 11:
                    act.wait_ge(s("pe_x5T"), g - 2)
                    fn(part_of(x5T[g], g), bank(LBANKS[g][0]).bitcast(BF16)[:, 0:N[g] * P], ACT.Copy).then_inc(s("x5T"), 1)
                if 12 <= i <= 12 + 2 * N[g] and i % 2 == 0:
                    j = i // 2 - 6
                    if j == 0:
                        act.wait_ge(s("gu_scale"), g - 2)
                    for b in gates_at(g, j):
                        act.wait_ge(s("pe_gu"), b + 1)
                        if b >= 2:
                            act.wait_ge(s("h_done"), b - 1)
                        fn(th[g][:, b % 2, :], bank(gate_bank(b)), ACT.Silu if g == LATES[-1] else ACT.Tanh,
                           scale=sm8[:, 4, b:b + 1])\
                            .then_inc(s("tanh"), 1)
                    if j:
                        b = B0[g] + j - 1
                        act.wait_ge(s("pe_hT"), b + 1)
                        if b >= 2:
                            act.wait_ge(s("pe_down"), b - 1)
                        fn(hT[g][:, b % 2, :], bank(LBANKS[g][0]).bitcast(BF16)[:, 0:INNER], ACT.Copy).then_inc(s("hT"), 1)
                if 13 <= i < 12 + 2 * N[g] and i % 2:
                    b = B0[g] + (i - 13) // 2
                    act.wait_ge(s("h_scale"), b + 1)
                    fn(hb[g][:, b % 2, :], hb[g][:, b % 2, :], ACT.Copy, bias=MAGIC,
                       scale=hs[:, 2 * (g - 3) + b % 2, 2:3]).then_inc(s("h_round"), 1)
                if i == 15 + 2 * N[g]:
                    normalise(g, 2)

            def run(t, k):
                for kind, g, i in TICKS.get((t, k), ()):
                    (mid if kind == "mid" else late)(g, i)

            for i in range(NPROJ):
                empty_projection(0, i)
            act.wait_ge(s("v_ones"), 1)
            for q in range(QP):
                empty_turned_v(0, q)
            for t in range(TICKS0):
                empty_next(t, 0)
                if t < NQ:
                    exp0(t)
                empty_next(t, 1)
                run(t, 0)
                empty_next(t, 2)
                run(t, 1)
                run(t, 2)
                if t >= T1:
                    scores(t - T1)
                    outputs(t - T1)
            for u in range(TICKS0 - T1, TICKS1):
                run(T1 + u, 0)
                scores(u)
                run(T1 + u, 1)
                outputs(u)
                run(T1 + u, 2)

        @block.vector
        def _(dve):
            step = [0]
            V_ = nc.vector
            tt, ts, stt = V_.tensor_tensor, V_.tensor_scalar, V_.scalar_tensor_tensor

            def link(ins):
                step[0] += 1
                ins.then_inc(s("dve_step"), 1)
                dve.wait_ge(s("dve_step"), step[0])

            def over(x, n, width):
                return x.unsqueeze(1).broadcast_to([P, n, width])

            def across(x, n, width):
                return x.unsqueeze(2).broadcast_to([P, n, width])

            dve.wait_ge(s("hi"), 1)
            tt(xl[:], xT[:], xh[:].bitcast(F32), ALU.subtract).then_inc(s("lo"), 1)
            for w in range(3):
                for j in range(2):
                    cols = slice(512 * j, 512 * j + 512)
                    dve.wait_ge(s("hi"), 2 * w + j + 2)
                    tt(w0l[:, w, cols], w0[:, w, cols], w0h[:, w, cols].bitcast(F32), ALU.subtract)\
                        .then_inc(s("lo"), 1)

            def lower_parts(p, i):
                at = i % 8 if p == 0 else i % 2
                src = bank(at).rearrange("p (g n t) -> p g n t", g=2, t=8)
                dve.wait_ge(s("qk_hi"), 8 * p + i + 1)
                upper = by_column((KA, QA)[i // 4][p % 2][0:64, :], i)
                lower = by_column((KA[p % 2][64:P, :], QB[p % 2][0:64, :])[i // 4], i)
                for a in range(2):
                    m = tt(lower[:, a], src[a * 64:(a + 1) * 64], upper[:, a], ALU.subtract)
                m.then_inc(s("qk_lo") if p == 0 else pj_free[i % 2], 1)

            def maxima(Q):
                dve.wait_ge(s("sq_done"), Q + 1)
                V_.reduce_max(rowmax[:, 4 * Q:4 * Q + 4], tok(bank(quad_bank(Q))), AX_X)\
                    .then_inc(s("max_done"), 1)

            def negated_maxima(event, count, src, b, done):
                dve.wait_ge(s(event), count)
                link(ts(MR[0:H, b % 2, :], src[0:H, 0:P], -1.0, None, ALU.mult))
                stt(MR[32:32 + H, b % 2, :], src[0:H, 0:P], -1.0, MR[0:H, b % 2, :],
                    ALU.mult, ALU.subtract).then_inc(s(done), 1)

            def max_rows(b):
                if b == 0:
                    dve.wait_ge(s("setup"), 1)
                if b >= 2:
                    dve.wait_ge(s("sk_done"), 4 * (b - 1))
                negated_maxima("turn_done", z_max(b) + 1, bank(5), b, "turn_free")

            def normalize(Q):
                n = 4 * (Q % QP)
                o = bank(4)[:, 0:4 * VW].rearrange("p (n d) -> p n d", n=4)
                dve.wait_ge(s("pv_done"), Q + 1)
                if Q >= QP:
                    dve.wait_ge(s("turn_done"), z_out((Q - QP) // 2) + 1)
                link(V_.reciprocal(rec[:, Q % 2, 0:4], o[:, :, DH0]))
                tt(On[:, n:n + 4, :], o[:, :, 0:DH0], across(rec[:, Q % 2, 0:4], 4, DH0), ALU.mult)\
                    .then_inc(s("norm_done"), 1)

            def place_out(o):
                b = o // 2
                dve.wait_ge(s("turn_done"), z_out(o) + 1)
                src = bank(5).rearrange("p (r a g t) -> p r a g t", r=4, a=2, g=G)
                dst = OT[:, b % 2, :, :].rearrange("p g (m h t) -> p h m g t", h=2, t=8)
                if b >= 2 and o % 2 == 0:
                    dve.wait_ge(s("turn_done"), z_y(b - 2) + 1)
                for h in range(2):
                    for a in range(2):
                        m = V_.tensor_copy(dst[a * 64:(a + 1) * 64, h, 4 * (o % 2):4 * (o % 2) + 4],
                                           src[h * 64:(h + 1) * 64, :, a])
                m.then_inc(s("turn_free"), 1)

            def add_out(b):
                if b == 0:
                    dve.wait_ge(s("ld_wo"), 32)
                dve.wait_ge(s("turn_done"), z_y(b) + 1)
                tt(res[:, b, :], bank(5)[:, 0:P], xt[:, b, :], ALU.add).then_inc(s("turn_free"), 1)

            def lower_next(t, k):
                for p, i in next_projection(t, k):
                    if i < 8:
                        lower_parts(p, i)

            def moments(g, *last):
                if last:
                    dve.wait_ge(*last)
                for b in range(B0[g], B0[g] + N[g]):
                    m = V_.bn_stats(stats[:, b, :], res[:, b, :])
                link(m)
                for b in range(B0[g], B0[g] + N[g]):
                    m = V_.bn_aggr(mv[:, b, :], stats[:, b, :])
                if g in ON_POOL:
                    m.then_inc(s(f"moments{g}"), 1)
                    return
                link(m)
                v, y, e = (nwt[:, i, B0[g]:B0[g] + N[g]] for i in range(3))
                r = batches(rstd, g)
                link(ts(v, batches(mv, g)[:, :, 1], EPS, 0.5, ALU.add, ALU.mult))
                link(ts(y.bitcast(I32), v.bitcast(I32), -0.5, RSQRT_BITS - 2 ** 22, ALU.mult, ALU.add))
                for i in range(3):
                    link(stt(e, y, -1.0, y, ALU.mult, ALU.mult))
                    link(tt(e, e, v, ALU.mult))
                    link(stt(r if i == 2 else y, e, 1.5, y, ALU.add, ALU.mult))
                stt(batches(shift, g), batches(mv, g)[:, :, 0], -1.0, r, ALU.mult, ALU.mult)\
                    .then_inc(s(f"rstd{g}"), 1)
                if g == LATES[-1]:

                    for b in range(B0[g] + 2, B0[g] + 4):
                        ts(xt[:, b, :], res[:, b, :], mv[:, b, 0:1], rstd[:, b:b + 1], ALU.subtract, ALU.mult)\
                            .then_inc(s("xn4_dve"), 1)

            def mid(g, i):
                hb4 = slice(B0[g], B0[g] + N[g])
                if i == 0:
                    moments(g, s("turn_free"), z_y(LAST[g]) + 1)
                if i == 5:
                    dve.wait_ge(s("pe_s0"), g + 1)
                    link(V_.reduce_max(sm8[:, 0, hb4], tok(part_of(bank(6), g), N[g]), AX_X))
                    tt(tok(part_of(mC, g), N[g]), tok(part_of(bank(6), g), N[g]), across(sm8[:, 0, hb4], N[g], P), ALU.subtract).then_inc(s("sub0"), 1)
                if i == 7:
                    dve.wait_ge(s("exp0"), g + 1)
                    link(V_.reduce_sum(sm8[:, 1, hb4], tok(part_of(mC, g), N[g]), AX_X))
                    link(V_.reciprocal(sm8[:, 2, hb4], sm8[:, 1, hb4]))
                if i == 8:
                    dve.wait_ge(s(f"x1b{g}"), 1)
                    dve.wait_ge(s("pe_o0"), g + 1)
                    for j in range(N[g]):
                        b = B0[g] + j
                        m = stt(res[:, b, :], part_of(bank(6), g)[:, j * P:(j + 1) * P], sm8[:, 2, b:b + 1],
                                tB[:, b * P:(b + 1) * P], ALU.mult, ALU.add)
                    link(m)
                if i == 9:
                    moments(g)
                if i == 13:
                    if g == 0:
                        dve.wait_ge(s("ld_mid"), 160)
                    dve.wait_ge(s("pe_ffn"), g + 1)
                    ge = PS[:, 6:8, :].rearrange("p k (i c) -> p (k i) c", i=2)[:, 0:N[g]]
                    l4 = batches(lgt, g)
                    link(tt(l4, ge[:, :, P:P + NE], over(bge_s[:, P:P + NE], N[g], NE), ALU.add))
                    link(V_.reduce_max(sm8[:, 0, hb4], l4, AX_X))
                    tt(l4, l4, across(sm8[:, 0, hb4], N[g], NE), ALU.subtract).then_inc(s("gate_sub"), 1)
                    tt(tok(part_of(mC, g), N[g]), ge[:, :, 0:P], over(bge_s[:, 0:P], N[g], P), ALU.add)
                if i == 15:
                    dve.wait_ge(s("gate_exp"), g + 1)
                    link(V_.reduce_sum(sm8[:, 1, hb4], batches(lgt, g), AX_X))
                    link(V_.reciprocal(sm8[:, 2, hb4], sm8[:, 1, hb4]))
                    for j in range(N[g]):
                        b = B0[g] + j
                        m = stt(res[:, b, :], mC[:, j * P:(j + 1) * P], sm8[:, 2, b:b + 1], xt[:, b, :],
                                ALU.mult, ALU.add)
                    link(m)
                    moments(g)
                if i == 19:
                    dve.wait_ge(s(f"kp_hi{g}"), 1)
                    stt(tokens(kpl, g), part_of(bank(7), g), b1[:, 1:2], tokens(kph, g), ALU.add, ALU.subtract)\
                        .then_inc(s(f"kp_lo{g}"), 1)
                if i == 20:
                    dve.wait_ge(s(f"qp_hi{g}"), 1)
                    stt(tokens(qpl, g), part_of(bank(6), g), b1[:, 0:1], tokens(qph, g), ALU.add, ALU.subtract)\
                        .then_inc(s(f"qp_lo{g}"), 1)
                if i == 21:
                    dve.wait_ge(s("ve_ones"), 1)
                    dve.wait_ge(s("pe_v1a"), g + 1)
                    tt(VE[g].rearrange("p (b n c) -> p b n c", b=N[g], n=H)[:, :, :, 0:DH1],
                       part_of(bank(7), g).rearrange("p (b n c) -> p b n c", b=N[g], n=H),
                       bv1_s[:].rearrange("p (n c) -> p n c", n=H).unsqueeze(1).broadcast_to([P, N[g], H, DH1]),
                       ALU.add).then_inc(s(f"ve_done{g}"), 1)

            def scores(u):
                for b in range(NB):
                    if 0 <= u - u1(b) < 4:
                        q = u - u1(b)
                        w = q_use[b, q]
                        dve.wait_ge(s("scores1_done"), w + 1)
                        V_.reduce_max(rowmax[:, b * H + 4 * q:b * H + 4 * q + 4], tok(bank(w % 3)), AX_X)\
                            .then_inc(s1_free[w % 3], 1)
                    if u - u1(b) == 4:
                        if b >= 2:
                            dve.wait_ge(s("scores1_done"), k_use[b - 2, 3] + 1)
                        negated_maxima("pe_mt1", b + 1, bank(4), b, "mr1_done")

            def outputs(u):
                for b in range(NB):
                    if 0 in out_step(b, u):
                        o = bank(4).rearrange("p (n c) -> p n c", n=H)
                        dve.wait_ge(s("pe_ot1"), b + 1)
                        link(V_.reciprocal(rec[:, b % 2, :], o[:, :, DH1]))
                        if b:
                            dve.wait_ge(s("pe_on1"), b)
                        tt(On1.rearrange("p (n c) -> p n c", n=H), o[:, :, 0:DH1],
                           across(rec[:, b % 2, :], H, DH1), ALU.mult).then_inc(s("on1_done"), 1)
                    if 2 in out_step(b, u):
                        dve.wait_ge(s(f"x3b{GROUP[b]}"), 1)
                        dve.wait_ge(s("pe_y1"), b + 1)
                        tt(res[:, b, :], bank(4)[:, P:2 * P], tB[:, b * P:(b + 1) * P], ALU.add)\
                            .then_inc(s("res1_done"), 1)

            def hidden_product(b):
                g = LATES[b >= B0[-1]]
                h, sc = hb[g][:, b % 2, :], hs[:, 2 * (g - 3) + b % 2, :]
                dve.wait_ge(s("tanh"), b + 1)
                silu = th[g][:, b % 2, :]
                if g != LATES[-1]:
                    link(stt(h, silu, 1.0, bank(gate_bank(b)), ALU.add, ALU.mult))
                    silu = h
                stt(h, bank(gate_bank(b) + 1), sm8[:, 5, b:b + 1], silu, ALU.mult, ALU.mult)\
                    .then_inc(s("h_done"), 1)
                dve.wait_ge(s("h_done"), b + 1)
                link(V_.tensor_reduce(sc[:, 0:1], h, AX_X, ALU.max, apply_absolute_value=True))

                link(ts(sc[:, 1:2], sc[:, 0:1], 1e-5, 1.0 / 127.0, ALU.max, ALU.mult))
                V_.reciprocal(sc[:, 2:3], sc[:, 1:2]).then_inc(s("h_scale"), 1)

            def hidden_whole(b):
                g = LATES[b >= B0[-1]]
                h, sc = hb[g][:, b % 2, :], hs[:, 2 * (g - 3) + b % 2, :]
                dve.wait_ge(s("h_round"), b + 1)
                if b >= 2:
                    dve.wait_ge(s("pe_hT"), b - 1)
                ts(hi[g][:, b % 2, :], h, MAGIC + 127.0, MAGIC, ALU.min, ALU.subtract).then_inc(s("h_int"), 1)
                link(ts(sm8[:, 6, b:b + 1], sc[:, 1:2], wscl[:, 2:3], None, ALU.mult))

            def add_down(b):
                dve.wait_ge(s("pe_down"), b + 1)
                stt(res[:, b, :], bank(down_bank(b))[:, 0:P], sm8[:, 6, b:b + 1], xt[:, b, :],
                    ALU.mult, ALU.add).then_inc(s("res_f1"), 1)

            def late(g, i):
                hb4 = slice(B0[g], B0[g] + N[g])
                if i == 0:
                    moments(g, s("res1_done"), B0[g] + N[g])
                    dve.wait_ge(s("pe_k1"), g - 2)
                    tt(tok(part_of(lD[g], g), N[g]), tok(part_of(bank(LBANKS[g][1]), g), N[g]), over(rot_s[:, 2, :], N[g], P), ALU.mult)
                    tt(tok(part_of(lC[g], g), N[g]), tok(part_of(bank(LBANKS[g][2]), g), N[g]), over(rot_s[:, 3, :], N[g], P), ALU.mult).then_inc(s("k1_mul"), 1)
                    dve.wait_ge(s("k1_mul"), g - 2)
                    tt(part_of(kx1[g], g), part_of(lD[g], g), part_of(lC[g], g), ALU.add).then_inc(s("k1_rot"), 1)
                if i == 4:
                    dve.wait_ge(s("pe_q"), g - 2)
                    tt(tok(part_of(lA[g], g), N[g]), tok(part_of(bank(LBANKS[g][1]), g), N[g]), over(rot_s[:, 0, :], N[g], P), ALU.mult)
                    tt(tok(part_of(lE[g], g), N[g]), tok(part_of(bank(LBANKS[g][2]), g), N[g]), over(rot_s[:, 1, :], N[g], P), ALU.mult).then_inc(s("q_mul"), 1)
                    dve.wait_ge(s("q_mul"), g - 2)
                    tt(part_of(lA[g], g), part_of(lA[g], g), part_of(lE[g], g), ALU.add).then_inc(s("q_rot"), 1)
                if i == 6:
                    dve.wait_ge(s("pe_sx1"), g - 2)
                    tt(tok(part_of(lD[g], g), N[g]), tok(part_of(bank(LBANKS[g][0]), g), N[g]), over(decay_s[:], N[g], P), ALU.mult).then_inc(s("sx1"), 1)
                if i == 7:
                    dve.wait_ge(s("pe_ox1"), g - 2)
                    link(tt(batches(res, g), tok(part_of(bank(LBANKS[g][1]), g), N[g]), batches(xt, g), ALU.add))
                    moments(g)
                if i == 10:
                    for j in range(N[g]):
                        dve.wait_ge(*normalised(g, 1, j))
                    link(V_.tensor_reduce(sm8[:, 0, hb4], batches(xt, g), AX_X, ALU.max,
                                          apply_absolute_value=True))
                    link(ts(sm8[:, 1, hb4], sm8[:, 0, hb4], 1e-5, 1.0 / 127.0, ALU.max, ALU.mult))
                    link(V_.reciprocal(sm8[:, 2, hb4], sm8[:, 1, hb4]))
                    for j in range(N[g]):
                        b = B0[g] + j
                        m = ts(x5r[g][:, j * P:(j + 1) * P], xt[:, b, :], sm8[:, 2, b:b + 1], MAGIC,
                               ALU.mult, ALU.add)
                    link(m)
                    ts(part_of(x5q[g], g), part_of(x5r[g], g), MAGIC + 127.0, MAGIC, ALU.min, ALU.subtract).then_inc(s("x5q"), 1)
                    last = g == LATES[-1]
                    link(ts(sm8[:, 4, hb4], sm8[:, 1, hb4], wscl[:, 0:1], 1.0 if last else 0.5, ALU.mult, ALU.mult))
                    m = ts(sm8[:, 5, hb4], sm8[:, 1, hb4], wscl[:, 1:2], None, ALU.mult)
                    if not last:
                        link(m)
                        m = tt(sm8[:, 5, hb4], sm8[:, 5, hb4], sm8[:, 4, hb4], ALU.mult)
                    m.then_inc(s("gu_scale"), 1)
                if 12 <= i <= 12 + 2 * N[g] and i % 2 == 0:
                    j = i // 2 - 6
                    if j == 0:
                        dve.wait_ge(s("gu_scale"), g - 2)
                    if j:
                        hidden_whole(B0[g] + j - 1)
                    if j < N[g]:
                        hidden_product(B0[g] + j)
                    if j:
                        add_down(B0[g] + j - 1)
                if i == 13 + 2 * N[g]:
                    moments(g, s("res_f1"), B0[g] + N[g])

            def run(t, k):
                for kind, g, i in TICKS.get((t, k), ()):
                    (mid if kind == "mid" else late)(g, i)

            for i in range(8):
                lower_parts(0, i)
            for Q in range(AHEAD):
                maxima(Q)
            max_rows(0)
            for t in range(TICKS0):
                lower_next(t, 0)
                if t % 4 == 3 and t < NQ - 1:
                    max_rows(t // 4 + 1)
                lower_next(t, 1)
                if t == 0:
                    dve.wait_ge(s("ld_late"), 32)
                    for i in range(2):
                        V_.tensor_reduce(wabs[:, i:i + 1], wgu_s[:, i * INNER:(i + 1) * INNER], AX_X, ALU.add,
                                         apply_absolute_value=True)
                    V_.tensor_reduce(wabs[:, 2:3], wdn_s[:], AX_X, ALU.add, apply_absolute_value=True)\
                        .then_inc(s("w_abs"), 1)
                if t == 2:
                    dve.wait_ge(s("pe_wsum"), 1)
                    link(ts(wscl[:, 0:3], bank(6)[:, 0:3], 1.0 / NW, 1e-5, ALU.mult, ALU.max))
                    V_.reciprocal(wscl[:, 4:7], wscl[:, 0:3]).then_inc(s("w_scale"), 1)
                run(t, 0)
                if 1 <= t <= NQ:
                    normalize(t - 1)
                lower_next(t, 2)
                run(t, 1)
                if t % 2 and t >= 3:
                    place_out((t - 3) // 2)
                if t + AHEAD < NQ:
                    maxima(t + AHEAD)
                if t % 4 == 2 and t >= 6:
                    add_out((t - 6) // 4)
                run(t, 2)
                if t >= T1:
                    scores(t - T1)
                    outputs(t - T1)
            for u in range(TICKS0 - T1, TICKS1):
                run(T1 + u, 0)
                scores(u)
                run(T1 + u, 1)
                outputs(u)
                run(T1 + u, 2)


def kernel(**inputs):
    import numpy as np
    import concourse.bacc as bacc
    from concourse.bass_utils import run_bass_kernel_spmd

    f = {k: np.asarray(v) for k, v in inputs.items()}
    c = np.ascontiguousarray

    def by_group(w):
        return c(w.reshape(2, G, DH0, P).transpose(3, 1, 0, 2).reshape(P, 1024))

    swap = np.arange(P) ^ 1
    f32 = np.float32
    base = (np.arange(0, P, 2, dtype=f32) + f32(0.4 * P)) / f32(1.4 * P)
    pos = np.arange(P, dtype=f32)
    scale = base[None, :] ** (pos / f32(512.0))[:, None]
    freqs = f32(1.0) / f32(10000.0) ** (np.arange(P // 2, dtype=f32) / f32(P // 2))
    angle = pos[:, None] * freqs[None, :]
    sign = np.where(np.arange(P) % 2 == 0, -1.0, 1.0).astype(f32)

    def twice(t):
        return np.repeat(t, 2, axis=1).T.astype(f32)
    rot = np.stack([twice(np.cos(angle) * scale), twice(np.sin(angle) * scale) * sign[:, None],
                    twice(np.cos(angle) * (f32(1.0) / scale)),
                    twice(np.sin(angle) * (f32(1.0) / scale)) * sign[:, None]], axis=1)
    ahead = pos[None, :] - pos[:, None]
    decay = np.where(ahead >= 0, f32(0.96875) ** np.maximum(ahead, 0), 0).astype(f32)

    wa, ba = f["L1_attn_W_attn"], f["L1_attn_b_attn"]
    arrays = {
        "x_tok": c(f["x"].transpose(1, 0, 2)), "x_T": c(f["x"].transpose(2, 0, 1).reshape(P, NTOK)),
        "ctx_T": c(f["ctx_1024"].transpose(2, 0, 1).reshape(P, NTOK)),
        "wq0": by_group(f["L0_attn_wq"]), "wk0": by_group(f["L0_attn_wk"]), "wv0": by_group(f["L0_attn_wv"]),
        "wo0": c(f["L0_attn_wo"].reshape(P, 2, G, DH0).transpose(1, 3, 2, 0).reshape(P, G, P)),
        "xwq0": c(f["L0_xattn_Wq"].T), "xbq0": f["L0_xattn_bq"].reshape(P, 1),
        "xwk0": c(f["L0_xattn_Wk"].T), "xbk0": f["L0_xattn_bk"].reshape(P, 1),
        "xwv0": c(f["L0_xattn_Wv"].T), "xbv0": f["L0_xattn_bv"].reshape(1, P),
        "wge": c(np.concatenate([f["L0_ffn_We"], f["L0_ffn_Wg"]], axis=1)),
        "bge": np.concatenate([f["L0_ffn_be"], f["L0_ffn_bg"]]).reshape(1, P + NE),
        "wqk1": c(wa[:, 0:2 * P].reshape(P, 2, P)), "bqk1": c(ba[0:2 * P].reshape(2, P).T),
        "wv1": c(wa[:, 2 * P:3 * P]), "bv1": c(ba[2 * P:3 * P].reshape(1, P)),
        "wp1": f["L1_attn_W_proj"], "bp1": f["L1_attn_b_proj"].reshape(1, P),
        "xwq1": f["L1_xattn_Wq"], "xwq1s": c(f["L1_xattn_Wq"][:, swap]),
        "xwk1": f["L1_xattn_Wk"], "xwk1s": c(f["L1_xattn_Wk"][:, swap]), "xwv1": f["L1_xattn_Wv"],
        "wgu": c(np.concatenate([f["L1_ffn_w_gate"].T, f["L1_ffn_w_up"].T], axis=1)),
        "wdn": c(f["L1_ffn_w_down"].T.reshape(4, P, P).transpose(1, 0, 2).reshape(P, INNER)),
        "rot": c(rot), "decay": decay,
    }
    nc = bacc.Bacc("TRN2", target_bir_lowering=False, num_devices=1)
    args = [nc.dram_tensor(n, a.shape, mybir.dt.from_np(a.dtype), kind="ExternalInput").ap()
            for n, a in arrays.items()]
    result = nc.dram_tensor("out", (NB, P, P), F32, kind="ExternalOutput").ap()
    decoder(nc, *args, result)
    done = run_bass_kernel_spmd(nc, [arrays], core_ids=[0])
    return done.results[0]["out"]
```
